# Optimizing a Trainium2 kernel written in Bass

```python
import numpy as np
import jax
import jax.numpy as jnp

def _softmax(x, axis=-1):
    return jax.nn.softmax(x, axis=axis)

def _gelu(x):
    return jax.nn.gelu(x, approximate=True)

def _silu(x):
    return jax.nn.silu(x)

def _sigmoid(x):
    return jax.nn.sigmoid(x)

def _layernorm(x, axis=-1, eps=1e-05):
    m = jnp.mean(x, axis=axis, keepdims=True)
    v = jnp.var(x, axis=axis, keepdims=True)
    return (x - m) / jnp.sqrt(v + eps)

def _scatter_add(tgt, idx, src, axis=0):
    return tgt.at[idx].add(src)

def _segment_sum(src, seg, n):
    return jax.ops.segment_sum(src, seg, n)
kernel_name = 'mk_gnn_resnorm_d4_gnn_r64_0cca1a'

def setup_inputs(seed: int=0):
    np.random.seed(seed)
    _w = jnp.asarray

    def _rec_inputs():
        import jax
        import jax.numpy as jnp
        _gk = jax.random.key(seed)
        x = -0.000202 + 1 * jax.random.normal(jax.random.fold_in(_gk, 1), (50000, 128), jnp.float32)
        src = jax.random.randint(jax.random.fold_in(_gk, 2), (25000,), 0, 50000, jnp.int32)
        dst = jnp.minimum((50000 * jax.random.uniform(jax.random.fold_in(_gk, 3), (25000,)) ** 2.0).astype(jnp.int32), 49999)
        _o = jnp.argsort(dst, stable=True)
        src = src[_o]
        dst = dst[_o]
        edge_type_9 = jax.random.randint(jax.random.fold_in(_gk, 13), (25000,), 0, 9, jnp.int32)
        edge_weight = jax.random.uniform(jax.random.fold_in(_gk, 14), (25000,), jnp.float32, 0.0, 0.999998)
        return (x, src, dst, edge_type_9, edge_weight)
    x, src, dst, edge_type_9, edge_weight = _rec_inputs()

    def _L0_gnn_setup():
        import jax, jax.numpy as jnp
        import numpy as np
        N, IN, H, D = (50000, 128, 4, 32)
        HID = H * D
        E = 12500
        key = jax.random.key(seed)
        ks = jax.random.split(key, 16)
        s_in = 1.0 / np.sqrt(IN)
        s_g = 1.0 / np.sqrt(3 * HID)
        inp = {'feat': jax.random.normal(ks[0], (N, IN), jnp.float32), 'src': jax.random.randint(ks[1], (E,), 0, N, jnp.int32), 'dst': jax.random.randint(ks[2], (E,), 0, N, jnp.int32), 'Wq': jax.random.normal(ks[3], (IN, HID), jnp.float32) * s_in, 'bq': jnp.zeros((HID,), jnp.float32), 'Wk': jax.random.normal(ks[4], (IN, HID), jnp.float32) * s_in, 'bk': jnp.zeros((HID,), jnp.float32), 'Wv': jax.random.normal(ks[5], (IN, HID), jnp.float32) * s_in, 'bv': jnp.zeros((HID,), jnp.float32), 'Ws': jax.random.normal(ks[6], (IN, HID), jnp.float32) * s_in, 'bs': jnp.zeros((HID,), jnp.float32), 'Wg': jax.random.normal(ks[7], (3 * HID, 1), jnp.float32) * s_g, 'bg': jnp.zeros((1,), jnp.float32), 'gamma': jnp.ones((HID,), jnp.float32), 'beta': jnp.zeros((HID,), jnp.float32), 'alpha': jnp.asarray(0.25, jnp.float32)}
        return inp
    _L0_gnn_all = _L0_gnn_setup()
    _L0_gnn_in = {k: v for k, v in _L0_gnn_all.items() if k in ('Wq', 'bq', 'Wk', 'bk', 'Wv', 'bv', 'Ws', 'bs', 'Wg', 'bg', 'gamma', 'beta', 'alpha')}
    del _L0_gnn_all

    def _L1_gnn_setup():
        import jax, jax.numpy as jnp
        import numpy as np
        N_NODES = 100000
        N_EDGES = 9375
        C_IN = 128
        C_OUT = 128
        key = jax.random.key(seed)
        k_x, k_ei, k_ew, k_pw, k_pb, k_fw, k_fb = jax.random.split(key, 7)
        x = jax.random.normal(k_x, (N_NODES, C_IN), dtype=jnp.float32)
        edge_index = jax.random.randint(k_ei, (2, N_EDGES), 0, N_NODES, dtype=jnp.int64)
        edge_weight = jax.random.uniform(k_ew, (N_EDGES,), dtype=jnp.float32)
        s1 = 1.0 / np.sqrt(C_IN)
        s2 = 1.0 / np.sqrt(2 * C_IN)
        pool_w = jax.random.uniform(k_pw, (C_IN, C_IN), jnp.float32, -s1, s1)
        pool_b = jax.random.uniform(k_pb, (C_IN,), jnp.float32, -s1, s1)
        final_w = jax.random.uniform(k_fw, (C_OUT, 2 * C_IN), jnp.float32, -s2, s2)
        final_b = jax.random.uniform(k_fb, (C_OUT,), jnp.float32, -s2, s2)
        return {'x': x, 'edge_index': edge_index, 'edge_weight': edge_weight, 'pool_w': pool_w, 'pool_b': pool_b, 'final_w': final_w, 'final_b': final_b}
    _L1_gnn_all = _L1_gnn_setup()
    _L1_gnn_in = {k: v for k, v in _L1_gnn_all.items() if k in ('pool_w', 'pool_b', 'final_w', 'final_b')}
    del _L1_gnn_all

    def _L2_gnn_setup():
        import jax, jax.numpy as jnp
        import numpy as np
        NUM_EDGE_TYPES = 8
        HIDDEN = 128
        N_NODES = 50000
        N_EDGES = 9375

        def _gru_cell(x, h, W_ih, W_hh, b_ih, b_hh):
            H = h.shape[-1]
            gi = x @ W_ih.T + b_ih
            gh = h @ W_hh.T + b_hh
            i_r, i_z, i_n = (gi[:, :H], gi[:, H:2 * H], gi[:, 2 * H:])
            h_r, h_z, h_n = (gh[:, :H], gh[:, H:2 * H], gh[:, 2 * H:])
            r = jax.nn.sigmoid(i_r + h_r)
            z = jax.nn.sigmoid(i_z + h_z)
            n = jnp.tanh(i_n + r * h_n)
            return (1.0 - z) * n + z * h
        key = jax.random.key(seed)
        ks = jax.random.split(key, 10)
        H = HIDDEN
        h = jax.random.normal(ks[0], (N_NODES, H), dtype=jnp.float32)
        edge_index = jax.random.randint(ks[1], (2, N_EDGES), 0, N_NODES, dtype=jnp.int32)
        edge_type = jax.random.randint(ks[2], (N_EDGES,), 0, NUM_EDGE_TYPES + 1, dtype=jnp.int32)
        s = 1.0 / np.sqrt(H)
        W_msg = jax.random.uniform(ks[3], (H, H), jnp.float32, -s, s)
        b_msg = jax.random.uniform(ks[4], (H,), jnp.float32, -s, s)
        edge_embed = jax.random.normal(ks[5], (NUM_EDGE_TYPES + 1, H), dtype=jnp.float32)
        W_ih = jax.random.uniform(ks[6], (3 * H, H), jnp.float32, -s, s)
        W_hh = jax.random.uniform(ks[7], (3 * H, H), jnp.float32, -s, s)
        b_ih = jax.random.uniform(ks[8], (3 * H,), jnp.float32, -s, s)
        b_hh = jax.random.uniform(ks[9], (3 * H,), jnp.float32, -s, s)
        return {'h': h, 'edge_index': edge_index, 'edge_type': edge_type, 'num_nodes': N_NODES, 'W_msg': W_msg, 'b_msg': b_msg, 'edge_embed': edge_embed, 'W_ih': W_ih, 'W_hh': W_hh, 'b_ih': b_ih, 'b_hh': b_hh}
    _L2_gnn_all = _L2_gnn_setup()
    _L2_gnn_in = {k: v for k, v in _L2_gnn_all.items() if k in ('W_msg', 'b_msg', 'edge_embed', 'W_ih', 'W_hh', 'b_ih', 'b_hh')}
    del _L2_gnn_all

    def _L3_gnn_setup():
        import jax, jax.numpy as jnp
        import numpy as np
        N, E, D, L = (50000, 12500, 128, 2)
        NEG_SLOPE = 0.2
        LN_EPS = 1e-05
        key = jax.random.key(seed)
        ks = jax.random.split(key, 6)
        scale = 1.0 / np.sqrt(D)
        x = jax.random.normal(ks[0], (N, D), dtype=jnp.float32)
        edge_index = jax.random.randint(ks[1], (2, E), 0, N, dtype=jnp.int64)
        W = jax.random.normal(ks[2], (L, D, D), dtype=jnp.float32) * scale
        att_src = jax.random.normal(ks[3], (L, D), dtype=jnp.float32) * scale
        att_dst = jax.random.normal(ks[4], (L, D), dtype=jnp.float32) * scale
        bias = jnp.zeros((L, D), dtype=jnp.float32)
        gamma = jnp.ones((L, D), dtype=jnp.float32)
        beta = jnp.zeros((L, D), dtype=jnp.float32)
        return {'x': x, 'edge_index': edge_index, 'W': W, 'att_src': att_src, 'att_dst': att_dst, 'bias': bias, 'gamma': gamma, 'beta': beta}
    _L3_gnn_all = _L3_gnn_setup()
    _L3_gnn_in = {k: v for k, v in _L3_gnn_all.items() if k in ('W', 'att_src', 'att_dst', 'bias', 'gamma', 'beta')}
    del _L3_gnn_all
    return {'x': x, 'src': src, 'dst': dst, 'edge_type_9': edge_type_9, 'edge_weight': edge_weight, 'L0_gnn_Wq': _L0_gnn_in['Wq'], 'L0_gnn_bq': _L0_gnn_in['bq'], 'L0_gnn_Wk': _L0_gnn_in['Wk'], 'L0_gnn_bk': _L0_gnn_in['bk'], 'L0_gnn_Wv': _L0_gnn_in['Wv'], 'L0_gnn_bv': _L0_gnn_in['bv'], 'L0_gnn_Ws': _L0_gnn_in['Ws'], 'L0_gnn_bs': _L0_gnn_in['bs'], 'L0_gnn_Wg': _L0_gnn_in['Wg'], 'L0_gnn_bg': _L0_gnn_in['bg'], 'L0_gnn_gamma': _L0_gnn_in['gamma'], 'L0_gnn_beta': _L0_gnn_in['beta'], 'L0_gnn_alpha': _L0_gnn_in['alpha'], 'L1_gnn_pool_w': _L1_gnn_in['pool_w'], 'L1_gnn_pool_b': _L1_gnn_in['pool_b'], 'L1_gnn_final_w': _L1_gnn_in['final_w'], 'L1_gnn_final_b': _L1_gnn_in['final_b'], 'L2_gnn_W_msg': _L2_gnn_in['W_msg'], 'L2_gnn_b_msg': _L2_gnn_in['b_msg'], 'L2_gnn_edge_embed': _L2_gnn_in['edge_embed'], 'L2_gnn_W_ih': _L2_gnn_in['W_ih'], 'L2_gnn_W_hh': _L2_gnn_in['W_hh'], 'L2_gnn_b_ih': _L2_gnn_in['b_ih'], 'L2_gnn_b_hh': _L2_gnn_in['b_hh'], 'L3_gnn_W': _L3_gnn_in['W'], 'L3_gnn_att_src': _L3_gnn_in['att_src'], 'L3_gnn_att_dst': _L3_gnn_in['att_dst'], 'L3_gnn_bias': _L3_gnn_in['bias'], 'L3_gnn_gamma': _L3_gnn_in['gamma'], 'L3_gnn_beta': _L3_gnn_in['beta']}

def reference(x, src, dst, edge_type_9, edge_weight, L0_gnn_Wq, L0_gnn_bq, L0_gnn_Wk, L0_gnn_bk, L0_gnn_Wv, L0_gnn_bv, L0_gnn_Ws, L0_gnn_bs, L0_gnn_Wg, L0_gnn_bg, L0_gnn_gamma, L0_gnn_beta, L0_gnn_alpha, L1_gnn_pool_w, L1_gnn_pool_b, L1_gnn_final_w, L1_gnn_final_b, L2_gnn_W_msg, L2_gnn_b_msg, L2_gnn_edge_embed, L2_gnn_W_ih, L2_gnn_W_hh, L2_gnn_b_ih, L2_gnn_b_hh, L3_gnn_W, L3_gnn_att_src, L3_gnn_att_dst, L3_gnn_bias, L3_gnn_gamma, L3_gnn_beta):
    import jax
    import jax.numpy as jnp

    def _L0_gnn_ref(feat, src, dst, Wq, bq, Wk, bk, Wv, bv, Ws, bs, Wg, bg, gamma, beta, alpha):
        import jax, jax.numpy as jnp
        import numpy as np
        N, IN, H, D = (50000, 128, 4, 32)
        HID = H * D
        E = 12500
        n = feat.shape[0]
        q = (feat @ Wq + bq).reshape(n, H, D)
        k = (feat @ Wk + bk).reshape(n, H, D)
        v = (feat @ Wv + bv).reshape(n, H, D)
        a = jnp.einsum('ehd,ehd->eh', q[src], k[dst]) / jnp.sqrt(jnp.float32(D))
        m = jax.ops.segment_max(a, dst, num_segments=n)
        m = jax.lax.stop_gradient(jnp.where(jnp.isfinite(m), m, 0.0))
        ex = jnp.exp(a - m[dst])
        denom = jax.ops.segment_sum(ex, dst, num_segments=n)
        denom = jnp.where(denom > 0, denom, 1.0)
        sa = ex / denom[dst]
        msg = v[src] * sa[:, :, None]
        agg = jax.ops.segment_sum(msg, dst, num_segments=n).reshape(n, HID)
        skip = feat @ Ws + bs
        g = jax.nn.sigmoid(jnp.concatenate([skip, agg, skip - agg], axis=-1) @ Wg + bg)
        rst = g * skip + (1.0 - g) * agg
        mu = rst.mean(-1, keepdims=True)
        var = rst.var(-1, keepdims=True)
        rst = (rst - mu) * jax.lax.rsqrt(var + 1e-05) * gamma + beta
        rst = jnp.where(rst >= 0, rst, alpha * rst)
        return rst

    def _L1_gnn_ref(x, edge_index, edge_weight, pool_w, pool_b, final_w, final_b):
        import jax, jax.numpy as jnp
        import numpy as np
        N_NODES = 100000
        N_EDGES = 9375
        C_IN = 128
        C_OUT = 128
        src, dst = (edge_index[0], edge_index[1])
        msg = x[src] * edge_weight[:, None]
        pooled = jax.nn.relu(msg @ pool_w.T + pool_b)
        aggregate = jax.ops.segment_max(pooled, dst, num_segments=x.shape[0])
        aggregate = jnp.maximum(aggregate, 0.0)
        h = jnp.concatenate([x, aggregate], axis=-1)
        out = jax.nn.relu(h @ final_w.T + final_b)
        return out

    def _L2_gnn_ref(h, edge_index, edge_type, num_nodes, W_msg, b_msg, edge_embed, W_ih, W_hh, b_ih, b_hh):
        import jax, jax.numpy as jnp
        import numpy as np
        NUM_EDGE_TYPES = 8
        HIDDEN = 128
        N_NODES = 50000
        N_EDGES = 9375

        def _gru_cell(x, h, W_ih, W_hh, b_ih, b_hh):
            H = h.shape[-1]
            gi = x @ W_ih.T + b_ih
            gh = h @ W_hh.T + b_hh
            i_r, i_z, i_n = (gi[:, :H], gi[:, H:2 * H], gi[:, 2 * H:])
            h_r, h_z, h_n = (gh[:, :H], gh[:, H:2 * H], gh[:, 2 * H:])
            r = jax.nn.sigmoid(i_r + h_r)
            z = jax.nn.sigmoid(i_z + h_z)
            n = jnp.tanh(i_n + r * h_n)
            return (1.0 - z) * n + z * h
        src = edge_index[0]
        dst = edge_index[1]
        src_h = h[src] @ W_msg.T + b_msg
        emb = edge_embed[jnp.clip(edge_type, 0, NUM_EDGE_TYPES)]
        msg = src_h + emb
        messages = jax.ops.segment_sum(msg, dst, num_segments=num_nodes)
        h_new = _gru_cell(messages, h[:num_nodes], W_ih, W_hh, b_ih, b_hh)
        result = jnp.zeros_like(h).at[:num_nodes].set(h_new)
        return result

    def _L3_gnn_ref(x, edge_index, W, att_src, att_dst, bias, gamma, beta):
        import jax, jax.numpy as jnp
        import numpy as np
        N, E, D, L = (50000, 12500, 128, 2)
        NEG_SLOPE = 0.2
        LN_EPS = 1e-05
        n = x.shape[0]
        loops = jnp.arange(n, dtype=edge_index.dtype)
        ei = jnp.concatenate([edge_index, jnp.stack([loops, loops])], axis=1)
        src, dst = (ei[0], ei[1])
        for l in range(W.shape[0]):
            h = x @ W[l]
            a_src = h @ att_src[l]
            a_dst = h @ att_dst[l]
            logit = jax.nn.leaky_relu(a_src[src] + a_dst[dst], NEG_SLOPE)
            m = jax.ops.segment_max(logit, dst, num_segments=n)
            e = jnp.exp(logit - m[dst])
            s = jax.ops.segment_sum(e, dst, num_segments=n)
            alpha = e / s[dst]
            msg = h[src] * alpha[:, None]
            x_att = jax.ops.segment_sum(msg, dst, num_segments=n) + bias[l]
            y = x + x_att
            mu = jnp.mean(y, axis=-1, keepdims=True)
            var = jnp.var(y, axis=-1, keepdims=True)
            x = (y - mu) * jax.lax.rsqrt(var + LN_EPS) * gamma[l] + beta[l]
        return x
    edge_index = jnp.stack([src, dst])
    x = _layernorm(x + _L0_gnn_ref(x, src, dst, L0_gnn_Wq, L0_gnn_bq, L0_gnn_Wk, L0_gnn_bk, L0_gnn_Wv, L0_gnn_bv, L0_gnn_Ws, L0_gnn_bs, L0_gnn_Wg, L0_gnn_bg, L0_gnn_gamma, L0_gnn_beta, L0_gnn_alpha), axis=-1)
    x = _layernorm(x + _L1_gnn_ref(x, edge_index, edge_weight, L1_gnn_pool_w, L1_gnn_pool_b, L1_gnn_final_w, L1_gnn_final_b), axis=-1)
    x = _layernorm(x + _L2_gnn_ref(x, edge_index, edge_type_9, 50000, L2_gnn_W_msg, L2_gnn_b_msg, L2_gnn_edge_embed, L2_gnn_W_ih, L2_gnn_W_hh, L2_gnn_b_ih, L2_gnn_b_hh), axis=-1)
    x = _layernorm(x + _L3_gnn_ref(x, edge_index, L3_gnn_W, L3_gnn_att_src, L3_gnn_att_dst, L3_gnn_bias, L3_gnn_gamma, L3_gnn_beta), axis=-1)
    return x

_drawn_inputs = setup_inputs


def setup_inputs(seed=0):
    import zlib

    import numpy as np

    out = dict(_drawn_inputs(seed))
    spreads = {'L0_gnn_bq': (0.0, 0.8),
     'L0_gnn_bk': (0.0, 0.8),
     'L0_gnn_bv': (0.0, 0.27),
     'L0_gnn_bs': (0.0, 0.1),
     'L0_gnn_gamma': (1.0, 0.2),
     'L0_gnn_beta': (0.0, 0.1),
     'L3_gnn_bias': (0.0, 0.1),
     'L3_gnn_gamma': (1.0, 0.2),
     'L3_gnn_beta': (0.0, 0.1)}
    factors = {'edge_weight': 2.866,
     'L1_gnn_pool_b': 8.0,
     'L2_gnn_b_msg': 7.335,
     'L2_gnn_b_ih': 3.002,
     'L2_gnn_b_hh': 4.868}
    for name, (base, spread) in spreads.items():
        noise = np.random.default_rng([zlib.crc32(name.encode()), seed]).standard_normal(out[name].shape)
        drawn = base * np.exp(spread * noise) if base else spread * noise
        out[name] = jnp.asarray(drawn.astype(out[name].dtype))
    for name, factor in factors.items():
        out[name] = (out[name] * factor).astype(out[name].dtype)
    return out
```

```python
from contextlib import ExitStack

import concourse.bass as bass
from concourse import mybir

F32 = mybir.dt.float32
BF16 = mybir.dt.bfloat16
I32 = mybir.dt.int32
ALU = mybir.AluOpType
ACT = mybir.ActivationFunctionType

P = 128
U = 4
BIG = 1e30
NO_ROW = 65536
PAD_DST = 60000
EPS = 1e-5
SLOPE = 0.2


class Step:

    def __init__(self, h, u):
        self.h, self.u = h, u

    def back(self, k):
        t = self.u - k
        return Step(self.h + t // U if t < 0 else self.h, t % U)

    @property
    def index(self):
        return self.h * U + self.u

    def exists(self, n):
        return not isinstance(self.h, int) or 0 <= self.index < n


class Signal:

    def __init__(self, sem, steps, before):
        self.sem, self.steps, self.before = sem, steps, before

    def at(self, step):
        return self.sem, step.h * U + (step.u + 1 + self.before)

    def end(self):
        return self.sem, self.before + self.steps


class DmaSignals:

    def __init__(self, sems, steps, dmas, before):
        self.sems, self.steps, self.unit, self.before = sems, steps, 16 * dmas, before

    def sem(self, step):
        return self.sems[step.u]

    def at(self, step):
        return self.sems[step.u], step.h * self.unit + (self.unit + self.before[step.u])

    def end(self):
        return [(s, self.before[u] + self.unit * ((self.steps - u + U - 1) // U)) for u, s in enumerate(self.sems)]


def run_steps(eng, n, lag, body, first=2):
    last = (n - 1) // U
    for j in range(first * U):
        body(Step(j // U, j % U))
    with eng.Fori(first, last) as h:
        for u in range(U):
            body(Step(h, u))
    for j in range(last * U, n + lag):
        body(Step(j // U, j % U))


def gnn_kernel(nc, x, src, dst, edge_type, edge_weight,
               Wq, bq, Wk, bk, Wv, bv, Ws, bs, Wg, bg, gamma0, beta0, alpha,
               pool_w, pool_b, final_w, final_b,
               W_msg, b_msg, edge_embed, W_ih, W_hh, b_ih, b_hh,
               W3, att_src, att_dst, bias3, gamma3, beta3, out):
    N, H = x.shape
    E = src.shape[0]
    HEADS = 4
    HEAD = H // HEADS
    TYPES = edge_embed.shape[0]
    L3 = W3.shape[0]
    EB = 512
    ET = EB // P
    EG = -(-E // EB)
    EPAD = EG * EB
    TILES = EPAD // P
    W0 = H + 2
    G = 4
    NB = -(-N // (G * P))
    G2 = 2
    NB2 = -(-N // (G2 * P))
    assert H == P and TYPES <= P and N < NO_ROW

    ctx = ExitStack()
    with ctx:
        def sb(name, shape, dt=F32):
            return ctx.enter_context(nc.sbuf_tensor(name, shape, dt))

        def ring(name, shape, depth, dt=F32):
            whole = sb(name, [shape[0], depth, *shape[1:]], dt)
            return [whole[:, i] for i in range(depth)]

        def sem(name):
            return ctx.enter_context(nc.semaphore(name))

        def dram(name, shape, dt=F32):
            return nc.dram_tensor(name, shape, dt, kind="Internal").ap()

        dst_pad = dram("dst_pad", [EPAD + 2], I32)
        src_pad = dram("src_pad", [EPAD], I32)
        type_pad = dram("type_pad", [EPAD], I32)
        weight_pad = dram("weight_pad", [EPAD])
        edge_table = dram("edge_table", [P, EG * 4 * ET], I32)
        xa = dram("xa", [N, H])
        xb = dram("xb", [N, H])
        att_rows = dram("att_rows", [N, W0])
        msg_rows = dram("msg_rows", [N, H])

        banks = [ctx.enter_context(nc.psum_tensor(f"bank{i}", [P, 512], F32)) for i in range(8)]

        ident = sb("ident", [P, P])
        head_ones = sb("head_ones", [P, P])
        one = sb("one", [P, P])
        ones_bf = sb("ones_bf", [P, P], BF16)
        neg_half = sb("neg_half", [P, G])
        w_nat = sb("w_nat", [P, 13, P])
        wT = sb("wT", [P, 16, P])
        POOL, FIN_X, FIN_A, MSG, IH, WS_T, HH, W3_T = 0, 1, 2, 3, 4, 7, 8, 11
        wqkvs = sb("wqkvs", [P, 4, P])
        w3 = sb("w3", [P, L3, P])
        cols = sb("cols", [P, 16])
        BQ, BK, BV, BS, BPOOL, WG, ASRC, ADST = 0, 1, 2, 3, 4, 5, 8, 10
        gate_w = sb("gate_w", [P, 2])
        bs_wide = sb("bs_wide", [P, P])
        products = sb("products", [P, 8])
        self_col = sb("self_col", [P, L3])
        att_wide = sb("att_wide", [P, 2 * L3, P])
        scal = sb("scal", [P, 4])
        embed = sb("embed", [P, 2, P])
        embed_b = sb("embed_b", [P, P])
        type_id = sb("type_id", [P, 1])
        wide = sb("wide", [P, 8, P])
        GAM0, BET0, BIAS3, GAM3, BET3 = 0, 1, 2, 4, 6
        rows = sb("rows", [1, 4, 512])
        split = sb("split", [P, 3, 512], BF16)
        zeros = sb("zeros", [80, 25 * W0])
        zeros_msg = sb("zeros_msg", [80, 25 * H])
        pad_vals = sb("pad_vals", [P, 512], I32)
        type_i = sb("type_i", [P, 1], I32)
        lists = sb("lists", [P, 3, 2, P], I32)
        lists_w = sb("lists_w", [P, 2, P])
        lists_f = sb("lists_f", [P, 4, 2, P])
        table_sb = sb("table_sb", [P, EG * 4 * ET], I32)

        etab = ring("etab", [P, 4 * ET], 4, I32)
        dstb = ring("dstb", [P, EB + 1], 4, I32)
        x_src = ring("x_src", [P, ET, P], 4)
        x_dst = ring("x_dst", [P, ET, P], 4)
        typeb = [b.rearrange("p t f -> p (t f)").bitcast(I32) for b in x_dst]
        srcT = ring("srcT", [P, EB], 2)
        dstT = ring("dstT", [P, EB], 2)
        same = ring("same", [P, EB], 2)
        fresh = ring("fresh", [P, EB], 2)
        e1 = ring("e1", [P, EB], 2)
        e2 = ring("e2", [P, EB], 2)
        top = ring("top", [P, EB + 1], 2)
        pair = ring("pair", [P, 2, EB], 2)
        expd = ring("expd", [P, 2, EB], 2)
        total = ring("total", [P, EB], 2)
        acc = ring("acc", [P, EB], 2)
        row_out = ring("row_out", [P, ET, W0], 4)

        x_in, x_res, msg_in, xT = x_src, x_dst, row_out, srcT
        n1 = ring("n1", [P, G, P], 4)
        n2 = ring("n2", [P, G, P], 4)
        n3 = ring("n3", [P, G, P], 2)
        gates = ring("gates", [P, G2, 2, P], 2)
        y_all = sb("y_out", [P, 4, G * P])
        y_out = [y_all[:, i].rearrange("p (g f) -> p g f", g=G) for i in range(4)]
        rest0, rest1 = y_all[0:1, 0:3, :], sb("rest1", [1, 3, 512])
        small = ring("small", [P, 16, G], 4)
        stats = ring("stats", [P, 2, G, 6], 2)
        mv = ring("mv", [P, 2, G, 2], 4)

        s_pads = sem("pads_set")
        s_lists = sem("edge_lists_in_dram")
        s_weights = sem("weights_loaded")
        s_rows_in = sem("edge_rows_loaded")
        s_ident = sem("identity_made")
        s_const = sem("constants_made")
        s_turned = sem("setup_pe_done")
        s_prep = sem("setup_dve_done")
        s_table = sem("edge_table_stored")
        s_settled = sem("settled")
        s_list_steps = sem("edge_list_steps")
        s_zero = sem("zeros_made")
        s_fill_att = sem("att_rows_filled")
        s_fill_msg = sem("msg_rows_filled")

        softmax_edges = ("turned_src turned_dst copied_src copied_dst projected logits same fresh top carried "
                         "t0 d0 d1 exp total wv acc rows copied ")
        NAMES = {
            "e0": softmax_edges + "q prod inv agg",
            "e1": "weighted turned_src copied_src projected act same acc rows copied",
            "e2": "turned_src copied_src clipped onehot projected same acc rows copied",
            "e3": softmax_edges + "sloped h_projected",
            "n0": "turned copied product z gate diff mix stats mv var rstd norm scaled shifted act residual sum "
                  "stats2 mv2 var2 rstd2 out",
            "n1": "turned copied product sum stats mv var rstd out",
            "n2": "turned copied product gates rn npre n diff zd hn sum stats mv var rstd out",
            "n3": "turned copied product sloped z top pair exp s0 s1 inv coef xb y1 y2 stats mv var rstd norm scaled out",
        }
        DMAS = {
            "e0": {"table": 2, "src": ET, "dst": ET, "scattered": ET},
            "e1": {"table": 2, "src": ET, "scattered": ET},
            "e2": {"table": 3, "src": ET, "scattered": ET},
            "e3": {"table": 2, "src": ET, "dst": ET, "scattered": ET},
            "n0": {"loaded": 2, "stored": 1}, "n1": {"loaded": 2, "stored": 1}, "n2": {"loaded": 2, "stored": 1},
            "n3": {"loaded": 2, "stored": 1},
        }
        passes = [("e0", 0), ("n0", 0), ("e1", 0), ("n1", 0), ("e2", 0), ("n2", 0)]
        for l in range(L3):
            passes += [("e3", l), ("n3", l)]
        sems, value = {}, {}

        def pass_signals(kind, turn):
            steps = EG if kind[0] == "e" else NB2 if kind == "n2" else NB
            names, dmas = NAMES[kind], dict(DMAS[kind])
            if kind == "n3" and turn == L3 - 1:
                names += " sum stats2 mv2 var2 rstd2 out2"
                dmas["res"] = 1
            found = {}
            for name in names.split():
                key = ("edge_" if kind[0] == "e" else "node_") + name
                if key not in sems:
                    sems[key], value[key] = sem(key), 0
                found[name] = Signal(sems[key], steps, value[key])
                value[key] += steps
            for name, n in dmas.items():
                key = ("edge_" if kind[0] == "e" else "node_") + name
                if key not in sems:
                    sems[key], value[key] = [sem(f"{key}{u}") for u in range(U)], [0] * U
                found[name] = DmaSignals(sems[key], steps, n, value[key])
                value[key] = [v for _, v in found[name].end()]
            return found

        S = {p: pass_signals(*p) for p in passes}
        PREP_LISTS, PREP_TABLE, PREP_TURNED, PREP_ALL = 1, 2, 3, 13
        N_WEIGHTS = 48
        x_of = {("e0", 0): x, ("n0", 0): (x, xa), ("e1", 0): xa, ("n1", 0): (xa, xb),
                ("e2", 0): xb, ("n2", 0): (xb, xa), ("e3", 0): xa, ("n3", 0): (xa, xb),
                ("e3", 1): xb, ("n3", 1): (xb, out)}

        def node_rows(a, step, g, nb, width):
            if isinstance(step.h, int):
                base = min(step.index * g * P, N - g * P)
            else:
                base = step.index * (g * P)
            flat = a.rearrange("n f -> (n f)")
            return flat[bass.ds(base * width, g * P * width)].rearrange("(p k) -> p k", p=P)

        def settled(eng):
            eng.sem_inc(s_settled, 1)

        block = ctx.enter_context(nc.Block())

        @block.sync
        def _(sp):
            n_w = [0]

            def load(to, frm):
                sp.dma_start(to, frm).then_inc(s_weights, 16)
                n_w[0] += 1

            sp.dma_start(dst_pad[1:E + 1].rearrange("(a b) -> a b", a=8), dst.rearrange("(a b) -> a b", a=8)).then_inc(s_lists, 16)
            sp.dma_start(src_pad[0:E].rearrange("(a b) -> a b", a=8), src.rearrange("(a b) -> a b", a=8)).then_inc(s_lists, 16)
            sp.dma_start(type_pad[0:E].rearrange("(a b) -> a b", a=8), edge_type.rearrange("(a b) -> a b", a=8)).then_inc(s_lists, 16)
            sp.dma_start(weight_pad[0:E].rearrange("(a b) -> a b", a=8), edge_weight.rearrange("(a b) -> a b", a=8)).then_inc(s_lists, 16)
            sp.wait_ge(s_pads, 3)
            pad = EPAD - E
            sp.dma_start(dst_pad[0:1].unsqueeze(0), pad_vals[0:1, 0:1]).then_inc(s_lists, 16)
            sp.dma_start(dst_pad[E + 1:EPAD + 2].unsqueeze(0), pad_vals[0:1, 1:pad + 2]).then_inc(s_lists, 16)
            sp.dma_start(src_pad[E:EPAD].unsqueeze(0), pad_vals[0:1, 256:256 + pad]).then_inc(s_lists, 16)
            sp.dma_start(type_pad[E:EPAD].unsqueeze(0), pad_vals[0:1, 256:256 + pad]).then_inc(s_lists, 16)
            sp.dma_start(weight_pad[E:EPAD].unsqueeze(0), pad_vals[0:1, 256:256 + pad].bitcast(F32)).then_inc(s_lists, 16)
            sp.wait_ge(s_lists, 9 * 16)
            for k, (a, off) in enumerate([(src_pad, 0), (dst_pad, 1), (dst_pad, 2), (weight_pad, 0)]):
                lo = a[off:off + P * P].rearrange("(t p) -> t p", p=P)
                hi = a[off + P * P:off + EPAD].rearrange("(t p) -> t p", p=P)
                to = lists_w if k == 3 else lists[:, k]
                sp.dma_start(to[:, 0, :], lo).then_inc(s_rows_in, 16)
                sp.dma_start(to[0:TILES - P, 1, :], hi).then_inc(s_rows_in, 16)

            for i, w in enumerate((Wq, Wk, Wv, Ws)):
                load(wqkvs[:, i, :], w)
            load(w3[:, :, :], W3.rearrange("l i o -> i l o"))
            load(w_nat[:, POOL, :], pool_w)
            load(w_nat[:, FIN_X:FIN_A + 1, :], final_w.rearrange("o (c i) -> o c i", c=2))
            load(w_nat[:, MSG, :], W_msg)
            ih = W_ih.rearrange("(c o) i -> o c i", c=3)
            load(w_nat[:, IH, :], ih[:, 2, :])
            load(w_nat[:, IH + 1:IH + 3, :], ih[:, 0:2, :])
            load(w_nat[:, WS_T, :], Ws)
            load(w_nat[:, HH:HH + 3, :], W_hh.rearrange("(c o) i -> o c i", c=3))
            load(w_nat[:, W3_T:W3_T + L3, :], W3.rearrange("l i o -> i l o"))
            for c, v in ((BQ, bq), (BK, bk), (BV, bv), (BS, bs), (BPOOL, pool_b)):
                load(cols[:, c:c + 1], v.unsqueeze(1))
            for c in range(3):
                load(cols[:, WG + c:WG + c + 1], Wg[c * P:(c + 1) * P, :])
            for l in range(L3):
                load(cols[:, ASRC + l:ASRC + l + 1], att_src[l].unsqueeze(1))
                load(cols[:, ADST + l:ADST + l + 1], att_dst[l].unsqueeze(1))
            load(scal[:, 0:1], alpha.partition_broadcast(P))
            load(scal[:, 1:2], bg.partition_broadcast(P))
            load(embed[0:TYPES, 0, :], edge_embed)
            load(embed[0:TYPES, 1, :], b_msg.partition_broadcast(TYPES))
            load(wide[:, GAM0, :], gamma0.partition_broadcast(P))
            load(wide[:, BET0, :], beta0.partition_broadcast(P))
            for l in range(L3):
                load(wide[:, BIAS3 + l, :], bias3[l].partition_broadcast(P))
                load(wide[:, GAM3 + l, :], gamma3[l].partition_broadcast(P))
                load(wide[:, BET3 + l, :], beta3[l].partition_broadcast(P))
            for g in range(G):
                load(rows[:, 0, g * H:(g + 1) * H], bs.unsqueeze(0))
                load(rows[:, 1, g * H:(g + 1) * H], final_b.unsqueeze(0))
            sp.wait_ge(s_const, 1)
            load(rows[:, 2, 0:H], b_ih[2 * H:3 * H].unsqueeze(0))
            load(rows[:, 2, H:3 * H], b_ih[0:2 * H].unsqueeze(0))
            load(rows[:, 3, H:4 * H], b_hh.unsqueeze(0))
            assert n_w[0] == N_WEIGHTS, n_w

            sp.wait_ge(s_zero, 2)
            for a, w, s in ((att_rows, W0, s_fill_att), (msg_rows, H, s_fill_msg)):
                v = a.rearrange("(p j r) w -> j p (r w)", p=80, j=25)
                src_tile = zeros[:, :] if w == W0 else zeros_msg[:, :]
                for j in range(25):
                    sp.dma_start(v[j], src_tile).then_inc(s, 16)

            sp.wait_ge(s_prep, PREP_TABLE)
            sp.dma_start(edge_table, table_sb[:, :]).then_inc(s_table, 16)
            sp.wait_ge(s_table, 16)

            def edge_loads(kind, turn):
                s = S[kind, turn]

                def body(step):
                    u = step.u
                    if step.back(4).exists(EG):
                        sp.wait_ge(*s["scattered"].at(step.back(4)))
                    settled(sp)
                    sp.dma_start(etab[u][:, :], edge_table[:, bass.ds(step.index * (4 * ET), 4 * ET)]
                                 ).then_inc(s["table"].sem(step), 16)
                    sp.dma_start(dstb[u][:, :], dst_pad[bass.ds(step.index * EB, EB + 1)].partition_broadcast(P)
                                 ).then_inc(s["table"].sem(step), 16)
                    if kind == "e2":
                        sp.dma_start(typeb[u][0:TYPES, :],
                                     type_pad[bass.ds(step.index * EB, EB)].partition_broadcast(TYPES)
                                     ).then_inc(s["table"].sem(step), 16)
                run_steps(sp, EG, 0, body)

            def node_moves(kind, turn):
                s = S[kind, turn]
                g, nb = (G2, NB2) if kind == "n2" else (G, NB)
                x_now, x_new = x_of[kind, turn]
                msgs, w = (att_rows, W0) if kind in ("n0", "n3") else (msg_rows, H)
                last_use = "norm" if kind == "n3" and turn < L3 - 1 else "sum"
                out_sig = "out2" if (kind, turn) == ("n3", L3 - 1) else "out"
                for s_, v_ in S["e" + kind[1], turn]["scattered"].end():
                    sp.wait_ge(s_, v_)

                def body(step):
                    done = step.back(5)
                    if done.exists(nb):
                        sp.wait_ge(*s[out_sig].at(done))
                        if isinstance(done.h, int) and done.index == nb - 1:
                            sp.wait_ge(*s["stored"].at(done.back(1)))
                        settled(sp)
                        sp.dma_start(node_rows(x_new, done, g, nb, H),
                                     y_out[done.u][:, 0:g, :].rearrange("p g f -> p (g f)")
                                     ).then_inc(s["stored"].sem(done), 16)
                    if step.exists(nb):
                        u = step.u
                        if step.back(4).exists(nb):
                            sp.wait_ge(*s[last_use].at(step.back(4)))
                        settled(sp)
                        sp.dma_start(x_in[u][:, 0:g, :].rearrange("p g f -> p (g f)"), node_rows(x_now, step, g, nb, H)
                                     ).then_inc(s["loaded"].sem(step), 16)
                        to = msg_in[u][:, 0:g, :] if w == W0 else msg_in[u][:, :, :].rearrange(
                            "p g f -> p (g f)")[:, 0:g * H]
                        if w == W0:
                            to = to.rearrange("p g f -> p (g f)")
                        sp.dma_start(to, node_rows(msgs, step, g, nb, w)).then_inc(s["loaded"].sem(step), 16)
                        if out_sig == "out2":
                            sp.dma_start(x_res[u][:, :, :].rearrange("p g f -> p (g f)"),
                                         node_rows(xa, step, g, nb, H)).then_inc(s["res"].sem(step), 16)
                run_steps(sp, nb, 5, body, first=3)
                for s_, v_ in s["stored"].end():
                    sp.wait_ge(s_, v_)

            for kind, turn in passes:
                (edge_loads if kind[0] == "e" else node_moves)(kind, turn)

        @block.gpsimd
        def _(pool):
            gp = nc.gpsimd
            gp.memset(pad_vals[:, 0:1], -1).then_inc(s_pads, 1)
            gp.memset(pad_vals[:, 1:256], PAD_DST).then_inc(s_pads, 1)
            gp.memset(pad_vals[:, 256:512], 0).then_inc(s_pads, 1)
            gp.memset(zeros[:, :], 0.0).then_inc(s_zero, 1)
            pool.wait_ge(s_zero, 1)
            gp.memset(zeros[:, :].rearrange("p (r w) -> p r w", w=W0)[:, :, W0 - 1:W0], -BIG)
            gp.memset(zeros_msg[:, :], 0.0).then_inc(s_zero, 1)
            gp.memset(ident[:, :], 0.0).then_inc(s_ident, 1)
            pool.wait_ge(s_ident, 1)
            gp.affine_select(out=ident[:, :], in_=ident[:, :], compare_op=ALU.not_equal, fill=1.0, base=0,
                             pattern=[[-1, P]], channel_multiplier=1).then_inc(s_ident, 1)
            gp.iota(type_i[:, :], pattern=[[0, 1]], base=0, channel_multiplier=1).then_inc(s_ident, 1)
            gp.memset(neg_half[:, :], -0.5).then_inc(s_ident, 1)
            pool.wait_ge(s_ident, 4)

            def edge_moves(kind, turn):
                s = S[kind, turn]
                x_now = x_of[kind, turn]
                target = att_rows if kind in ("e0", "e3") else msg_rows
                w = W0 if kind in ("e0", "e3") else H
                if kind == "e0":
                    pool.wait_ge(s_fill_att, 16 * 25)
                elif kind == "e1":
                    pool.wait_ge(s_fill_msg, 16 * 25)
                if kind != "e0":
                    before = passes[passes.index((kind, turn)) - 1]
                    for s_, v_ in S[before]["stored"].end():
                        pool.wait_ge(s_, v_)

                def body(step):
                    u = step.u
                    if step.exists(EG):
                        pool.wait_ge(*s["table"].at(step))
                        if step.back(4).exists(EG):
                            pool.wait_ge(*s["turned_src"].at(step.back(4)))
                        settled(pool)
                        for k in range(ET):
                            gp.indirect_dma_start(
                                out=x_src[u][:, k, :], out_offset=None, in_=x_now,
                                in_offset=bass.IndirectOffsetOnAxis(ap=etab[u][:, k:k + 1], axis=0),
                            ).then_inc(s["src"].sem(step), 16)
                        if kind in ("e0", "e3"):
                            if step.back(4).exists(EG):
                                pool.wait_ge(*s["turned_dst"].at(step.back(4)))
                            settled(pool)
                            for k in range(ET):
                                gp.indirect_dma_start(
                                    out=x_dst[u][:, k, :], out_offset=None, in_=x_now,
                                    in_offset=bass.IndirectOffsetOnAxis(ap=etab[u][:, ET + k:ET + k + 1], axis=0),
                                ).then_inc(s["dst"].sem(step), 16)
                    done = step.back(2)
                    if done.exists(EG):
                        pool.wait_ge(*s["copied"].at(done))
                        settled(pool)
                        for k in range(ET):
                            rows_k = (row_out[done.u][:, k, :] if w == W0 else
                                      row_out[done.u][:, :, :].rearrange("p t f -> p (t f)")[:, k * H:(k + 1) * H])
                            gp.indirect_dma_start(
                                out=target,
                                out_offset=bass.IndirectOffsetOnAxis(ap=etab[done.u][:, 2 * ET + k:2 * ET + k + 1], axis=0),
                                in_=rows_k, in_offset=None, bounds_check=N - 1, oob_is_err=False,
                            ).then_inc(s["scattered"].sem(done), 16)
                run_steps(pool, EG, 2, body)

            def power(s, step, stat, g, var_sig, rstd_sig, mv_sig):
                u = step.u
                k = 2 * stat
                pool.wait_ge(*s[mv_sig].at(step))
                settled(pool)
                gp.tensor_scalar(small[u][:, 8 + k, 0:g], mv[u][:, stat, 0:g, 1], EPS, None, ALU.add
                                 ).then_inc(s[var_sig].sem, 1)
                pool.wait_ge(*s[var_sig].at(step))
                gp.tensor_tensor(small[u][:, 9 + k, 0:g], small[u][:, 8 + k, 0:g], neg_half[:, 0:g], ALU.pow
                                 ).then_inc(s[rstd_sig].sem, 1)

            def node_0(turn):
                s = S["n0", 0]

                def body(step):
                    if step.exists(NB):
                        power(s, step, 0, G, "var", "rstd", "mv")
                    one_back = step.back(1)
                    if one_back.exists(NB):
                        pool.wait_ge(*s["norm"].at(one_back))
                        gp.tensor_tensor(n2[one_back.u][:, :, :], n2[one_back.u][:, :, :],
                                         wide[:, GAM0, :].unsqueeze(1).broadcast_to([P, G, P]), ALU.mult
                                         ).then_inc(s["scaled"].sem, 1)
                        pool.wait_ge(*s["act"].at(one_back))
                        e = one_back.u % 2
                        gp.tensor_tensor(n3[e][:, :, :], n3[e][:, :, :], x_in[one_back.u][:, :, :], ALU.add
                                         ).then_inc(s["residual"].sem, 1)
                    two = step.back(2)
                    if two.exists(NB):
                        power(s, two, 1, G, "var2", "rstd2", "mv2")
                pool.wait_ge(s_weights, 16 * N_WEIGHTS)
                run_steps(pool, NB, 2, body)

            def node_1(turn):
                s = S["n1", 0]
                run_steps(pool, NB, 0, lambda step: power(s, step, 0, G, "var", "rstd", "mv"))

            def node_2(turn):
                s = S["n2", 0]
                run_steps(pool, NB2, 0, lambda step: power(s, step, 0, G2, "var", "rstd", "mv"))

            def node_3(turn):
                s = S["n3", turn]
                final = turn == L3 - 1

                def body(step):
                    if step.exists(NB):
                        u = step.u
                        pool.wait_ge(*s["loaded"].at(step))
                        gp.tensor_tensor(n1[u][:, :, :], x_in[u][:, :, :],
                                         wide[:, BIAS3 + turn, :].unsqueeze(1).broadcast_to([P, G, P]), ALU.add
                                         ).then_inc(s["xb"].sem, 1)
                        power(s, step, 0, G, "var", "rstd", "mv")
                    one_back = step.back(1)
                    if one_back.exists(NB):
                        pool.wait_ge(*s["norm"].at(one_back))
                        gp.tensor_tensor(n2[one_back.u][:, :, :], n2[one_back.u][:, :, :],
                                         wide[:, GAM3 + turn, :].unsqueeze(1).broadcast_to([P, G, P]), ALU.mult
                                         ).then_inc(s["scaled"].sem, 1)
                        if final:
                            power(s, one_back, 1, G, "var2", "rstd2", "mv2")
                run_steps(pool, NB, 1, body)

            nodes = {"n0": node_0, "n1": node_1, "n2": node_2, "n3": node_3}
            for kind, turn in passes:
                if kind[0] == "e":
                    edge_moves(kind, turn)
                else:
                    nodes[kind](turn)

        @block.tensor
        def _(pe):
            te = nc.tensor
            pe.wait_ge(s_ident, 2)
            pe.wait_ge(s_prep, 1)
            for k in range(4):
                te.transpose(banks[k][:, 0:P], lists_f[:, k, 0, :], ident[:, :])
                last = te.transpose(banks[k][:, P:TILES], lists_f[0:TILES - P, k, 1, :],
                                    ident[0:TILES - P, 0:TILES - P])
            last.then_inc(s_turned, 1)
            pe.wait_ge(s_weights, 16 * N_WEIGHTS)
            for i in range(13):
                last = te.transpose(banks[4 + i // 4][:, (i % 4) * P:(i % 4 + 1) * P], w_nat[:, i, :], ident[:, :])
            last.then_inc(s_turned, 1)
            pe.wait_ge(s_prep, PREP_TURNED)
            te.matmul(banks[0][:, 0:1], wT[:, WS_T, :], gate_w[:, 0:1], start=True, stop=True)
            for l in range(L3):
                te.matmul(banks[0][:, 1 + l:2 + l], wT[:, W3_T + l, :], cols[:, ASRC + l:ASRC + l + 1],
                          start=True, stop=True)
                te.matmul(banks[0][:, 1 + L3 + l:2 + L3 + l], wT[:, W3_T + l, :], cols[:, ADST + l:ADST + l + 1],
                          start=True, stop=True)
            te.matmul(banks[0][:, 5:6], bs_wide[:, :], gate_w[:, 0:1], start=True, stop=True).then_inc(s_turned, 1)
            pe.wait_ge(s_prep, PREP_ALL)

            def turn_edges(s, step, turn, which, bank, rows_in, ready, s_ready):
                pe.wait_ge(*ready)
                if step.back(1).exists(EG):
                    pe.wait_ge(*s["copied_" + which].at(step.back(1)))
                for k in range(ET):
                    last = te.transpose(banks[bank][:, k * P:(k + 1) * P], rows_in[:, k, :], ident[:, :])
                last.then_inc(s_ready.sem, 1)

            def edge(kind, turn):
                s = S[kind, turn]

                def body(step):
                    u, d = step.u, step.u % 2
                    before = step.back(1)
                    if step.exists(EG):
                        if kind == "e1":
                            turn_edges(s, step, turn, "src", 0, x_src[u], s["weighted"].at(step), s["turned_src"])
                        else:
                            turn_edges(s, step, turn, "src", 0, x_src[u], s["src"].at(step), s["turned_src"])
                        if kind in ("e0", "e3"):
                            turn_edges(s, step, turn, "dst", 1, x_dst[u], s["dst"].at(step), s["turned_dst"])
                        pe.wait_ge(*s["copied_src"].at(step))
                        if kind == "e0":
                            if before.exists(EG):
                                pe.wait_ge(*s["wv"].at(before))
                                pe.wait_ge(*s["prod"].at(before))
                            te.matmul(banks[2][:, :], wqkvs[:, 0, :], srcT[d][:, :], start=True, stop=True)
                            te.matmul(banks[4][:, :], wqkvs[:, 2, :], srcT[d][:, :], start=True, stop=True)
                            pe.wait_ge(*s["copied_dst"].at(step))
                            te.matmul(banks[3][:, :], wqkvs[:, 1, :], dstT[d][:, :], start=True, stop=True
                                      ).then_inc(s["projected"].sem, 1)
                        elif kind == "e1":
                            if before.exists(EG):
                                pe.wait_ge(*s["act"].at(before))
                            te.matmul(banks[2][:, :], wT[:, POOL, :], srcT[d][:, :], start=True, stop=True
                                      ).then_inc(s["projected"].sem, 1)
                        elif kind == "e2":
                            if before.exists(EG):
                                pe.wait_ge(*s["acc"].at(before))
                            te.matmul(banks[2][:, :], wT[:, MSG, :], srcT[d][:, :], start=True, stop=False)
                            pe.wait_ge(*s["onehot"].at(step))
                            te.matmul(banks[2][:, :], embed_b[0:TYPES, :], e1[d][0:TYPES, :], start=False, stop=True
                                      ).then_inc(s["projected"].sem, 1)
                        else:
                            if before.exists(EG):
                                pe.wait_ge(*s["logits"].at(before))
                            te.matmul(banks[5][:, :], att_wide[:, turn, :], srcT[d][:, :], start=True, stop=False)
                            pe.wait_ge(*s["copied_dst"].at(step))
                            te.matmul(banks[5][:, :], att_wide[:, L3 + turn, :], dstT[d][:, :], start=False, stop=True
                                      ).then_inc(s["projected"].sem, 1)
                            if before.exists(EG):
                                pe.wait_ge(*s["wv"].at(before))
                            te.matmul(banks[4][:, :], w3[:, turn, :], srcT[d][:, :], start=True, stop=True
                                      ).then_inc(s["h_projected"].sem, 1)
                    if before.exists(EG):
                        b = before.u % 2
                        if before.back(1).exists(EG):
                            pe.wait_ge(*s["copied"].at(before.back(1)))
                        if kind == "e0":
                            pe.wait_ge(*s["agg"].at(before))
                            for k in range(ET):
                                o = (k % 2) * 256
                                lhs = e2[b][:, k * P:(k + 1) * P]
                                te.transpose(banks[6 + k // 2][:, o:o + P], lhs, ident[:, :])
                                last = te.matmul(banks[6 + k // 2][:, o + P:o + P + 1], lhs, gate_w[:, 1:2],
                                                 start=True, stop=True)
                        elif kind == "e3":
                            pe.wait_ge(*s["acc"].at(before))
                            for k in range(ET):
                                o = (k % 2) * 256
                                cs = slice(k * P, (k + 1) * P)
                                te.transpose(banks[6 + k // 2][:, o:o + P], acc[b][:, cs], ident[:, :])
                                te.matmul(banks[6 + k // 2][:, o + P:o + P + 1], total[b][0:1, cs], one[0:1, 0:1],
                                          start=True, stop=True)
                                last = te.matmul(banks[6 + k // 2][:, o + P + 1:o + P + 2],
                                                 top[b][0:1, k * P + 1:(k + 1) * P + 1], one[0:1, 0:1],
                                                 start=True, stop=True)
                        else:
                            pe.wait_ge(*s["acc"].at(before))
                            for k in range(ET):
                                cs = slice(k * P, (k + 1) * P)
                                if kind == "e1":
                                    last = te.matmul(banks[6][:, cs], acc[b][:, cs], wT[:, FIN_A, :],
                                                     start=True, stop=True)
                                else:
                                    last = te.transpose(banks[6][:, cs], acc[b][:, cs], ident[:, :])
                        last.then_inc(s["rows"].sem, 1)
                    if step.exists(EG) and kind == "e0":
                        pe.wait_ge(*s["prod"].at(step))
                        if before.exists(EG):
                            pe.wait_ge(*s["d1"].at(before))
                        te.matmul(banks[5][:, :], head_ones[:, :], e1[d][:, :], start=True, stop=True
                                  ).then_inc(s["logits"].sem, 1)
                run_steps(pe, EG, 1, body)

            def node(kind, turn):
                s = S[kind, turn]
                g, nb = (G2, NB2) if kind == "n2" else (G, NB)
                e = S["e" + kind[1], turn]
                pe.wait_ge(*e["copied"].end())

                def body(step):
                    u, d = step.u, step.u % 2
                    two = step.back(2)
                    if step.exists(nb):
                        pe.wait_ge(*s["loaded"].at(step))
                        if two.exists(nb):
                            pe.wait_ge(*s["copied"].at(two))
                        for k in range(g):
                            last = te.transpose(banks[d][:, k * P:(k + 1) * P], x_in[u][:, k, :], ident[:, :])
                        if kind == "n2":
                            msgs = msg_in[u][:, :, :].rearrange("p g f -> p (g f)")
                            for k in range(g):
                                last = te.transpose(banks[d][:, (g + k) * P:(g + k + 1) * P],
                                                    msgs[:, k * P:(k + 1) * P], ident[:, :])
                        last.then_inc(s["turned"].sem, 1)
                    now = step.back(1)
                    if not now.exists(nb):
                        return
                    u, d = now.u, now.u % 2
                    two = now.back(2)
                    pe.wait_ge(*s["copied"].at(now))
                    if two.exists(nb):
                        pe.wait_ge(*s[{"n0": "diff", "n1": "sum", "n2": "npre", "n3": "y2"}[kind]].at(two))
                    if kind == "n0":
                        te.matmul(banks[2 + d][:, :], ones_bf[:, :], split[:, 0, :], start=True, stop=True)
                        for k in range(g):
                            te.matmul(banks[2 + d][:, k * P:(k + 1) * P], xT[d][:, k * P:(k + 1) * P], wqkvs[:, 3, :],
                                      start=False, stop=True, skip_group_check=True)
                            last = te.matmul(banks[4 + d][:, k:k + 1], xT[d][:, k * P:(k + 1) * P], products[:, 0:1],
                                             start=True, stop=True)
                    elif kind == "n1":
                        te.matmul(banks[2 + d][:, :], ones_bf[:, :], split[:, 1, :], start=True, stop=True)
                        te.matmul(banks[2 + d][:, :], ident[:, :],
                                  msg_in[u][:, :, :].rearrange("p g f -> p (g f)")[:, 0:g * P], start=False, stop=True,
                                  skip_group_check=True)
                        for k in range(g):
                            last = te.matmul(banks[2 + d][:, k * P:(k + 1) * P], xT[d][:, k * P:(k + 1) * P],
                                             wT[:, FIN_X, :], start=False, stop=True, skip_group_check=True)
                    elif kind == "n2":
                        for k in range(g):
                            bank = banks[2 + 2 * d + k]
                            te.matmul(bank[:, :], ones_bf[:, :], split[:, 2, :], start=True, stop=True)
                            te.matmul(bank[:, H:4 * H], xT[d][:, k * P:(k + 1) * P],
                                      wT[:, HH:HH + 3, :].rearrange("p c o -> p (c o)"),
                                      start=False, stop=True, skip_group_check=True)
                            last = te.matmul(bank[:, 0:3 * H], xT[d][:, (g + k) * P:(g + k + 1) * P],
                                             wT[:, IH:IH + 3, :].rearrange("p c o -> p (c o)"),
                                             start=False, stop=True, skip_group_check=True)
                    else:
                        for k in range(g):
                            xk = xT[d][:, k * P:(k + 1) * P]
                            te.matmul(banks[4 + d][:, k:k + 1], xk, self_col[:, turn:turn + 1], start=True, stop=True)
                            last = te.matmul(banks[2 + d][:, k * P:(k + 1) * P], xk, w3[:, turn, :],
                                             start=True, stop=True)
                    last.then_inc(s["product"].sem, 1)
                run_steps(pe, nb, 1, body)

            for kind, turn in passes:
                (edge if kind[0] == "e" else node)(kind, turn)

        @block.scalar
        def _(act):
            sc = nc.scalar
            act.wait_ge(s_prep, PREP_ALL)

            def edge(kind, turn):
                s = S[kind, turn]

                def body(step):
                    d = step.u % 2
                    two, before = step.back(2), step.back(1)
                    if step.exists(EG):
                        act.wait_ge(*s["turned_src"].at(step))
                        if two.exists(EG):
                            act.wait_ge(*s["h_projected" if kind == "e3" else "projected"].at(two))
                        sc.copy(srcT[d][:, :], banks[0][:, :]).then_inc(s["copied_src"].sem, 1)
                        if kind in ("e0", "e3"):
                            act.wait_ge(*s["turned_dst"].at(step))
                            sc.copy(dstT[d][:, :], banks[1][:, :]).then_inc(s["copied_dst"].sem, 1)
                        act.wait_ge(*s["projected"].at(step))
                        if kind == "e0":
                            if two.exists(EG):
                                act.wait_ge(*s["rows"].at(two))
                            sc.activation(e2[d][:, :], banks[2][:, :], ACT.Identity, bias=cols[:, BQ:BQ + 1]
                                          ).then_inc(s["q"].sem, 1)
                        elif kind == "e1":
                            if two.exists(EG):
                                act.wait_ge(*s["acc"].at(two))
                            sc.activation(e1[d][:, :], banks[2][:, :], ACT.Relu, bias=cols[:, BPOOL:BPOOL + 1]
                                          ).then_inc(s["act"].sem, 1)
                        elif kind == "e3":
                            if two.exists(EG):
                                act.wait_ge(*s["d1"].at(two))
                            sc.mul(e1[d][:, :], banks[5][:, :], SLOPE).then_inc(s["sloped"].sem, 1)
                    if before.exists(EG):
                        v = before.u
                        act.wait_ge(*s["rows"].at(before))
                        if before.back(4).exists(EG):
                            act.wait_ge(*s["scattered"].at(before.back(4)))
                        if kind in ("e0", "e3"):
                            w = H + 1 if kind == "e0" else H + 2
                            for k in range(2):
                                last = sc.copy(row_out[v][:, 2 * k:2 * k + 2, 0:w],
                                               banks[6 + k][:, :].rearrange("p (t f) -> p t f", t=2)[:, :, 0:w])
                        else:
                            last = sc.copy(row_out[v][:, :, :].rearrange("p t f -> p (t f)")[:, 0:EB], banks[6][:, :])
                        last.then_inc(s["copied"].sem, 1)
                    if step.exists(EG) and kind in ("e0", "e3"):
                        act.wait_ge(*s["d1"].at(step))
                        act.wait_ge(*s["d0"].at(step))
                        if two.exists(EG):
                            act.wait_ge(*s["acc"].at(two))
                        sc.activation(expd[d][:, :, :], pair[d][:, :, :], ACT.Exp).then_inc(s["exp"].sem, 1)
                run_steps(act, EG, 1, body)

            def node(kind, turn):
                s = S[kind, turn]
                g, nb = (G2, NB2) if kind == "n2" else (G, NB)

                def body(step):
                    d = step.u % 2
                    if step.exists(nb):
                        act.wait_ge(*s["turned"].at(step))
                        if step.back(2).exists(nb):
                            act.wait_ge(*s["product"].at(step.back(2)))
                        sc.copy(xT[d][:, :], banks[d][:, :]).then_inc(s["copied"].sem, 1)
                    now = step.back(1)
                    u, d = now.u, now.u % 2
                    if now.exists(nb):
                        if kind == "n0":
                            act.wait_ge(*s["z"].at(now))
                            sc.activation(small[u][:, 1, :], small[u][:, 0, :], ACT.Sigmoid, bias=scal[:, 2:3]
                                          ).then_inc(s["gate"].sem, 1)
                        elif kind == "n2":
                            act.wait_ge(*s["product"].at(now))
                            if now.back(2).exists(nb):
                                act.wait_ge(*s["zd"].at(now.back(2)))
                            for k in range(g):
                                last = sc.activation(gates[d][:, k, :, :].rearrange("p a f -> p (a f)"),
                                                     banks[2 + 2 * d + k][:, H:3 * H], ACT.Sigmoid)
                            last.then_inc(s["gates"].sem, 1)
                            act.wait_ge(*s["npre"].at(now))
                            sc.activation(n2[u][:, 0:g, :], n1[u][:, 0:g, :], ACT.Tanh).then_inc(s["n"].sem, 1)
                        elif kind == "n3":
                            act.wait_ge(*s["pair"].at(now))
                            sc.activation(small[u][:, 4:6, :], small[u][:, 2:4, :], ACT.Exp).then_inc(s["exp"].sem, 1)
                run_steps(act, nb, 1, body)

            for kind, turn in passes:
                (edge if kind[0] == "e" else node)(kind, turn)

        @block.vector
        def _(dve):
            ve = nc.vector
            prep = [0]

            def step_done(ins, at=None):
                prep[0] += 1
                ins.then_inc(s_prep, 1)
                dve.wait_ge(s_prep, prep[0])
                assert at is None or prep[0] == at, prep[0]

            ve.memset(rows[:, 2:4, :], 0.0).then_inc(s_const, 1)
            ve.memset(ones_bf[:, :], 1.0)
            ve.memset(split[:, :, :], 0.0)
            ve.memset(head_ones[:, :], 0.0).then_inc(s_const, 1)
            dve.wait_ge(s_const, 2)
            for k in range(HEADS):
                b = slice(k * HEAD, (k + 1) * HEAD)
                ve.memset(head_ones[b, b], float(HEAD) ** -0.5)
            for u in range(4):
                last = ve.memset(row_out[u][:, :, H:W0], -BIG)
            last.then_inc(s_const, 1)
            dve.wait_ge(s_const, 3)
            dve.wait_ge(s_rows_in, 8 * 16)
            T1 = TILES - P
            halves = ((slice(0, P), 0), (slice(0, T1), 1))
            chain = [0]

            def linked(ins):
                chain[0] += 1
                ins.then_inc(s_list_steps, 1)
                dve.wait_ge(s_list_steps, chain[0])

            for p, i in halves:
                ve.tensor_copy(lists_f[p, 0:3, i, :], lists[p, :, i, :])
                linked(ve.tensor_copy(lists_f[p, 3, i, :], lists_w[p, i, :]))
            for p, i in halves:
                linked(ve.tensor_tensor(lists_f[p, 2, i, :], lists_f[p, 1, i, :], lists_f[p, 2, i, :], ALU.is_equal))
                linked(ve.scalar_tensor_tensor(lists_f[p, 2, i, :], lists_f[p, 2, i, :], float(NO_ROW),
                                               lists_f[p, 1, i, :], ALU.mult, ALU.add))
                linked(ve.tensor_scalar(lists_f[p, 1, i, :], lists_f[p, 1, i, :], float(N - 1), None, ALU.min))
            step_done(ve.memset(one[:, :], 1.0), PREP_LISTS)
            dve.wait_ge(s_turned, 1)
            tab = table_sb[:, :].rearrange("p (g c k) -> p g c k", c=4, k=ET)
            for k in range(4):
                frm = banks[k][:, 0:TILES].rearrange("p (g k) -> p g k", k=ET)
                to = tab[:, :, k, :]
                if k == 3:
                    to = to.bitcast(F32)
                last = ve.tensor_copy(to, frm)
            step_done(last, PREP_TABLE)
            dve.wait_ge(s_turned, 2)
            for i in range(4):
                n = min(4, 13 - 4 * i)
                ve.tensor_copy(wT[:, 4 * i:4 * i + n, :].rearrange("p c o -> p (c o)"), banks[4 + i][:, 0:n * P])
            ve.tensor_tensor(gate_w[:, 0:1], cols[:, WG:WG + 1], cols[:, WG + 2:WG + 3], ALU.add)
            ve.tensor_tensor(gate_w[:, 1:2], cols[:, WG + 1:WG + 2], cols[:, WG + 2:WG + 3], ALU.subtract)
            step_done(ve.tensor_copy(bs_wide[:, :], cols[:, BS:BS + 1].broadcast_to([P, P])), PREP_TURNED)
            dve.wait_ge(s_turned, 3)
            step_done(ve.tensor_copy(products[:, 0:6], banks[0][:, 0:6]))
            step_done(ve.tensor_tensor(self_col[:, :], products[:, 1:1 + L3], products[:, 1 + L3:1 + 2 * L3], ALU.add))
            ve.tensor_tensor(scal[:, 2:3], products[:, 5:6], scal[:, 1:2], ALU.add)
            for i in range(2 * L3):
                ve.tensor_copy(att_wide[:, i, :], products[:, 1 + i:2 + i].broadcast_to([P, P]))
            dve.wait_ge(s_ident, 3)
            ve.tensor_copy(type_id[:, :], type_i[:, :])
            step_done(ve.tensor_tensor(embed_b[0:TYPES, :], embed[0:TYPES, 0, :], embed[0:TYPES, 1, :], ALU.add))
            step_done(ve.tensor_tensor(rows[:, 2, :], rows[:, 2, :], rows[:, 3, :], ALU.add))
            step_done(ve.tensor_copy(split[0:1, :, :], rows[:, 0:3, :]))
            step_done(ve.tensor_tensor(rest0, rows[:, 0:3, :], split[0:1, :, :], ALU.subtract))
            step_done(ve.tensor_copy(split[32:33, :, :], rest0))
            step_done(ve.tensor_copy(rest1[:, :, :], split[32:33, :, :]))
            step_done(ve.tensor_tensor(rest0, rest0, rest1[:, :, :], ALU.subtract))
            step_done(ve.tensor_copy(split[64:65, :, :], rest0), PREP_ALL)

            def edge(kind, turn):
                s = S[kind, turn]
                soft = kind in ("e0", "e3")

                def body(step):
                    if not step.exists(EG):
                        return
                    u, d = step.u, step.u % 2
                    o = 1 - d
                    before = step.back(1)
                    first = not before.exists(EG)
                    dve.wait_ge(*s["table"].at(step))
                    ve.tensor_tensor(same[d][:, :], dstb[u][:, 1:], dstb[u][:, 0:EB], ALU.is_equal
                                     ).then_inc(s["same"].sem, 1)
                    dve.wait_ge(*s["same"].at(step))
                    if kind == "e1":
                        dve.wait_ge(*s["src"].at(step))
                        w = etab[u][:, 3 * ET:4 * ET].bitcast(F32)
                        for k in range(ET):
                            last = ve.tensor_scalar(x_src[u][:, k, :], x_src[u][:, k, :], w[:, k:k + 1], None, ALU.mult)
                        last.then_inc(s["weighted"].sem, 1)
                        dve.wait_ge(*s["act"].at(step))
                        if step.back(2).exists(EG):
                            dve.wait_ge(*s["rows"].at(step.back(2)))
                        if not first:
                            dve.wait_ge(*s["acc"].at(before))
                        ve.tensor_tensor_scan(acc[d][:, :], same[d][:, :], e1[d][:, :],
                                              0.0 if first else acc[o][:, EB - 1:EB], ALU.mult, ALU.max
                                              ).then_inc(s["acc"].sem, 1)
                        return
                    if kind == "e2":
                        ve.tensor_scalar(e2[d][0:TYPES, :], typeb[u][0:TYPES, :], float(TYPES - 1), 0.0,
                                         ALU.min, ALU.max).then_inc(s["clipped"].sem, 1)
                        dve.wait_ge(*s["clipped"].at(step))
                        if step.back(2).exists(EG):
                            dve.wait_ge(*s["projected"].at(step.back(2)))
                        ve.tensor_scalar(e1[d][0:TYPES, :], e2[d][0:TYPES, :], type_id[0:TYPES, :], None, ALU.is_equal
                                         ).then_inc(s["onehot"].sem, 1)
                        dve.wait_ge(*s["projected"].at(step))
                        if step.back(2).exists(EG):
                            dve.wait_ge(*s["rows"].at(step.back(2)))
                        if not first:
                            dve.wait_ge(*s["acc"].at(before))
                        ve.tensor_tensor_scan(acc[d][:, :], same[d][:, :], banks[2][:, :],
                                              0.0 if first else acc[o][:, EB - 1:EB], ALU.mult, ALU.add
                                              ).then_inc(s["acc"].sem, 1)
                        return
                    ve.tensor_scalar(fresh[d][:, :], same[d][:, :], -1.0, BIG, ALU.add, ALU.mult
                                     ).then_inc(s["fresh"].sem, 1)
                    if kind == "e0":
                        dve.wait_ge(*s["q"].at(step))
                        if step.back(2).exists(EG):
                            dve.wait_ge(*s["logits"].at(step.back(2)))
                        ve.scalar_tensor_tensor(e1[d][:, :], banks[3][:, :], cols[:, BK:BK + 1], e2[d][:, :],
                                                ALU.add, ALU.mult).then_inc(s["prod"].sem, 1)
                    else:
                        dve.wait_ge(*s["sloped"].at(step))
                        ve.tensor_tensor(e1[d][:, :], e1[d][:, :], banks[5][:, :], ALU.max
                                         ).then_inc(s["logits"].sem, 1)
                    dve.wait_ge(*s["fresh"].at(step))
                    dve.wait_ge(*s["logits"].at(step))
                    logit = banks[5][:, :] if kind == "e0" else e1[d][:, :]
                    if step.back(2).exists(EG):
                        dve.wait_ge(*s["rows"].at(step.back(2)))
                    if first:
                        ve.memset(top[d][:, 0:1], 0.0).then_inc(s["carried"].sem, 1)
                    else:
                        dve.wait_ge(*s["top"].at(before))
                        ve.tensor_copy(top[d][:, 0:1], top[o][:, EB:EB + 1]).then_inc(s["carried"].sem, 1)
                    dve.wait_ge(*s["carried"].at(step))
                    ve.tensor_tensor_scan(top[d][:, 1:], fresh[d][:, :], logit, top[d][:, 0:1], ALU.add, ALU.max
                                          ).then_inc(s["top"].sem, 1)
                    if step.back(2).exists(EG):
                        dve.wait_ge(*s["exp"].at(step.back(2)))
                    dve.wait_ge(*s["top"].at(step))
                    ve.tensor_tensor(pair[d][:, 0, :], top[d][:, 0:EB], fresh[d][:, :], ALU.add
                                     ).then_inc(s["t0"].sem, 1)
                    ve.tensor_tensor(pair[d][:, 1, :], logit, top[d][:, 1:], ALU.subtract).then_inc(s["d1"].sem, 1)
                    dve.wait_ge(*s["t0"].at(step))
                    ve.tensor_tensor(pair[d][:, 0, :], pair[d][:, 0, :], top[d][:, 1:], ALU.subtract
                                     ).then_inc(s["d0"].sem, 1)
                    dve.wait_ge(*s["exp"].at(step))
                    if not first:
                        dve.wait_ge(*s["total"].at(before))
                    ve.tensor_tensor_scan(total[d][:, :], expd[d][:, 0, :], expd[d][:, 1, :],
                                          0.0 if first else total[o][:, EB - 1:EB], ALU.mult, ALU.add
                                          ).then_inc(s["total"].sem, 1)
                    if kind == "e0":
                        ve.scalar_tensor_tensor(e1[d][:, :], banks[4][:, :], cols[:, BV:BV + 1], expd[d][:, 1, :],
                                                ALU.add, ALU.mult).then_inc(s["wv"].sem, 1)
                    else:
                        dve.wait_ge(*s["h_projected"].at(step))
                        ve.tensor_tensor(e2[d][:, :], banks[4][:, :], expd[d][:, 1, :], ALU.mult
                                         ).then_inc(s["wv"].sem, 1)
                    dve.wait_ge(*s["wv"].at(step))
                    if not first:
                        dve.wait_ge(*s["acc"].at(before))
                    ve.tensor_tensor_scan(acc[d][:, :], expd[d][:, 0, :], (e1 if kind == "e0" else e2)[d][:, :],
                                          0.0 if first else acc[o][:, EB - 1:EB], ALU.mult, ALU.add
                                          ).then_inc(s["acc"].sem, 1)
                    if kind == "e0":
                        dve.wait_ge(*s["total"].at(step))
                        ve.reciprocal(same[d][:, :], total[d][:, :]).then_inc(s["inv"].sem, 1)
                        dve.wait_ge(*s["inv"].at(step))
                        dve.wait_ge(*s["acc"].at(step))
                        ve.tensor_tensor(e2[d][:, :], acc[d][:, :], same[d][:, :], ALU.mult).then_inc(s["agg"].sem, 1)
                run_steps(dve, EG, 0, body)

            def layernorm_stats(s, step, v, stat, g, stats_sig, mv_sig):
                u, d = step.u, step.u % 2
                for k in range(g):
                    last = ve.bn_stats(stats[d][:, stat, k, :], v[:, k, :])
                last.then_inc(stats_sig.sem, 1)
                dve.wait_ge(*stats_sig.at(step))
                settled(dve)
                for k in range(g):
                    last = ve.bn_aggr(mv[u][:, stat, k, :], stats[d][:, stat, k, :])
                last.then_inc(mv_sig.sem, 1)

            def normalise(step, v, to, stat, g):
                u = step.u
                for k in range(g):
                    last = ve.tensor_scalar(to[:, k, :], v[:, k, :], mv[u][:, stat, k, 0:1],
                                            small[u][:, 9 + 2 * stat, k:k + 1], ALU.subtract, ALU.mult)
                return last

            def finish(s, step, v, stat, g, rstd_sig, out_sig, nb):
                dve.wait_ge(*s[rstd_sig].at(step))
                if step.back(4).exists(nb):
                    dve.wait_ge(*s["stored"].at(step.back(4)))
                normalise(step, v, y_out[step.u], stat, g).then_inc(s[out_sig].sem, 1)

            def node_0(turn):
                s = S["n0", 0]

                def body(step):
                    u, d = step.u, step.u % 2
                    if step.exists(NB):
                        dve.wait_ge(*s["loaded"].at(step))
                        dve.wait_ge(*s["product"].at(step))
                        ve.tensor_tensor(small[u][:, 0, :], banks[4 + d][:, 0:G], msg_in[u][:, :, H], ALU.add
                                         ).then_inc(s["z"].sem, 1)
                        if step.back(4).exists(NB):
                            dve.wait_ge(*s["out"].at(step.back(4)))
                        ve.tensor_tensor(n1[u][:, :, :], banks[2 + d][:, :].rearrange("p (g f) -> p g f", g=G),
                                         msg_in[u][:, :, 0:H], ALU.subtract).then_inc(s["diff"].sem, 1)
                    one_back = step.back(1)
                    if one_back.exists(NB):
                        v = one_back.u
                        dve.wait_ge(*s["rstd"].at(one_back))
                        normalise(one_back, n2[v], n2[v], 0, G).then_inc(s["norm"].sem, 1)
                    if step.exists(NB):
                        dve.wait_ge(*s["gate"].at(step))
                        dve.wait_ge(*s["diff"].at(step))
                        for k in range(G):
                            last = ve.scalar_tensor_tensor(n2[u][:, k, :], n1[u][:, k, :], small[u][:, 1, k:k + 1],
                                                           msg_in[u][:, k, 0:H], ALU.mult, ALU.add)
                        last.then_inc(s["mix"].sem, 1)
                        dve.wait_ge(*s["mix"].at(step))
                        layernorm_stats(s, step, n2[u], 0, G, s["stats"], s["mv"])
                    if one_back.exists(NB):
                        v = one_back.u
                        dve.wait_ge(*s["scaled"].at(one_back))
                        ve.tensor_tensor(n2[v][:, :, :], n2[v][:, :, :],
                                         wide[:, BET0, :].unsqueeze(1).broadcast_to([P, G, P]), ALU.add
                                         ).then_inc(s["shifted"].sem, 1)
                        dve.wait_ge(*s["shifted"].at(one_back))
                        ve.tensor_scalar(n3[v % 2][:, :, :], n2[v][:, :, :], 0.0, scal[:, 0:1], ALU.min, ALU.mult
                                         ).then_inc(s["act"].sem, 1)
                    two = step.back(2)
                    if two.exists(NB):
                        v = two.u
                        dve.wait_ge(*s["residual"].at(two))
                        ve.scalar_tensor_tensor(n1[v][:, :, :], n2[v][:, :, :], 0.0, n3[v % 2][:, :, :],
                                                ALU.max, ALU.add).then_inc(s["sum"].sem, 1)
                        dve.wait_ge(*s["sum"].at(two))
                        layernorm_stats(s, two, n1[v], 1, G, s["stats2"], s["mv2"])
                    three = step.back(3)
                    if three.exists(NB):
                        finish(s, three, n1[three.u], 1, G, "rstd2", "out", NB)
                run_steps(dve, NB, 3, body)

            def node_1(turn):
                s = S["n1", 0]

                def body(step):
                    u, d = step.u, step.u % 2
                    if step.exists(NB):
                        dve.wait_ge(*s["product"].at(step))
                        ve.scalar_tensor_tensor(n1[u][:, :, :].rearrange("p g f -> p (g f)"), banks[2 + d][:, :], 0.0,
                                                x_in[u][:, :, :].rearrange("p g f -> p (g f)"), ALU.max, ALU.add
                                                ).then_inc(s["sum"].sem, 1)
                        dve.wait_ge(*s["sum"].at(step))
                        layernorm_stats(s, step, n1[u], 0, G, s["stats"], s["mv"])
                    one_back = step.back(1)
                    if one_back.exists(NB):
                        finish(s, one_back, n1[one_back.u], 0, G, "rstd", "out", NB)
                run_steps(dve, NB, 1, body)

            def node_2(turn):
                s = S["n2", 0]
                g = G2

                def gate_bank(d, k, c):
                    return banks[2 + 2 * d + k][:, c * H:(c + 1) * H]

                def body(step):
                    u, d = step.u, step.u % 2
                    if step.exists(NB2):
                        dve.wait_ge(*s["gates"].at(step))
                        for k in range(g):
                            last = ve.tensor_tensor(n1[u][:, k, :], gates[d][:, k, 0, :], gate_bank(d, k, 3), ALU.mult)
                        last.then_inc(s["rn"].sem, 1)
                        dve.wait_ge(*s["rn"].at(step))
                        for k in range(g):
                            last = ve.tensor_tensor(n1[u][:, k, :], n1[u][:, k, :], gate_bank(d, k, 0), ALU.add)
                        last.then_inc(s["npre"].sem, 1)
                    one_back = step.back(1)
                    if one_back.exists(NB2):
                        v, e = one_back.u, one_back.u % 2
                        dve.wait_ge(*s["n"].at(one_back))
                        ve.tensor_tensor(n3[e][:, 0:g, :], x_in[v][:, 0:g, :], n2[v][:, 0:g, :], ALU.subtract
                                         ).then_inc(s["diff"].sem, 1)
                        ve.tensor_tensor(n2[v][:, 0:g, :], n2[v][:, 0:g, :], x_in[v][:, 0:g, :], ALU.add
                                         ).then_inc(s["hn"].sem, 1)
                        dve.wait_ge(*s["diff"].at(one_back))
                        ve.tensor_tensor(n3[e][:, 0:g, :], n3[e][:, 0:g, :], gates[e][:, :, 1, :], ALU.mult
                                         ).then_inc(s["zd"].sem, 1)
                        dve.wait_ge(*s["zd"].at(one_back))
                        dve.wait_ge(*s["hn"].at(one_back))
                        ve.tensor_tensor(n2[v][:, 0:g, :], n2[v][:, 0:g, :], n3[e][:, 0:g, :], ALU.add
                                         ).then_inc(s["sum"].sem, 1)
                        dve.wait_ge(*s["sum"].at(one_back))
                        layernorm_stats(s, one_back, n2[v], 0, g, s["stats"], s["mv"])
                    two = step.back(2)
                    if two.exists(NB2):
                        finish(s, two, n2[two.u], 0, g, "rstd", "out", NB2)
                run_steps(dve, NB2, 2, body)

            def node_3(turn):
                s = S["n3", turn]
                final = turn == L3 - 1

                def body(step):
                    u, d = step.u, step.u % 2
                    if step.exists(NB):
                        dve.wait_ge(*s["loaded"].at(step))
                        dve.wait_ge(*s["product"].at(step))
                        sm = small[u]
                        ve.tensor_scalar(sm[:, 15, :], banks[4 + d][:, 0:G], SLOPE, None, ALU.mult
                                         ).then_inc(s["sloped"].sem, 1)
                        dve.wait_ge(*s["sloped"].at(step))
                        ve.tensor_tensor(sm[:, 0, :], sm[:, 15, :], banks[4 + d][:, 0:G], ALU.max
                                         ).then_inc(s["z"].sem, 1)
                        dve.wait_ge(*s["z"].at(step))
                        ve.tensor_tensor(sm[:, 1, :], sm[:, 0, :], msg_in[u][:, :, H + 1], ALU.max
                                         ).then_inc(s["top"].sem, 1)
                        dve.wait_ge(*s["top"].at(step))
                        ve.tensor_tensor(sm[:, 2, :], msg_in[u][:, :, H + 1], sm[:, 1, :], ALU.subtract)
                        ve.tensor_tensor(sm[:, 3, :], sm[:, 0, :], sm[:, 1, :], ALU.subtract
                                         ).then_inc(s["pair"].sem, 1)
                    one_back = step.back(1)
                    if one_back.exists(NB):
                        v = one_back.u
                        dve.wait_ge(*s["rstd"].at(one_back))
                        normalise(one_back, n1[v], n2[v], 0, G).then_inc(s["norm"].sem, 1)
                    if step.exists(NB):
                        dve.wait_ge(*s["exp"].at(step))
                        ve.tensor_tensor(sm[:, 6, :], sm[:, 4, :], msg_in[u][:, :, H], ALU.mult
                                         ).then_inc(s["s0"].sem, 1)
                        dve.wait_ge(*s["s0"].at(step))
                        ve.tensor_tensor(sm[:, 7, :], sm[:, 6, :], sm[:, 5, :], ALU.add).then_inc(s["s1"].sem, 1)
                        dve.wait_ge(*s["s1"].at(step))
                        ve.reciprocal(sm[:, 12, :], sm[:, 7, :]).then_inc(s["inv"].sem, 1)
                        dve.wait_ge(*s["inv"].at(step))
                        ve.tensor_tensor(sm[:, 13, :], sm[:, 4, :], sm[:, 12, :], ALU.mult)
                        ve.tensor_tensor(sm[:, 14, :], sm[:, 5, :], sm[:, 12, :], ALU.mult).then_inc(s["coef"].sem, 1)
                        dve.wait_ge(*s["coef"].at(step))
                        dve.wait_ge(*s["xb"].at(step))
                        for k in range(G):
                            last = ve.scalar_tensor_tensor(n1[u][:, k, :], msg_in[u][:, k, 0:H], sm[:, 13, k:k + 1],
                                                           n1[u][:, k, :], ALU.mult, ALU.add)
                        last.then_inc(s["y1"].sem, 1)
                        dve.wait_ge(*s["y1"].at(step))
                        for k in range(G):
                            last = ve.scalar_tensor_tensor(n1[u][:, k, :], banks[2 + d][:, k * P:(k + 1) * P],
                                                           sm[:, 14, k:k + 1], n1[u][:, k, :], ALU.mult, ALU.add)
                        last.then_inc(s["y2"].sem, 1)
                        dve.wait_ge(*s["y2"].at(step))
                        layernorm_stats(s, step, n1[u], 0, G, s["stats"], s["mv"])
                    if one_back.exists(NB):
                        v = one_back.u
                        dve.wait_ge(*s["scaled"].at(one_back))
                        beta = wide[:, BET3 + turn, :].unsqueeze(1).broadcast_to([P, G, P])
                        if not final:
                            if one_back.back(4).exists(NB):
                                dve.wait_ge(*s["stored"].at(one_back.back(4)))
                            ve.tensor_tensor(y_out[v][:, :, :], n2[v][:, :, :], beta, ALU.add
                                             ).then_inc(s["out"].sem, 1)
                        else:
                            ve.tensor_tensor(n2[v][:, :, :], n2[v][:, :, :], beta, ALU.add).then_inc(s["out"].sem, 1)
                            dve.wait_ge(*s["out"].at(one_back))
                            dve.wait_ge(*s["res"].at(one_back))
                            ve.tensor_tensor(n2[v][:, :, :], n2[v][:, :, :], x_res[v][:, :, :], ALU.add
                                             ).then_inc(s["sum"].sem, 1)
                            dve.wait_ge(*s["sum"].at(one_back))
                            layernorm_stats(s, one_back, n2[v], 1, G, s["stats2"], s["mv2"])
                    two = step.back(2)
                    if final and two.exists(NB):
                        finish(s, two, n2[two.u], 1, G, "rstd2", "out2", NB)
                run_steps(dve, NB, 2, body)

            nodes = {"n0": node_0, "n1": node_1, "n2": node_2, "n3": node_3}
            for kind, turn in passes:
                if kind[0] == "e":
                    edge(kind, turn)
                else:
                    nodes[kind](turn)


_INS = ['x', 'src', 'dst', 'edge_type_9', 'edge_weight',
        'L0_gnn_Wq', 'L0_gnn_bq', 'L0_gnn_Wk', 'L0_gnn_bk', 'L0_gnn_Wv', 'L0_gnn_bv', 'L0_gnn_Ws', 'L0_gnn_bs',
        'L0_gnn_Wg', 'L0_gnn_bg', 'L0_gnn_gamma', 'L0_gnn_beta', 'L0_gnn_alpha',
        'L1_gnn_pool_w', 'L1_gnn_pool_b', 'L1_gnn_final_w', 'L1_gnn_final_b',
        'L2_gnn_W_msg', 'L2_gnn_b_msg', 'L2_gnn_edge_embed', 'L2_gnn_W_ih', 'L2_gnn_W_hh', 'L2_gnn_b_ih', 'L2_gnn_b_hh',
        'L3_gnn_W', 'L3_gnn_att_src', 'L3_gnn_att_dst', 'L3_gnn_bias', 'L3_gnn_gamma', 'L3_gnn_beta']


def kernel(**inputs):
    import numpy as np
    import concourse.bacc as bacc
    from concourse import mybir as _mybir
    from concourse.bass_utils import run_bass_kernel_spmd

    nc = bacc.Bacc("TRN2", target_bir_lowering=False, num_devices=1)
    arrays, args = {}, []
    for name in _INS:
        a = np.ascontiguousarray(inputs[name])
        arrays[f"in_{name}"] = a
        args.append(nc.dram_tensor(f"in_{name}", a.shape, _mybir.dt.from_np(a.dtype), kind="ExternalInput").ap())
    out = nc.dram_tensor("out_x", inputs["x"].shape, _mybir.dt.float32, kind="ExternalOutput").ap()
    gnn_kernel(nc, *args, out)
    result = run_bass_kernel_spmd(nc, [arrays], core_ids=[0])
    return result.results[0]["out_x"]
```

```python
from contextlib import ExitStack

import concourse.bass as bass
from concourse import mybir

F32 = mybir.dt.float32
BF16 = mybir.dt.bfloat16
I32 = mybir.dt.int32
ALU = mybir.AluOpType
ACT = mybir.ActivationFunctionType

P = 128
U = 8
BIG = 1e30
NO_ROW = 65536
PAD_DST = 60000
EPS = 1e-5
SLOPE = 0.2


class Step:

    def __init__(self, h, u):
        self.h, self.u = h, u

    def back(self, k):
        t = self.u - k
        return Step(self.h + t // U if t < 0 else self.h, t % U)

    @property
    def index(self):
        return self.h * U + self.u

    def exists(self, n=None):
        return not isinstance(self.h, int) or 0 <= self.index and (n is None or self.index < n)


class Signal:

    def __init__(self, sem, steps, before):
        self.sem, self.steps, self.before = sem, steps, before

    def at(self, step):
        return self.sem, step.h * U + (step.u + 1 + self.before)

    def end(self):
        return self.sem, self.before + self.steps


class DmaSignals:

    def __init__(self, sems, steps, dmas, before):
        self.sems, self.steps, self.unit, self.before = sems, steps, 16 * dmas, before

    def sem(self, step):
        return self.sems[step.u]

    def at(self, step):
        return self.sems[step.u], step.h * self.unit + (self.unit + self.before[step.u])

    def end(self):
        return [(s, self.before[u] + self.unit * ((self.steps - u + U - 1) // U)) for u, s in enumerate(self.sems)]


class Ring(list):

    def __getitem__(self, u):
        return list.__getitem__(self, u % len(self))


def run_steps(eng, n, lag, body, first=2):
    last = (n - 1) // U
    for j in range(first * U):
        body(Step(j // U, j % U))
    with eng.Fori(first, last) as h:
        for u in range(U):
            body(Step(h, u))
    for j in range(last * U, n + lag):
        body(Step(j // U, j % U))


def gnn_kernel(nc, x, src, dst, edge_type, edge_weight,
               Wq, bq, Wk, bk, Wv, bv, Ws, bs, Wg, bg, gamma0, beta0, alpha,
               pool_w, pool_b, final_w, final_b,
               W_msg, b_msg, edge_embed, W_ih, W_hh, b_ih, b_hh,
               W3, att_src, att_dst, bias3, gamma3, beta3, out):
    N, H = x.shape
    E = src.shape[0]
    HEADS = 4
    HEAD = H // HEADS
    TYPES = edge_embed.shape[0]
    L3 = W3.shape[0]
    EB = 512
    ET = EB // P
    EG = -(-E // EB)
    EPAD = EG * EB
    TILES = EPAD // P
    W0 = H + 2
    G = 4
    NB = -(-N // (G * P))
    G2 = 2
    NB2 = -(-N // (G2 * P))
    assert H == P and TYPES <= P and N < NO_ROW

    ctx = ExitStack()
    with ctx:
        def sb(name, shape, dt=F32):
            return ctx.enter_context(nc.sbuf_tensor(name, shape, dt))

        def ring(name, shape, depth, dt=F32):
            whole = sb(name, [shape[0], depth, *shape[1:]], dt)
            return Ring(whole[:, i] for i in range(depth))

        def sem(name):
            return ctx.enter_context(nc.semaphore(name))

        def dram(name, shape, dt=F32):
            return nc.dram_tensor(name, shape, dt, kind="Internal").ap()

        dst_pad = dram("dst_pad", [EPAD + 2], I32)
        src_pad = dram("src_pad", [EPAD], I32)
        type_pad = dram("type_pad", [EPAD], I32)
        weight_pad = dram("weight_pad", [EPAD])
        edge_table = dram("edge_table", [P, EG * 4 * ET], I32)
        xa = dram("xa", [N, H])
        xb = dram("xb", [N, H])
        att_rows = dram("att_rows", [N, W0])
        msg_rows = dram("msg_rows", [N, H])

        psum = ctx.enter_context(nc.psum_tensor("psum", [P, 8, 512], F32))
        banks = [psum[:, i, :] for i in range(8)]
        row_banks = psum[:, 6:8, :].rearrange("p b (t f) -> p (b t) f", t=2)

        ident = sb("ident", [P, P])
        neg_ident = sb("neg_ident", [P, P])
        gate_heads = sb("gate_heads", [P, HEADS])
        head_first = sb("head_first", [P, HEADS])
        head_ones = sb("head_ones", [P, P])
        one = sb("one", [P, P])
        ones_bf = sb("ones_bf", [P, P], BF16)
        neg_half = sb("neg_half", [P, 2, G])
        w_nat = sb("w_nat", [P, 13, P])
        wT = sb("wT", [P, 16, P])
        POOL, FIN_X, FIN_A, MSG, IH, WS_T, HH, W3_T = 0, 1, 2, 3, 4, 7, 8, 11
        wqkvs = sb("wqkvs", [P, 4, P])
        w3 = sb("w3", [P, L3, P])
        cols = sb("cols", [P, 16])
        BQ, BK, BV, BS, BPOOL, WG, ASRC, ADST = 0, 1, 2, 3, 4, 5, 8, 10
        gate_w = sb("gate_w", [P, 2])
        bs_wide = sb("bs_wide", [P, P])
        products = sb("products", [P, 8])
        self_col = sb("self_col", [P, L3])
        att_wide = sb("att_wide", [P, 2 * L3, P])
        scal = sb("scal", [P, 4])
        embed = sb("embed", [P, 2, P])
        embed_b = sb("embed_b", [P, P])
        type_id = sb("type_id", [P, 1])
        wide = sb("wide", [P, 8, P])
        GAM0, BET0, BIAS3, GAM3, BET3 = 0, 1, 2, 4, 6
        rows = sb("rows", [1, 4, 512])
        split = sb("split", [P, 3, 512], BF16)
        zeros = sb("zeros", [80, 25 * W0])
        zeros_msg = sb("zeros_msg", [80, 25 * H])
        pad_vals = sb("pad_vals", [P, 512], I32)
        type_i = sb("type_i", [P, 1], I32)
        lists = sb("lists", [P, 3, 2, P], I32)
        lists_w = sb("lists_w", [P, 2, P])
        lists_f = sb("lists_f", [P, 4, 2, P])
        table_sb = sb("table_sb", [P, EG * 4 * ET], I32)

        etab = ring("etab", [P, 4 * ET], 4, I32)
        dstb = ring("dstb", [P, EB + 1], 4, I32)
        x_src = ring("x_src", [P, ET, P], 4)
        x_dst = ring("x_dst", [P, ET, P], 4)
        typeb = Ring(b.rearrange("p t f -> p (t f)").bitcast(I32) for b in x_dst)
        srcT = ring("srcT", [P, EB], 2)
        dstT = ring("dstT", [P, EB], 2)
        same = ring("same", [P, EB], 2)
        fresh = ring("fresh", [P, EB], 2)
        e1 = ring("e1", [P, EB], 2)
        e2 = ring("e2", [P, EB], 2)
        top = ring("top", [P, EB + 1], 2)
        pair = ring("pair", [P, 2, EB], 2)
        expd = ring("expd", [P, 2, EB], 2)
        total = ring("total", [P, EB], 2)
        acc = ring("acc", [P, EB], 2)
        row_out = ring("row_out", [P, ET, W0], 4)

        x_in, x_res, msg_in, xT = x_src, x_dst, row_out, srcT
        x_deep = Ring(list(x_src) + list(x_dst))

        def x_ring(kind):
            return x_in if kind == "n3" else x_deep

        n1 = ring("n1", [P, G, P], 4)
        n2 = ring("n2", [P, G, P], 4)
        n3 = ring("n3", [P, G, P], 2)
        gates = ring("gates", [P, G2, 2, P], 2)
        y_all = sb("y_out", [P, 4, G * P])
        y_out = Ring(y_all[:, i].rearrange("p (g f) -> p g f", g=G) for i in range(4))
        rest0, rest1 = y_all[0:1, 0:3, :], sb("rest1", [1, 3, 512])
        small = ring("small", [P, 16, G], 4)
        stats = ring("stats", [P, 2, G, 6], 2)
        mv = ring("mv", [P, 2, G, 2], 4)
        neg_mean = ring("neg_mean", [P, 2, G], 4)
        var_eps = ring("var_eps", [P, 2, G], 4)
        rstd = ring("rstd", [P, 2, G], 4)
        shift = ring("shift", [P, 2, G], 4)
        inv_heads = ring("inv_heads", [P, ET, HEADS], 2)
        head_dots = ring("head_dots", [P, ET, HEADS], 2)

        s_pads = sem("pads_set")
        s_lists = sem("edge_lists_in_dram")
        s_weights = sem("weights_loaded")
        s_rows_in = sem("edge_rows_loaded")
        s_ident = sem("identity_made")
        s_const = sem("constants_made")
        s_turned = sem("setup_pe_done")
        s_prep = sem("setup_dve_done")
        s_table = sem("edge_table_stored")
        s_settled = sem("settled")
        s_list_steps = sem("edge_list_steps")
        s_zero = sem("zeros_made")
        s_fill_att = sem("att_rows_filled")
        s_fill_msg = sem("msg_rows_filled")

        softmax_edges = ("turned_src turned_dst copied_src copied_dst projected logits same fresh top carried "
                         "t0 d0 d1 exp total wv acc rows copied ")
        NAMES = {
            "e0": softmax_edges + "q prod inv dots",
            "e1": "weighted turned_src copied_src projected act same acc rows copied",
            "e2": "turned_src copied_src clipped onehot projected same acc rows copied",
            "e3": softmax_edges + "sloped h_projected",
            "n0": "turned copied product z gate gated mix stats mv scaled shifted act residual sum stats2 mv2 "
                  "moments rstd shift norm out",
            "n1": "turned copied product sum stats mv moments rstd shift out",
            "n2": "turned copied product gates rn npre n diff zd hn sum stats mv moments rstd shift out",
            "n3": "turned copied product sloped z top pair exp s0 s1 inv coef own xb y1 y2 stats mv moments rstd "
                  "shift norm scaled out",
        }
        DMAS = {
            "e0": {"table": 2, "src": ET, "dst": ET, "scattered": ET},
            "e1": {"table": 2, "src": ET, "scattered": ET},
            "e2": {"table": 3, "src": ET, "scattered": ET},
            "e3": {"table": 2, "src": ET, "dst": ET, "scattered": ET},
            "n0": {"loaded": 2, "stored": 1}, "n1": {"loaded": 2, "stored": 1}, "n2": {"loaded": 2, "stored": 1},
            "n3": {"loaded": 2, "stored": 1},
        }
        passes = [("e0", 0), ("n0", 0), ("e1", 0), ("n1", 0), ("e2", 0), ("n2", 0)]
        for l in range(L3):
            passes += [("e3", l), ("n3", l)]
        sems, value = {}, {}

        def pass_signals(kind, turn):
            steps = EG if kind[0] == "e" else NB2 if kind == "n2" else NB
            names, dmas = NAMES[kind], dict(DMAS[kind])
            if kind == "n3" and turn == L3 - 1:
                names += " sum stats2 mv2 out2"
                dmas["res"] = 1
            powers = steps + {"n0": 6, "n1": 0, "n2": 1, "n3": 5 if turn == L3 - 1 else 4}.get(kind, 0)
            found = {}
            for name in names.split():
                key = ("edge_" if kind[0] == "e" else "node_") + name
                if key not in sems:
                    sems[key], value[key] = sem(key), 0
                found[name] = Signal(sems[key], powers if name in ("moments", "rstd", "shift") else steps, value[key])
                value[key] += found[name].steps
            for name, n in dmas.items():
                key = ("edge_" if kind[0] == "e" else "node_") + name
                if key not in sems:
                    sems[key], value[key] = [sem(f"{key}{u}") for u in range(U)], [0] * U
                found[name] = DmaSignals(sems[key], steps, n, value[key])
                value[key] = [v for _, v in found[name].end()]
            return found

        LAG = {"n0": 7, "n1": 2, "n2": 3, "n3": 6}
        STORE = {"n0": 9, "n1": 5, "n2": 6, "n3": 9}
        S = {p: pass_signals(*p) for p in passes}
        PREP_LISTS, PREP_TABLE, PREP_TURNED, PREP_ALL = 1, 2, 3, 13
        N_WEIGHTS = 48
        x_of = {("e0", 0): x, ("n0", 0): (x, xa), ("e1", 0): xa, ("n1", 0): (xa, xb),
                ("e2", 0): xb, ("n2", 0): (xb, xa), ("e3", 0): xa, ("n3", 0): (xa, xb),
                ("e3", 1): xb, ("n3", 1): (xb, out)}

        def node_rows(a, step, g, nb, width):
            if isinstance(step.h, int):
                base = min(step.index * g * P, N - g * P)
            else:
                base = step.index * (g * P)
            flat = a.rearrange("n f -> (n f)")
            return flat[bass.ds(base * width, g * P * width)].rearrange("(p k) -> p k", p=P)

        def settled(eng):
            eng.sem_inc(s_settled, 1)

        block = ctx.enter_context(nc.Block())

        @block.sync
        def _(sp):
            n_w = [0]

            def load(to, frm):
                sp.dma_start(to, frm).then_inc(s_weights, 16)
                n_w[0] += 1

            sp.dma_start(dst_pad[1:E + 1].rearrange("(a b) -> a b", a=8), dst.rearrange("(a b) -> a b", a=8)).then_inc(s_lists, 16)
            sp.dma_start(src_pad[0:E].rearrange("(a b) -> a b", a=8), src.rearrange("(a b) -> a b", a=8)).then_inc(s_lists, 16)
            sp.dma_start(type_pad[0:E].rearrange("(a b) -> a b", a=8), edge_type.rearrange("(a b) -> a b", a=8)).then_inc(s_lists, 16)
            sp.dma_start(weight_pad[0:E].rearrange("(a b) -> a b", a=8), edge_weight.rearrange("(a b) -> a b", a=8)).then_inc(s_lists, 16)
            sp.wait_ge(s_pads, 3)
            pad = EPAD - E
            sp.dma_start(dst_pad[0:1].unsqueeze(0), pad_vals[0:1, 0:1]).then_inc(s_lists, 16)
            sp.dma_start(dst_pad[E + 1:EPAD + 2].unsqueeze(0), pad_vals[0:1, 1:pad + 2]).then_inc(s_lists, 16)
            sp.dma_start(src_pad[E:EPAD].unsqueeze(0), pad_vals[0:1, 256:256 + pad]).then_inc(s_lists, 16)
            sp.dma_start(type_pad[E:EPAD].unsqueeze(0), pad_vals[0:1, 256:256 + pad]).then_inc(s_lists, 16)
            sp.dma_start(weight_pad[E:EPAD].unsqueeze(0), pad_vals[0:1, 256:256 + pad].bitcast(F32)).then_inc(s_lists, 16)
            sp.wait_ge(s_lists, 9 * 16)
            for k, (a, off) in enumerate([(src_pad, 0), (dst_pad, 1), (dst_pad, 2), (weight_pad, 0)]):
                lo = a[off:off + P * P].rearrange("(t p) -> t p", p=P)
                hi = a[off + P * P:off + EPAD].rearrange("(t p) -> t p", p=P)
                to = lists_w if k == 3 else lists[:, k]
                sp.dma_start(to[:, 0, :], lo).then_inc(s_rows_in, 16)
                sp.dma_start(to[0:TILES - P, 1, :], hi).then_inc(s_rows_in, 16)

            for i, w in enumerate((Wq, Wk, Wv, Ws)):
                load(wqkvs[:, i, :], w)
            load(w3[:, :, :], W3.rearrange("l i o -> i l o"))
            load(w_nat[:, POOL, :], pool_w)
            load(w_nat[:, FIN_X:FIN_A + 1, :], final_w.rearrange("o (c i) -> o c i", c=2))
            load(w_nat[:, MSG, :], W_msg)
            ih = W_ih.rearrange("(c o) i -> o c i", c=3)
            load(w_nat[:, IH, :], ih[:, 2, :])
            load(w_nat[:, IH + 1:IH + 3, :], ih[:, 0:2, :])
            load(w_nat[:, WS_T, :], Ws)
            load(w_nat[:, HH:HH + 3, :], W_hh.rearrange("(c o) i -> o c i", c=3))
            load(w_nat[:, W3_T:W3_T + L3, :], W3.rearrange("l i o -> i l o"))
            for c, v in ((BQ, bq), (BK, bk), (BV, bv), (BS, bs), (BPOOL, pool_b)):
                load(cols[:, c:c + 1], v.unsqueeze(1))
            for c in range(3):
                load(cols[:, WG + c:WG + c + 1], Wg[c * P:(c + 1) * P, :])
            for l in range(L3):
                load(cols[:, ASRC + l:ASRC + l + 1], att_src[l].unsqueeze(1))
                load(cols[:, ADST + l:ADST + l + 1], att_dst[l].unsqueeze(1))
            load(scal[:, 0:1], alpha.partition_broadcast(P))
            load(scal[:, 1:2], bg.partition_broadcast(P))
            load(embed[0:TYPES, 0, :], edge_embed)
            load(embed[0:TYPES, 1, :], b_msg.partition_broadcast(TYPES))
            load(wide[:, GAM0, :], gamma0.partition_broadcast(P))
            load(wide[:, BET0, :], beta0.partition_broadcast(P))
            for l in range(L3):
                load(wide[:, BIAS3 + l, :], bias3[l].partition_broadcast(P))
                load(wide[:, GAM3 + l, :], gamma3[l].partition_broadcast(P))
                load(wide[:, BET3 + l, :], beta3[l].partition_broadcast(P))
            for g in range(G):
                load(rows[:, 0, g * H:(g + 1) * H], bs.unsqueeze(0))
                load(rows[:, 1, g * H:(g + 1) * H], final_b.unsqueeze(0))
            sp.wait_ge(s_const, 1)
            load(rows[:, 2, 0:H], b_ih[2 * H:3 * H].unsqueeze(0))
            load(rows[:, 2, H:3 * H], b_ih[0:2 * H].unsqueeze(0))
            load(rows[:, 3, H:4 * H], b_hh.unsqueeze(0))
            assert n_w[0] == N_WEIGHTS, n_w

            sp.wait_ge(s_prep, PREP_TABLE)
            sp.dma_start(edge_table, table_sb[:, :]).then_inc(s_table, 16)
            sp.wait_ge(s_table, 16)

            def edge_loads(kind, turn):
                s = S[kind, turn]

                def body(step):
                    u = step.u
                    if step.back(4).exists(EG):
                        sp.wait_ge(*s["scattered"].at(step.back(4)))
                    settled(sp)
                    sp.dma_start(etab[u][:, :], edge_table[:, bass.ds(step.index * (4 * ET), 4 * ET)]
                                 ).then_inc(s["table"].sem(step), 16)
                    sp.dma_start(dstb[u][:, :], dst_pad[bass.ds(step.index * EB, EB + 1)].partition_broadcast(P)
                                 ).then_inc(s["table"].sem(step), 16)
                    if kind == "e2":
                        sp.dma_start(typeb[u][0:TYPES, :],
                                     type_pad[bass.ds(step.index * EB, EB)].partition_broadcast(TYPES)
                                     ).then_inc(s["table"].sem(step), 16)
                run_steps(sp, EG, 0, body)

            def node_moves(kind, turn):
                s = S[kind, turn]
                g, nb = (G2, NB2) if kind == "n2" else (G, NB)
                x_now, x_new = x_of[kind, turn]
                msgs, w = (att_rows, W0) if kind in ("n0", "n3") else (msg_rows, H)
                x_last, x_depth = {"n0": ("residual", 8), "n1": ("sum", 8), "n2": ("sum", 8), "n3": ("y1", 4)}[kind]
                msg_last = {"n0": "mix", "n1": "sum", "n2": "turned", "n3": "y1"}[kind]
                out_sig = "out2" if (kind, turn) == ("n3", L3 - 1) else "out"
                for s_, v_ in S["e" + kind[1], turn]["scattered"].end():
                    sp.wait_ge(s_, v_)

                def body(step):
                    if step.exists(nb):
                        u = step.u
                        if step.back(x_depth).exists(nb):
                            sp.wait_ge(*s[x_last].at(step.back(x_depth)))
                            settled(sp)
                        sp.dma_start(x_ring(kind)[u][:, 0:g, :].rearrange("p g f -> p (g f)"), node_rows(x_now, step, g, nb, H)
                                     ).then_inc(s["loaded"].sem(step), 16)
                        if step.back(4).exists(nb):
                            sp.wait_ge(*s[msg_last].at(step.back(4)))
                            settled(sp)
                        to = msg_in[u][:, 0:g, :] if w == W0 else msg_in[u][:, :, :].rearrange(
                            "p g f -> p (g f)")[:, 0:g * H]
                        if w == W0:
                            to = to.rearrange("p g f -> p (g f)")
                        sp.dma_start(to, node_rows(msgs, step, g, nb, w)).then_inc(s["loaded"].sem(step), 16)
                    late = step.back(3)
                    if out_sig == "out2" and late.exists(nb):
                        if late.back(4).exists(nb):
                            sp.wait_ge(*s["sum"].at(late.back(4)))
                            settled(sp)
                        sp.dma_start(x_res[late.u][:, :, :].rearrange("p g f -> p (g f)"),
                                     node_rows(xa, late, g, nb, H)).then_inc(s["res"].sem(late), 16)
                    done = step.back(STORE[kind])
                    if done.exists(nb):
                        sp.wait_ge(*s[out_sig].at(done))
                        if isinstance(done.h, int) and done.index == nb - 1:
                            sp.wait_ge(*s["stored"].at(done.back(1)))
                        settled(sp)
                        sp.dma_start(node_rows(x_new, done, g, nb, H),
                                     y_out[done.u][:, 0:g, :].rearrange("p g f -> p (g f)")
                                     ).then_inc(s["stored"].sem(done), 16)
                run_steps(sp, nb, STORE[kind], body)
                for s_, v_ in s["stored"].end():
                    sp.wait_ge(s_, v_)

            for kind, turn in passes:
                (edge_loads if kind[0] == "e" else node_moves)(kind, turn)

        @block.gpsimd
        def _(pool):
            gp = nc.gpsimd
            gp.memset(pad_vals[:, 0:1], -1).then_inc(s_pads, 1)
            gp.memset(pad_vals[:, 1:256], PAD_DST).then_inc(s_pads, 1)
            gp.memset(pad_vals[:, 256:512], 0).then_inc(s_pads, 1)
            gp.memset(zeros[:, :], 0.0).then_inc(s_zero, 1)
            pool.wait_ge(s_zero, 1)
            gp.memset(zeros[:, :].rearrange("p (r w) -> p r w", w=W0)[:, :, W0 - 1:W0], -BIG)
            gp.memset(zeros_msg[:, :], 0.0).then_inc(s_zero, 1)
            gp.memset(ident[:, :], 0.0).then_inc(s_ident, 1)
            pool.wait_ge(s_ident, 1)
            gp.affine_select(out=ident[:, :], in_=ident[:, :], compare_op=ALU.not_equal, fill=1.0, base=0,
                             pattern=[[-1, P]], channel_multiplier=1).then_inc(s_ident, 1)
            gp.iota(type_i[:, :], pattern=[[0, 1]], base=0, channel_multiplier=1).then_inc(s_ident, 1)
            gp.memset(neg_half[:, :, :], -0.5).then_inc(s_ident, 1)
            pool.wait_ge(s_ident, 4)

            def edge_moves(kind, turn):
                s = S[kind, turn]
                x_now = x_of[kind, turn]
                target = att_rows if kind in ("e0", "e3") else msg_rows
                w = W0 if kind in ("e0", "e3") else H
                if kind == "e1":
                    pool.wait_ge(s_fill_msg, 16 * 25)
                if kind != "e0":
                    before = passes[passes.index((kind, turn)) - 1]
                    for s_, v_ in S[before]["stored"].end():
                        pool.wait_ge(s_, v_)

                def body(step):
                    u = step.u
                    if step.exists(EG):
                        pool.wait_ge(*s["table"].at(step))
                        if step.back(4).exists(EG):
                            pool.wait_ge(*s["turned_src"].at(step.back(4)))
                        settled(pool)
                        for k in range(ET):
                            gp.indirect_dma_start(
                                out=x_src[u][:, k, :], out_offset=None, in_=x_now,
                                in_offset=bass.IndirectOffsetOnAxis(ap=etab[u][:, k:k + 1], axis=0),
                            ).then_inc(s["src"].sem(step), 16)
                        if kind in ("e0", "e3"):
                            if step.back(4).exists(EG):
                                pool.wait_ge(*s["turned_dst"].at(step.back(4)))
                            settled(pool)
                            for k in range(ET):
                                gp.indirect_dma_start(
                                    out=x_dst[u][:, k, :], out_offset=None, in_=x_now,
                                    in_offset=bass.IndirectOffsetOnAxis(ap=etab[u][:, ET + k:ET + k + 1], axis=0),
                                ).then_inc(s["dst"].sem(step), 16)
                    done = step.back(2)
                    if done.exists(EG):
                        pool.wait_ge(*s["copied"].at(done))
                        if kind == "e0" and isinstance(done.h, int) and done.index == 0:
                            pool.wait_ge(s_fill_att, 16 * 25)
                        settled(pool)
                        for k in range(ET):
                            rows_k = (row_out[done.u][:, k, :] if w == W0 else
                                      row_out[done.u][:, :, :].rearrange("p t f -> p (t f)")[:, k * H:(k + 1) * H])
                            gp.indirect_dma_start(
                                out=target,
                                out_offset=bass.IndirectOffsetOnAxis(ap=etab[done.u][:, 2 * ET + k:2 * ET + k + 1], axis=0),
                                in_=rows_k, in_offset=None, bounds_check=N - 1, oob_is_err=False,
                            ).then_inc(s["scattered"].sem(done), 16)
                run_steps(pool, EG, 2, body)

            def powers(s, step, first, second, nb, g):
                u = step.u
                one = step.back(first).exists(nb)
                two = second is not None and step.back(second).exists(nb)
                k = 1 if second is None else 2
                if one:
                    pool.wait_ge(*s["mv"].at(step.back(first)))
                if two:
                    pool.wait_ge(*s["mv2"].at(step.back(second)))
                settled(pool)
                gp.tensor_scalar(neg_mean[u][:, 0:k, 0:g], mv[u][:, 0:k, 0:g, 0], -1.0, None, ALU.mult)
                gp.tensor_scalar(var_eps[u][:, 0:k, 0:g], mv[u][:, 0:k, 0:g, 1], EPS, None, ALU.add
                                 ).then_inc(s["moments"].sem, 1)
                pool.wait_ge(*s["moments"].at(step))
                gp.tensor_tensor(rstd[u][:, 0:k, 0:g], var_eps[u][:, 0:k, 0:g], neg_half[:, 0:k, 0:g], ALU.pow
                                 ).then_inc(s["rstd"].sem, 1)
                pool.wait_ge(*s["rstd"].at(step))
                gp.tensor_tensor(shift[u][:, 0:k, 0:g], neg_mean[u][:, 0:k, 0:g], rstd[u][:, 0:k, 0:g], ALU.mult
                                 ).then_inc(s["shift"].sem, 1)

            def along(i):
                return wide[:, i, :].unsqueeze(1).broadcast_to([P, G, P])

            def node_0(turn):
                s = S["n0", 0]

                def body(step):
                    four, five = step.back(4), step.back(5)
                    if four.exists(NB):
                        pool.wait_ge(*s["norm"].at(four))
                        gp.tensor_tensor(n2[four.u], n2[four.u], along(GAM0), ALU.mult).then_inc(s["scaled"].sem, 1)
                    if five.exists(NB):
                        pool.wait_ge(*s["act"].at(five))
                        gp.tensor_tensor(n3[five.u % 2], n3[five.u % 2], x_deep[five.u], ALU.add
                                         ).then_inc(s["residual"].sem, 1)
                    powers(s, step, 2, 6, NB, G)
                pool.wait_ge(s_prep, PREP_ALL)
                run_steps(pool, NB, 6, body)

            def node_1(turn):
                s = S["n1", 0]
                run_steps(pool, NB, 0, lambda step: powers(s, step, 0, None, NB, G))

            def node_2(turn):
                s = S["n2", 0]

                def body(step):
                    one = step.back(1)
                    if one.exists(NB2):
                        pool.wait_ge(*s["n"].at(one))
                        pool.wait_ge(*s["diff"].at(one))
                        gp.tensor_tensor(n2[one.u][:, 0:G2, :], n2[one.u][:, 0:G2, :], x_deep[one.u][:, 0:G2, :], ALU.add
                                         ).then_inc(s["hn"].sem, 1)
                    powers(s, step, 1, None, NB2, G2)
                run_steps(pool, NB2, 1, body)

            def node_3(turn):
                s = S["n3", turn]
                final = turn == L3 - 1

                def body(step):
                    u = step.u
                    four = step.back(4)
                    if four.exists(NB):
                        pool.wait_ge(*s["norm"].at(four))
                        gp.tensor_tensor(n2[four.u], n2[four.u], along(GAM3 + turn), ALU.mult
                                         ).then_inc(s["scaled"].sem, 1)
                    if step.exists(NB):
                        pool.wait_ge(*s["loaded"].at(step))
                        gp.tensor_tensor(n1[u], x_in[u], along(BIAS3 + turn), ALU.add).then_inc(s["xb"].sem, 1)
                    powers(s, step, 2, 5 if final else None, NB, G)
                run_steps(pool, NB, 5 if final else 4, body)

            nodes = {"n0": node_0, "n1": node_1, "n2": node_2, "n3": node_3}
            for kind, turn in passes:
                if kind[0] == "e":
                    edge_moves(kind, turn)
                else:
                    nodes[kind](turn)

        @block.tensor
        def _(pe):
            te = nc.tensor
            pe.wait_ge(s_ident, 2)
            pe.wait_ge(s_prep, 1)
            for k in range(4):
                te.transpose(banks[k][:, 0:P], lists_f[:, k, 0, :], ident[:, :])
                last = te.transpose(banks[k][:, P:TILES], lists_f[0:TILES - P, k, 1, :],
                                    ident[0:TILES - P, 0:TILES - P])
            last.then_inc(s_turned, 1)
            pe.wait_ge(s_weights, 16 * N_WEIGHTS)
            for i in range(13):
                last = te.transpose(banks[4 + i // 4][:, (i % 4) * P:(i % 4 + 1) * P], w_nat[:, i, :], ident[:, :])
            last.then_inc(s_turned, 1)
            pe.wait_ge(s_prep, PREP_TURNED)
            te.matmul(banks[0][:, 0:1], wT[:, WS_T, :], gate_w[:, 0:1], start=True, stop=True)
            for l in range(L3):
                te.matmul(banks[0][:, 1 + l:2 + l], wT[:, W3_T + l, :], cols[:, ASRC + l:ASRC + l + 1],
                          start=True, stop=True)
                te.matmul(banks[0][:, 1 + L3 + l:2 + L3 + l], wT[:, W3_T + l, :], cols[:, ADST + l:ADST + l + 1],
                          start=True, stop=True)
            te.matmul(banks[0][:, 5:6], bs_wide[:, :], gate_w[:, 0:1], start=True, stop=True).then_inc(s_turned, 1)
            pe.wait_ge(s_prep, PREP_ALL)

            def turn_edges(s, step, turn, which, bank, rows_in, ready, s_ready):
                pe.wait_ge(*ready)
                if step.back(1).exists(EG):
                    pe.wait_ge(*s["copied_" + which].at(step.back(1)))
                for k in range(ET):
                    last = te.transpose(banks[bank][:, k * P:(k + 1) * P], rows_in[:, k, :], ident[:, :])
                last.then_inc(s_ready.sem, 1)

            def edge(kind, turn):
                s = S[kind, turn]

                def body(step):
                    u, d = step.u, step.u % 2
                    before = step.back(1)
                    if step.exists(EG):
                        if kind == "e1":
                            turn_edges(s, step, turn, "src", 0, x_src[u], s["weighted"].at(step), s["turned_src"])
                        else:
                            turn_edges(s, step, turn, "src", 0, x_src[u], s["src"].at(step), s["turned_src"])
                        if kind in ("e0", "e3"):
                            turn_edges(s, step, turn, "dst", 1, x_dst[u], s["dst"].at(step), s["turned_dst"])
                        pe.wait_ge(*s["copied_src"].at(step))
                        if kind == "e0":
                            if before.exists(EG):
                                pe.wait_ge(*s["wv"].at(before))
                                pe.wait_ge(*s["prod"].at(before))
                            te.matmul(banks[2][:, :], wqkvs[:, 0, :], srcT[d][:, :], start=True, stop=True)
                            te.matmul(banks[4][:, :], wqkvs[:, 2, :], srcT[d][:, :], start=True, stop=True)
                            pe.wait_ge(*s["copied_dst"].at(step))
                            te.matmul(banks[3][:, :], wqkvs[:, 1, :], dstT[d][:, :], start=True, stop=True
                                      ).then_inc(s["projected"].sem, 1)
                        elif kind == "e1":
                            if before.exists(EG):
                                pe.wait_ge(*s["act"].at(before))
                            te.matmul(banks[2][:, :], wT[:, POOL, :], srcT[d][:, :], start=True, stop=True
                                      ).then_inc(s["projected"].sem, 1)
                        elif kind == "e2":
                            if before.exists(EG):
                                pe.wait_ge(*s["acc"].at(before))
                            te.matmul(banks[2][:, :], wT[:, MSG, :], srcT[d][:, :], start=True, stop=False)
                            pe.wait_ge(*s["onehot"].at(step))
                            te.matmul(banks[2][:, :], embed_b[0:TYPES, :], e1[d][0:TYPES, :], start=False, stop=True
                                      ).then_inc(s["projected"].sem, 1)
                        else:
                            if before.exists(EG):
                                pe.wait_ge(*s["logits"].at(before))
                            te.matmul(banks[5][:, :], att_wide[:, turn, :], srcT[d][:, :], start=True, stop=False)
                            pe.wait_ge(*s["copied_dst"].at(step))
                            te.matmul(banks[5][:, :], att_wide[:, L3 + turn, :], dstT[d][:, :], start=False, stop=True
                                      ).then_inc(s["projected"].sem, 1)
                            if before.exists(EG):
                                pe.wait_ge(*s["wv"].at(before))
                            te.matmul(banks[4][:, :], w3[:, turn, :], srcT[d][:, :], start=True, stop=True
                                      ).then_inc(s["h_projected"].sem, 1)
                    if before.exists(EG):
                        b = before.u % 2
                        if before.back(1).exists(EG):
                            pe.wait_ge(*s["copied"].at(before.back(1)))
                        if kind == "e0":
                            pe.wait_ge(*s["acc"].at(before))
                            for k in range(ET):
                                cs = slice(k * P, (k + 1) * P)
                                te.transpose(row_banks[:, k, 0:P], acc[b][:, cs], ident[:, :])
                                te.matmul(row_banks[:, k, P:P + HEADS], acc[b][:, cs], gate_heads[:, :],
                                          start=True, stop=True)
                                last = te.matmul(row_banks[:, k, P + HEADS:P + 2 * HEADS], total[b][:, cs],
                                                 head_first[:, :], start=True, stop=True)
                        elif kind == "e3":
                            pe.wait_ge(*s["acc"].at(before))
                            for k in range(ET):
                                o = (k % 2) * 256
                                cs = slice(k * P, (k + 1) * P)
                                te.transpose(banks[6 + k // 2][:, o:o + P], acc[b][:, cs], ident[:, :])
                                te.matmul(banks[6 + k // 2][:, o + P:o + P + 1], total[b][0:1, cs], one[0:1, 0:1],
                                          start=True, stop=True)
                                last = te.matmul(banks[6 + k // 2][:, o + P + 1:o + P + 2],
                                                 top[b][0:1, k * P + 1:(k + 1) * P + 1], one[0:1, 0:1],
                                                 start=True, stop=True)
                        else:
                            pe.wait_ge(*s["acc"].at(before))
                            for k in range(ET):
                                cs = slice(k * P, (k + 1) * P)
                                if kind == "e1":
                                    last = te.matmul(banks[6][:, cs], acc[b][:, cs], wT[:, FIN_A, :],
                                                     start=True, stop=True)
                                else:
                                    last = te.transpose(banks[6][:, cs], acc[b][:, cs], ident[:, :])
                        last.then_inc(s["rows"].sem, 1)
                    if step.exists(EG) and kind == "e0":
                        pe.wait_ge(*s["prod"].at(step))
                        if before.exists(EG):
                            pe.wait_ge(*s["d1"].at(before))
                        te.matmul(banks[5][:, :], head_ones[:, :], e1[d][:, :], start=True, stop=True
                                  ).then_inc(s["logits"].sem, 1)
                run_steps(pe, EG, 1, body)

            def node(kind, turn):
                s = S[kind, turn]
                g, nb = (G2, NB2) if kind == "n2" else (G, NB)
                e = S["e" + kind[1], turn]
                pe.wait_ge(*e["copied"].end())

                def turn_rows(step):
                    u, d = step.u, step.u % 2
                    two = step.back(2)
                    if step.exists(nb):
                        pe.wait_ge(*s["loaded"].at(step))
                        if two.exists(nb):
                            pe.wait_ge(*s["copied"].at(two))
                        for k in range(g):
                            last = te.transpose(banks[d][:, k * P:(k + 1) * P], x_ring(kind)[u][:, k, :], ident[:, :])
                        if kind == "n2":
                            msgs = msg_in[u][:, :, :].rearrange("p g f -> p (g f)")
                            for k in range(g):
                                last = te.transpose(banks[d][:, (g + k) * P:(g + k + 1) * P],
                                                    msgs[:, k * P:(k + 1) * P], ident[:, :])
                        last.then_inc(s["turned"].sem, 1)

                def products_of(now):
                    u, d = now.u, now.u % 2
                    two = now.back(2)
                    pe.wait_ge(*s["copied"].at(now))
                    if two.exists(nb):
                        pe.wait_ge(*s[{"n0": "gated", "n1": "sum", "n2": "npre", "n3": "own"}[kind]].at(two))
                    if kind == "n0":
                        te.matmul(banks[2 + d][:, :], ones_bf[:, :], split[:, 0, :], start=True, stop=True)
                        te.matmul(banks[2 + d][:, :].rearrange("p (g f) -> p g f", g=g), neg_ident[:, :],
                                  msg_in[u][:, :, 0:H], start=False, stop=True, skip_group_check=True)
                        for k in range(g):
                            te.matmul(banks[2 + d][:, k * P:(k + 1) * P], xT[d][:, k * P:(k + 1) * P], wqkvs[:, 3, :],
                                      start=False, stop=True, skip_group_check=True)
                            last = te.matmul(banks[4 + d][:, k:k + 1], xT[d][:, k * P:(k + 1) * P], products[:, 0:1],
                                             start=True, stop=True)
                    elif kind == "n1":
                        te.matmul(banks[2 + d][:, :], ones_bf[:, :], split[:, 1, :], start=True, stop=True)
                        te.matmul(banks[2 + d][:, :], ident[:, :],
                                  msg_in[u][:, :, :].rearrange("p g f -> p (g f)")[:, 0:g * P], start=False, stop=True,
                                  skip_group_check=True)
                        for k in range(g):
                            last = te.matmul(banks[2 + d][:, k * P:(k + 1) * P], xT[d][:, k * P:(k + 1) * P],
                                             wT[:, FIN_X, :], start=False, stop=True, skip_group_check=True)
                    elif kind == "n2":
                        for k in range(g):
                            bank = banks[2 + 2 * d + k]
                            te.matmul(bank[:, :], ones_bf[:, :], split[:, 2, :], start=True, stop=True)
                            te.matmul(bank[:, H:4 * H], xT[d][:, k * P:(k + 1) * P],
                                      wT[:, HH:HH + 3, :].rearrange("p c o -> p (c o)"),
                                      start=False, stop=True, skip_group_check=True)
                            last = te.matmul(bank[:, 0:3 * H], xT[d][:, (g + k) * P:(g + k + 1) * P],
                                             wT[:, IH:IH + 3, :].rearrange("p c o -> p (c o)"),
                                             start=False, stop=True, skip_group_check=True)
                    else:
                        for k in range(g):
                            xk = xT[d][:, k * P:(k + 1) * P]
                            te.matmul(banks[4 + d][:, k:k + 1], xk, self_col[:, turn:turn + 1], start=True, stop=True)
                            last = te.matmul(banks[2 + d][:, k * P:(k + 1) * P], xk, w3[:, turn, :],
                                             start=True, stop=True)
                    last.then_inc(s["product"].sem, 1)

                def body(step):
                    turn_rows(step)
                    if step.back(1).exists(nb):
                        products_of(step.back(1))

                run_steps(pe, nb, 1, body)

            for kind, turn in passes:
                (edge if kind[0] == "e" else node)(kind, turn)

        @block.scalar
        def _(act):
            sc = nc.scalar
            def fill(a, w, tile_, signal, j):
                v = a.rearrange("(p q) w -> p (q w)", p=80)
                act.dma_start(v[:, bass.ds(j * (25 * w), 25 * w)], tile_).then_inc(signal, 16)

            act.wait_ge(s_zero, 2)
            act.wait_ge(s_weights, 16 * N_WEIGHTS)
            for j in range(25):
                fill(att_rows, W0, zeros[:, :], s_fill_att, j)
            act.wait_ge(s_prep, PREP_ALL)

            def edge(kind, turn):
                s = S[kind, turn]

                def body(step):
                    d = step.u % 2
                    two, before = step.back(2), step.back(1)
                    last_step = isinstance(step.h, int) and step.index == EG - 1
                    if kind == "e0" and step.exists(EG) and (step.u % 2 == 1 or last_step):
                        fill(msg_rows, H, zeros_msg[:, :], s_fill_msg, step.h * (U // 2) + step.u // 2)
                    if step.exists(EG):
                        act.wait_ge(*s["turned_src"].at(step))
                        if two.exists(EG):
                            act.wait_ge(*s["h_projected" if kind == "e3" else "projected"].at(two))
                        sc.copy(srcT[d][:, :], banks[0][:, :]).then_inc(s["copied_src"].sem, 1)
                        if kind in ("e0", "e3"):
                            act.wait_ge(*s["turned_dst"].at(step))
                            sc.copy(dstT[d][:, :], banks[1][:, :]).then_inc(s["copied_dst"].sem, 1)
                        act.wait_ge(*s["projected"].at(step))
                        if kind == "e0":
                            if two.exists(EG):
                                act.wait_ge(*s["prod"].at(two))
                            sc.activation(e2[d][:, :], banks[2][:, :], ACT.Identity, bias=cols[:, BQ:BQ + 1]
                                          ).then_inc(s["q"].sem, 1)
                        elif kind == "e1":
                            if two.exists(EG):
                                act.wait_ge(*s["acc"].at(two))
                            sc.activation(e1[d][:, :], banks[2][:, :], ACT.Relu, bias=cols[:, BPOOL:BPOOL + 1]
                                          ).then_inc(s["act"].sem, 1)
                        elif kind == "e3":
                            if two.exists(EG):
                                act.wait_ge(*s["d1"].at(two))
                            sc.mul(e1[d][:, :], banks[5][:, :], SLOPE).then_inc(s["sloped"].sem, 1)
                    if before.exists(EG) and kind != "e0":
                        v = before.u
                        act.wait_ge(*s["rows"].at(before))
                        if before.back(4).exists(EG):
                            act.wait_ge(*s["scattered"].at(before.back(4)))
                        if kind == "e3":
                            last = sc.copy(row_out[v], row_banks[:, :, 0:W0])
                        else:
                            last = sc.copy(row_out[v][:, :, :].rearrange("p t f -> p (t f)")[:, 0:EB], banks[6][:, :])
                        last.then_inc(s["copied"].sem, 1)
                    if step.exists(EG) and kind in ("e0", "e3"):
                        act.wait_ge(*s["d1"].at(step))
                        act.wait_ge(*s["d0"].at(step))
                        if two.exists(EG):
                            act.wait_ge(*s["acc"].at(two))
                        sc.activation(expd[d][:, :, :], pair[d][:, :, :], ACT.Exp).then_inc(s["exp"].sem, 1)
                run_steps(act, EG, 1, body)

            def node(kind, turn):
                s = S[kind, turn]
                g, nb = (G2, NB2) if kind == "n2" else (G, NB)
                final = turn == L3 - 1

                def normalise(block, computed, v, to, stat, sig):
                    act.wait_ge(*s["shift"].at(computed))
                    c = computed.u
                    for k in range(g):
                        last = sc.activation(to[:, k, :], v[:, k, :], ACT.Identity,
                                             scale=rstd[c][:, stat, k:k + 1], bias=shift[c][:, stat, k:k + 1])
                    last.then_inc(s[sig].sem, 1)

                def turned_x(step):
                    act.wait_ge(*s["turned"].at(step))
                    if step.back(2).exists(nb):
                        act.wait_ge(*s["product"].at(step.back(2)))
                    sc.copy(xT[step.u % 2][:, :], banks[step.u % 2][:, :]).then_inc(s["copied"].sem, 1)

                def first_norm(step):
                    mid = step.back(3)
                    if mid.exists(nb):
                        if kind == "n3" and final and mid.back(4).exists(nb):
                            act.wait_ge(*s["out2"].at(mid.back(4)))
                        if kind == "n0" and mid.back(4).exists(nb):
                            act.wait_ge(*s["out"].at(mid.back(4)))
                        normalise(mid, step.back(1), n1[mid.u], n2[mid.u], 0, "norm")

                def last_norm(step):
                    end = step.back(LAG[kind])
                    if end.exists(nb):
                        if end.back(4).exists(nb):
                            act.wait_ge(*s["stored"].at(end.back(4)))
                        computed = {"n0": 1, "n1": 2, "n2": 2, "n3": 1}[kind]
                        normalise(end, step.back(computed), (n1 if kind == "n1" else n2)[end.u], y_out[end.u],
                                  1 if kind in ("n0", "n3") else 0, "out2" if kind == "n3" else "out")

                def body(step):
                    now = step.back(1)
                    u, d = now.u, now.u % 2
                    if kind == "n0":
                        if step.exists(nb):
                            turned_x(step)
                        if now.exists(nb):
                            act.wait_ge(*s["z"].at(now))
                            sc.activation(small[u][:, 1, :], small[u][:, 0, :], ACT.Sigmoid, bias=scal[:, 2:3]
                                          ).then_inc(s["gate"].sem, 1)
                        if now.exists(nb):
                            act.wait_ge(*s["gate"].at(now))
                            for k in range(g):
                                last = sc.activation(n1[u][:, k, :], banks[2 + d][:, k * P:(k + 1) * P], ACT.Copy,
                                                     scale=small[u][:, 1, k:k + 1])
                            last.then_inc(s["gated"].sem, 1)
                        last_norm(step)
                        first_norm(step)
                    elif kind == "n1":
                        if step.exists(nb):
                            turned_x(step)
                        last_norm(step)
                    elif kind == "n2":
                        if step.exists(nb):
                            turned_x(step)
                        if now.exists(nb):
                            act.wait_ge(*s["product"].at(now))
                            if now.back(2).exists(nb):
                                act.wait_ge(*s["zd"].at(now.back(2)))
                            sc.activation(gates[d].rearrange("p k a f -> p k (a f)"),
                                          psum[:, 2 + 2 * d:4 + 2 * d, H:3 * H], ACT.Sigmoid
                                          ).then_inc(s["gates"].sem, 1)
                            act.wait_ge(*s["npre"].at(now))
                            sc.activation(n2[u][:, 0:g, :], n1[u][:, 0:g, :], ACT.Tanh).then_inc(s["n"].sem, 1)
                        last_norm(step)
                    else:
                        if step.exists(nb):
                            turned_x(step)
                        if now.exists(nb):
                            act.wait_ge(*s["pair"].at(now))
                            sc.activation(small[u][:, 4:6, :], small[u][:, 2:4, :], ACT.Exp).then_inc(s["exp"].sem, 1)
                        first_norm(step)
                        if now.exists(nb):
                            act.wait_ge(*s["coef"].at(now))
                            if now.back(2).exists(nb):
                                act.wait_ge(*s["y2"].at(now.back(2)))
                            for k in range(g):
                                last = sc.activation(n3[d][:, k, :], banks[2 + d][:, k * P:(k + 1) * P], ACT.Copy,
                                                     scale=small[u][:, 14, k:k + 1])
                            last.then_inc(s["own"].sem, 1)
                        if final:
                            last_norm(step)
                run_steps(act, nb, 3 if kind == "n3" and not final else LAG[kind], body)

            for kind, turn in passes:
                (edge if kind[0] == "e" else node)(kind, turn)

        @block.vector
        def _(dve):
            ve = nc.vector
            prep = [0]

            def step_done(ins, at=None):
                prep[0] += 1
                ins.then_inc(s_prep, 1)
                dve.wait_ge(s_prep, prep[0])
                assert at is None or prep[0] == at, prep[0]

            ve.memset(rows[:, 2:4, :], 0.0).then_inc(s_const, 1)
            ve.memset(ones_bf[:, :], 1.0)
            ve.memset(split[:, :, :], 0.0)
            ve.memset(head_ones[:, :], 0.0).then_inc(s_const, 1)
            dve.wait_ge(s_const, 2)
            for k in range(HEADS):
                b = slice(k * HEAD, (k + 1) * HEAD)
                ve.memset(head_ones[b, b], float(HEAD) ** -0.5)
            for u in range(4):
                ve.memset(mv[u], 1.0)
            ve.memset(gate_heads[:, :], 0.0)
            ve.memset(head_first[:, :], 0.0)
            for u in range(4):
                last = ve.memset(row_out[u][:, :, H:W0], -BIG)
            last.then_inc(s_const, 1)
            dve.wait_ge(s_const, 3)
            dve.wait_ge(s_rows_in, 8 * 16)
            T1 = TILES - P
            halves = ((slice(0, P), 0), (slice(0, T1), 1))
            chain = [0]

            def linked(ins):
                chain[0] += 1
                ins.then_inc(s_list_steps, 1)
                dve.wait_ge(s_list_steps, chain[0])

            for p, i in halves:
                ve.tensor_copy(lists_f[p, 0:3, i, :], lists[p, :, i, :])
                linked(ve.tensor_copy(lists_f[p, 3, i, :], lists_w[p, i, :]))
            for p, i in halves:
                linked(ve.tensor_tensor(lists_f[p, 2, i, :], lists_f[p, 1, i, :], lists_f[p, 2, i, :], ALU.is_equal))
                linked(ve.scalar_tensor_tensor(lists_f[p, 2, i, :], lists_f[p, 2, i, :], float(NO_ROW),
                                               lists_f[p, 1, i, :], ALU.mult, ALU.add))
                linked(ve.tensor_scalar(lists_f[p, 1, i, :], lists_f[p, 1, i, :], float(N - 1), None, ALU.min))
            step_done(ve.memset(one[:, :], 1.0), PREP_LISTS)
            dve.wait_ge(s_turned, 1)
            tab = table_sb[:, :].rearrange("p (g c k) -> p g c k", c=4, k=ET)
            for k in range(4):
                frm = banks[k][:, 0:TILES].rearrange("p (g k) -> p g k", k=ET)
                to = tab[:, :, k, :]
                if k == 3:
                    to = to.bitcast(F32)
                last = ve.tensor_copy(to, frm)
            step_done(last, PREP_TABLE)
            dve.wait_ge(s_turned, 2)
            for i in range(4):
                n = min(4, 13 - 4 * i)
                ve.tensor_copy(wT[:, 4 * i:4 * i + n, :].rearrange("p c o -> p (c o)"), banks[4 + i][:, 0:n * P])
            ve.tensor_tensor(gate_w[:, 0:1], cols[:, WG:WG + 1], cols[:, WG + 2:WG + 3], ALU.add)
            ve.tensor_tensor(gate_w[:, 1:2], cols[:, WG + 1:WG + 2], cols[:, WG + 2:WG + 3], ALU.subtract)
            step_done(ve.tensor_copy(bs_wide[:, :], cols[:, BS:BS + 1].broadcast_to([P, P])), PREP_TURNED)
            dve.wait_ge(s_turned, 3)
            step_done(ve.tensor_copy(products[:, 0:6], banks[0][:, 0:6]))
            step_done(ve.tensor_tensor(self_col[:, :], products[:, 1:1 + L3], products[:, 1 + L3:1 + 2 * L3], ALU.add))
            ve.tensor_tensor(scal[:, 2:3], products[:, 5:6], scal[:, 1:2], ALU.add)
            for i in range(2 * L3):
                ve.tensor_copy(att_wide[:, i, :], products[:, 1 + i:2 + i].broadcast_to([P, P]))
            dve.wait_ge(s_ident, 3)
            ve.tensor_copy(type_id[:, :], type_i[:, :])
            step_done(ve.tensor_tensor(embed_b[0:TYPES, :], embed[0:TYPES, 0, :], embed[0:TYPES, 1, :], ALU.add))
            for k in range(HEADS):
                b = slice(k * HEAD, (k + 1) * HEAD)
                ve.tensor_copy(gate_heads[b, k:k + 1], gate_w[b, 1:2])
                ve.memset(head_first[k * HEAD:k * HEAD + 1, k:k + 1], 1.0)
            ve.tensor_scalar(neg_ident[:, :], ident[:, :], -1.0, None, ALU.mult)
            step_done(ve.tensor_tensor(rows[:, 2, :], rows[:, 2, :], rows[:, 3, :], ALU.add))
            step_done(ve.tensor_copy(split[0:1, :, :], rows[:, 0:3, :]))
            step_done(ve.tensor_tensor(rest0, rows[:, 0:3, :], split[0:1, :, :], ALU.subtract))
            step_done(ve.tensor_copy(split[32:33, :, :], rest0))
            step_done(ve.tensor_copy(rest1[:, :, :], split[32:33, :, :]))
            step_done(ve.tensor_tensor(rest0, rest0, rest1[:, :, :], ALU.subtract))
            step_done(ve.tensor_copy(split[64:65, :, :], rest0), PREP_ALL)

            def edge(kind, turn):
                s = S[kind, turn]

                def scale_rows(done):
                    b, v = done.u % 2, done.u
                    dve.wait_ge(*s["rows"].at(done))
                    ve.reciprocal(inv_heads[b], row_banks[:, :, P + HEADS:P + 2 * HEADS]).then_inc(s["inv"].sem, 1)
                    dve.wait_ge(*s["inv"].at(done))
                    ve.tensor_tensor(head_dots[b], row_banks[:, :, P:P + HEADS], inv_heads[b], ALU.mult
                                     ).then_inc(s["dots"].sem, 1)
                    if done.back(4).exists(EG):
                        dve.wait_ge(*s["scattered"].at(done.back(4)))
                    ve.tensor_tensor(row_out[v][:, :, 0:H].rearrange("p t (h f) -> p t h f", h=HEADS),
                                     row_banks[:, :, 0:H].rearrange("p t (h f) -> p t h f", h=HEADS),
                                     inv_heads[b].unsqueeze(3).broadcast_to([P, ET, HEADS, HEAD]), ALU.mult)
                    dve.wait_ge(*s["dots"].at(done))
                    ve.tensor_reduce(row_out[v][:, :, H], head_dots[b], mybir.AxisListType.X, ALU.add
                                     ).then_inc(s["copied"].sem, 1)

                def body(step):
                    if not step.exists(EG):
                        if kind == "e0":
                            scale_rows(step.back(1))
                        return
                    u, d = step.u, step.u % 2
                    o = 1 - d
                    before = step.back(1)
                    first = not before.exists(EG)
                    dve.wait_ge(*s["table"].at(step))
                    ve.tensor_tensor(same[d][:, :], dstb[u][:, 1:], dstb[u][:, 0:EB], ALU.is_equal
                                     ).then_inc(s["same"].sem, 1)
                    dve.wait_ge(*s["same"].at(step))
                    if kind == "e1":
                        dve.wait_ge(*s["src"].at(step))
                        w = etab[u][:, 3 * ET:4 * ET].bitcast(F32)
                        for k in range(ET):
                            last = ve.tensor_scalar(x_src[u][:, k, :], x_src[u][:, k, :], w[:, k:k + 1], None, ALU.mult)
                        last.then_inc(s["weighted"].sem, 1)
                        dve.wait_ge(*s["act"].at(step))
                        if step.back(2).exists(EG):
                            dve.wait_ge(*s["rows"].at(step.back(2)))
                        if not first:
                            dve.wait_ge(*s["acc"].at(before))
                        ve.tensor_tensor_scan(acc[d][:, :], same[d][:, :], e1[d][:, :],
                                              0.0 if first else acc[o][:, EB - 1:EB], ALU.mult, ALU.max
                                              ).then_inc(s["acc"].sem, 1)
                        return
                    if kind == "e2":
                        ve.tensor_scalar(e2[d][0:TYPES, :], typeb[u][0:TYPES, :], float(TYPES - 1), 0.0,
                                         ALU.min, ALU.max).then_inc(s["clipped"].sem, 1)
                        dve.wait_ge(*s["clipped"].at(step))
                        if step.back(2).exists(EG):
                            dve.wait_ge(*s["projected"].at(step.back(2)))
                        ve.tensor_scalar(e1[d][0:TYPES, :], e2[d][0:TYPES, :], type_id[0:TYPES, :], None, ALU.is_equal
                                         ).then_inc(s["onehot"].sem, 1)
                        dve.wait_ge(*s["projected"].at(step))
                        if step.back(2).exists(EG):
                            dve.wait_ge(*s["rows"].at(step.back(2)))
                        if not first:
                            dve.wait_ge(*s["acc"].at(before))
                        ve.tensor_tensor_scan(acc[d][:, :], same[d][:, :], banks[2][:, :],
                                              0.0 if first else acc[o][:, EB - 1:EB], ALU.mult, ALU.add
                                              ).then_inc(s["acc"].sem, 1)
                        return
                    ve.tensor_scalar(fresh[d][:, :], same[d][:, :], -1.0, BIG, ALU.add, ALU.mult
                                     ).then_inc(s["fresh"].sem, 1)
                    if kind == "e0":
                        dve.wait_ge(*s["q"].at(step))
                        if step.back(2).exists(EG):
                            dve.wait_ge(*s["logits"].at(step.back(2)))
                        ve.scalar_tensor_tensor(e1[d][:, :], banks[3][:, :], cols[:, BK:BK + 1], e2[d][:, :],
                                                ALU.add, ALU.mult).then_inc(s["prod"].sem, 1)
                        if not first:
                            scale_rows(before)
                    else:
                        dve.wait_ge(*s["sloped"].at(step))
                        ve.tensor_tensor(e1[d][:, :], e1[d][:, :], banks[5][:, :], ALU.max
                                         ).then_inc(s["logits"].sem, 1)
                    dve.wait_ge(*s["fresh"].at(step))
                    dve.wait_ge(*s["logits"].at(step))
                    logit = banks[5][:, :] if kind == "e0" else e1[d][:, :]
                    if step.back(2).exists(EG):
                        dve.wait_ge(*s["rows"].at(step.back(2)))
                    if first:
                        ve.memset(top[d][:, 0:1], 0.0).then_inc(s["carried"].sem, 1)
                    else:
                        dve.wait_ge(*s["top"].at(before))
                        ve.tensor_copy(top[d][:, 0:1], top[o][:, EB:EB + 1]).then_inc(s["carried"].sem, 1)
                    dve.wait_ge(*s["carried"].at(step))
                    ve.tensor_tensor_scan(top[d][:, 1:], fresh[d][:, :], logit, top[d][:, 0:1], ALU.add, ALU.max
                                          ).then_inc(s["top"].sem, 1)
                    if step.back(2).exists(EG):
                        dve.wait_ge(*s["exp"].at(step.back(2)))
                    dve.wait_ge(*s["top"].at(step))
                    ve.tensor_tensor(pair[d][:, 0, :], top[d][:, 0:EB], fresh[d][:, :], ALU.add
                                     ).then_inc(s["t0"].sem, 1)
                    ve.tensor_tensor(pair[d][:, 1, :], logit, top[d][:, 1:], ALU.subtract).then_inc(s["d1"].sem, 1)
                    dve.wait_ge(*s["t0"].at(step))
                    ve.tensor_tensor(pair[d][:, 0, :], pair[d][:, 0, :], top[d][:, 1:], ALU.subtract
                                     ).then_inc(s["d0"].sem, 1)
                    dve.wait_ge(*s["exp"].at(step))
                    if not first:
                        dve.wait_ge(*s["total"].at(before))
                    ve.tensor_tensor_scan(total[d][:, :], expd[d][:, 0, :], expd[d][:, 1, :],
                                          0.0 if first else total[o][:, EB - 1:EB], ALU.mult, ALU.add
                                          ).then_inc(s["total"].sem, 1)
                    if kind == "e0":
                        ve.scalar_tensor_tensor(e1[d][:, :], banks[4][:, :], cols[:, BV:BV + 1], expd[d][:, 1, :],
                                                ALU.add, ALU.mult).then_inc(s["wv"].sem, 1)
                    else:
                        dve.wait_ge(*s["h_projected"].at(step))
                        ve.tensor_tensor(e2[d][:, :], banks[4][:, :], expd[d][:, 1, :], ALU.mult
                                         ).then_inc(s["wv"].sem, 1)
                    dve.wait_ge(*s["wv"].at(step))
                    if not first:
                        dve.wait_ge(*s["acc"].at(before))
                    ve.tensor_tensor_scan(acc[d][:, :], expd[d][:, 0, :], (e1 if kind == "e0" else e2)[d][:, :],
                                          0.0 if first else acc[o][:, EB - 1:EB], ALU.mult, ALU.add
                                          ).then_inc(s["acc"].sem, 1)
                run_steps(dve, EG, 1 if kind == "e0" else 0, body)

            def row_stats(block, v, stat, g, sig):
                for k in range(g):
                    last = ve.bn_stats(stats[block.u % 2][:, stat, k, :], v[:, k, :])
                last.then_inc(sig.sem, 1)

            def moments(s, block, step, stat, g, stats_sig, sig):
                dve.wait_ge(*stats_sig.at(block))
                if step.back(4).exists():
                    dve.wait_ge(*s["moments"].at(step.back(4)))
                settled(dve)
                for k in range(g):
                    last = ve.bn_aggr(mv[step.u][:, stat, k, :], stats[block.u % 2][:, stat, k, :])
                last.then_inc(sig.sem, 1)

            def along(i):
                return wide[:, i, :].unsqueeze(1).broadcast_to([P, G, P])

            def node_0(turn):
                s = S["n0", 0]

                def body(step):
                    two, four, five, six = (step.back(k) for k in (2, 4, 5, 6))
                    if two.exists(NB):
                        dve.wait_ge(*s["gated"].at(two))
                        ve.tensor_tensor(n1[two.u], n1[two.u], msg_in[two.u][:, :, 0:H], ALU.add
                                         ).then_inc(s["mix"].sem, 1)
                    if six.exists(NB):
                        dve.wait_ge(*s["sum"].at(six))
                        row_stats(six, n2[six.u], 1, G, s["stats2"])
                    if two.exists(NB):
                        dve.wait_ge(*s["mix"].at(two))
                        row_stats(two, n1[two.u], 0, G, s["stats"])
                    if six.exists(NB):
                        moments(s, six, step, 1, G, s["stats2"], s["mv2"])
                    if two.exists(NB):
                        moments(s, two, step, 0, G, s["stats"], s["mv"])
                    if four.exists(NB):
                        dve.wait_ge(*s["scaled"].at(four))
                        ve.tensor_tensor(n2[four.u], n2[four.u], along(BET0), ALU.add).then_inc(s["shifted"].sem, 1)
                    if five.exists(NB):
                        dve.wait_ge(*s["residual"].at(five))
                        ve.scalar_tensor_tensor(n2[five.u], n2[five.u], 0.0, n3[five.u % 2],
                                                ALU.max, ALU.add).then_inc(s["sum"].sem, 1)
                    if four.exists(NB):
                        dve.wait_ge(*s["shifted"].at(four))
                        if four.back(2).exists(NB):
                            dve.wait_ge(*s["sum"].at(four.back(2)))
                        ve.tensor_scalar(n3[four.u % 2], n2[four.u], 0.0, scal[:, 0:1], ALU.min, ALU.mult
                                         ).then_inc(s["act"].sem, 1)
                    if step.exists(NB):
                        dve.wait_ge(*s["loaded"].at(step))
                        dve.wait_ge(*s["product"].at(step))
                        ve.tensor_tensor(small[step.u][:, 0, :], banks[4 + step.u % 2][:, 0:G],
                                         msg_in[step.u][:, :, H], ALU.add).then_inc(s["z"].sem, 1)
                run_steps(dve, NB, 6, body)

            def node_1(turn):
                s = S["n1", 0]

                def body(step):
                    u, d = step.u, step.u % 2
                    dve.wait_ge(*s["product"].at(step))
                    if step.back(4).exists(NB):
                        dve.wait_ge(*s["out"].at(step.back(4)))
                    ve.scalar_tensor_tensor(n1[u].rearrange("p g f -> p (g f)"), banks[2 + d], 0.0,
                                            x_deep[u].rearrange("p g f -> p (g f)"), ALU.max, ALU.add
                                            ).then_inc(s["sum"].sem, 1)
                    dve.wait_ge(*s["sum"].at(step))
                    row_stats(step, n1[u], 0, G, s["stats"])
                    moments(s, step, step, 0, G, s["stats"], s["mv"])
                run_steps(dve, NB, 0, body)

            def node_2(turn):
                s = S["n2", 0]
                g = G2

                def body(step):
                    u, d = step.u, step.u % 2
                    if step.exists(NB2):
                        gate_banks = psum[:, 2 + 2 * d:4 + 2 * d, :]
                        dve.wait_ge(*s["gates"].at(step))
                        ve.tensor_tensor(n1[u][:, 0:g, :], gates[d][:, :, 0, :], gate_banks[:, :, 3 * H:4 * H], ALU.mult
                                         ).then_inc(s["rn"].sem, 1)
                        dve.wait_ge(*s["rn"].at(step))
                        ve.tensor_tensor(n1[u][:, 0:g, :], n1[u][:, 0:g, :], gate_banks[:, :, 0:H], ALU.add
                                         ).then_inc(s["npre"].sem, 1)
                    one = step.back(1)
                    if one.exists(NB2):
                        v, e = one.u, one.u % 2
                        dve.wait_ge(*s["n"].at(one))
                        ve.tensor_tensor(n3[e][:, 0:g, :], x_deep[v][:, 0:g, :], n2[v][:, 0:g, :], ALU.subtract
                                         ).then_inc(s["diff"].sem, 1)
                        dve.wait_ge(*s["diff"].at(one))
                        ve.tensor_tensor(n3[e][:, 0:g, :], n3[e][:, 0:g, :], gates[e][:, :, 1, :], ALU.mult
                                         ).then_inc(s["zd"].sem, 1)
                        dve.wait_ge(*s["zd"].at(one))
                        dve.wait_ge(*s["hn"].at(one))
                        ve.tensor_tensor(n2[v][:, 0:g, :], n2[v][:, 0:g, :], n3[e][:, 0:g, :], ALU.add
                                         ).then_inc(s["sum"].sem, 1)
                        dve.wait_ge(*s["sum"].at(one))
                        row_stats(one, n2[v], 0, g, s["stats"])
                        moments(s, one, step, 0, g, s["stats"], s["mv"])
                run_steps(dve, NB2, 1, body)

            def node_3(turn):
                s = S["n3", turn]
                final = turn == L3 - 1

                def body(step):
                    one, two, four, five = (step.back(k) for k in (1, 2, 4, 5))
                    sm1, sm, dots = small[one.u], small[step.u], banks[4 + step.u % 2][:, 0:G]
                    edge_top = msg_in[step.u][:, :, H + 1]
                    if two.exists(NB):
                        dve.wait_ge(*s["own"].at(two))
                        dve.wait_ge(*s["y1"].at(two))
                        ve.tensor_tensor(n1[two.u], n1[two.u], n3[two.u % 2], ALU.add).then_inc(s["y2"].sem, 1)
                    if one.exists(NB):
                        dve.wait_ge(*s["exp"].at(one))
                        ve.tensor_tensor(sm1[:, 6, :], sm1[:, 4, :], msg_in[one.u][:, :, H], ALU.mult
                                         ).then_inc(s["s0"].sem, 1)
                    if final and five.exists(NB):
                        dve.wait_ge(*s["sum"].at(five))
                        row_stats(five, n2[five.u], 1, G, s["stats2"])
                    if two.exists(NB):
                        dve.wait_ge(*s["y2"].at(two))
                        row_stats(two, n1[two.u], 0, G, s["stats"])
                    if one.exists(NB):
                        dve.wait_ge(*s["s0"].at(one))
                        ve.tensor_tensor(sm1[:, 7, :], sm1[:, 6, :], sm1[:, 5, :], ALU.add).then_inc(s["s1"].sem, 1)
                    if final and five.exists(NB):
                        moments(s, five, step, 1, G, s["stats2"], s["mv2"])
                    if two.exists(NB):
                        moments(s, two, step, 0, G, s["stats"], s["mv"])
                    if four.exists(NB):
                        dve.wait_ge(*s["scaled"].at(four))
                        if not final and four.back(4).exists(NB):
                            dve.wait_ge(*s["stored"].at(four.back(4)))
                        ve.tensor_tensor(n2[four.u] if final else y_out[four.u], n2[four.u], along(BET3 + turn),
                                         ALU.add).then_inc(s["out"].sem, 1)
                    if one.exists(NB):
                        dve.wait_ge(*s["s1"].at(one))
                        ve.reciprocal(sm1[:, 12, :], sm1[:, 7, :]).then_inc(s["inv"].sem, 1)
                    if one.exists(NB):
                        dve.wait_ge(*s["inv"].at(one))
                        ve.tensor_tensor(sm1[:, 13, :], sm1[:, 4, :], sm1[:, 12, :], ALU.mult)
                        ve.tensor_tensor(sm1[:, 14, :], sm1[:, 5, :], sm1[:, 12, :], ALU.mult
                                         ).then_inc(s["coef"].sem, 1)
                    if step.exists(NB):
                        dve.wait_ge(*s["loaded"].at(step))
                        dve.wait_ge(*s["product"].at(step))
                        ve.tensor_scalar(sm[:, 15, :], dots, SLOPE, None, ALU.mult).then_inc(s["sloped"].sem, 1)
                    if final and four.exists(NB):
                        dve.wait_ge(*s["res"].at(four))
                        dve.wait_ge(*s["out"].at(four))
                        ve.tensor_tensor(n2[four.u], n2[four.u], x_res[four.u], ALU.add).then_inc(s["sum"].sem, 1)
                    if step.exists(NB):
                        dve.wait_ge(*s["sloped"].at(step))
                        ve.tensor_tensor(sm[:, 0, :], sm[:, 15, :], dots, ALU.max).then_inc(s["z"].sem, 1)

                    def message(tiles):
                        for k in tiles:
                            last = ve.scalar_tensor_tensor(n1[one.u][:, k, :], msg_in[one.u][:, k, 0:H],
                                                           sm1[:, 13, k:k + 1], n1[one.u][:, k, :],
                                                           ALU.mult, ALU.add)
                        return last

                    if one.exists(NB):
                        dve.wait_ge(*s["coef"].at(one))
                        dve.wait_ge(*s["xb"].at(one))
                        message(range(0, G // 2))
                    if step.exists(NB):
                        dve.wait_ge(*s["z"].at(step))
                        ve.tensor_tensor(sm[:, 1, :], sm[:, 0, :], edge_top, ALU.max).then_inc(s["top"].sem, 1)
                    if one.exists(NB):
                        message(range(G // 2, G)).then_inc(s["y1"].sem, 1)
                    if step.exists(NB):
                        dve.wait_ge(*s["top"].at(step))
                        ve.tensor_tensor(sm[:, 2, :], edge_top, sm[:, 1, :], ALU.subtract)
                        ve.tensor_tensor(sm[:, 3, :], sm[:, 0, :], sm[:, 1, :], ALU.subtract
                                         ).then_inc(s["pair"].sem, 1)
                run_steps(dve, NB, 5 if final else 4, body)

            nodes = {"n0": node_0, "n1": node_1, "n2": node_2, "n3": node_3}
            for kind, turn in passes:
                if kind[0] == "e":
                    edge(kind, turn)
                else:
                    nodes[kind](turn)


_INS = ['x', 'src', 'dst', 'edge_type_9', 'edge_weight',
        'L0_gnn_Wq', 'L0_gnn_bq', 'L0_gnn_Wk', 'L0_gnn_bk', 'L0_gnn_Wv', 'L0_gnn_bv', 'L0_gnn_Ws', 'L0_gnn_bs',
        'L0_gnn_Wg', 'L0_gnn_bg', 'L0_gnn_gamma', 'L0_gnn_beta', 'L0_gnn_alpha',
        'L1_gnn_pool_w', 'L1_gnn_pool_b', 'L1_gnn_final_w', 'L1_gnn_final_b',
        'L2_gnn_W_msg', 'L2_gnn_b_msg', 'L2_gnn_edge_embed', 'L2_gnn_W_ih', 'L2_gnn_W_hh', 'L2_gnn_b_ih', 'L2_gnn_b_hh',
        'L3_gnn_W', 'L3_gnn_att_src', 'L3_gnn_att_dst', 'L3_gnn_bias', 'L3_gnn_gamma', 'L3_gnn_beta']


def kernel(**inputs):
    import numpy as np
    import concourse.bacc as bacc
    from concourse import mybir as _mybir
    from concourse.bass_utils import run_bass_kernel_spmd

    nc = bacc.Bacc("TRN2", target_bir_lowering=False, num_devices=1)
    arrays, args = {}, []
    for name in _INS:
        a = np.ascontiguousarray(inputs[name])
        arrays[f"in_{name}"] = a
        args.append(nc.dram_tensor(f"in_{name}", a.shape, _mybir.dt.from_np(a.dtype), kind="ExternalInput").ap())
    out = nc.dram_tensor("out_x", inputs["x"].shape, _mybir.dt.float32, kind="ExternalOutput").ap()
    gnn_kernel(nc, *args, out)
    result = run_bass_kernel_spmd(nc, [arrays], core_ids=[0])
    return result.results[0]["out_x"]
```

```python
from contextlib import ExitStack

import concourse.bass as bass
from concourse import mybir

F32 = mybir.dt.float32
BF16 = mybir.dt.bfloat16
I32 = mybir.dt.int32
ALU = mybir.AluOpType
ACT = mybir.ActivationFunctionType

P = 128
U = 8
BIG = 1e30
NO_ROW = 65536
PAD_DST = 60000
EPS = 1e-5
SLOPE = 0.2


class Step:

    def __init__(self, h, u):
        self.h, self.u = h, u

    def back(self, k):
        t = self.u - k
        return Step(self.h + t // U if t < 0 else self.h, t % U)

    @property
    def index(self):
        return self.h * U + self.u

    def exists(self, n=None):
        return not isinstance(self.h, int) or 0 <= self.index and (n is None or self.index < n)


class Signal:

    def __init__(self, sem, steps, before):
        self.sem, self.steps, self.before = sem, steps, before

    def at(self, step):
        return self.sem, step.h * U + (step.u + 1 + self.before)

    def end(self):
        return self.sem, self.before + self.steps


class DmaSignals:

    def __init__(self, sems, steps, dmas, before):
        self.sems, self.steps, self.unit, self.before = sems, steps, 16 * dmas, before

    def sem(self, step):
        return self.sems[step.u]

    def at(self, step):
        return self.sems[step.u], step.h * self.unit + (self.unit + self.before[step.u])

    def end(self):
        return [(s, self.before[u] + self.unit * ((self.steps - u + U - 1) // U)) for u, s in enumerate(self.sems)]


class Ring(list):

    def __getitem__(self, u):
        return list.__getitem__(self, u % len(self))


def run_steps(eng, n, lag, body, first=2):
    last = (n - 1) // U
    for j in range(first * U):
        body(Step(j // U, j % U))
    with eng.Fori(first, last) as h:
        for u in range(U):
            body(Step(h, u))
    for j in range(last * U, n + lag):
        body(Step(j // U, j % U))


def gnn_kernel(nc, x, src, dst, edge_type, edge_weight,
               Wq, bq, Wk, bk, Wv, bv, Ws, bs, Wg, bg, gamma0, beta0, alpha,
               pool_w, pool_b, final_w, final_b,
               W_msg, b_msg, edge_embed, W_ih, W_hh, b_ih, b_hh,
               W3, att_src, att_dst, bias3, gamma3, beta3, out):
    N, H = x.shape
    E = src.shape[0]
    HEADS = 4
    HEAD = H // HEADS
    TYPES = edge_embed.shape[0]
    L3 = W3.shape[0]
    EB = 512
    ET = EB // P
    EG = -(-E // EB)
    EPAD = EG * EB
    TILES = EPAD // P
    W0 = H + 2
    G = 4
    NB = -(-N // (G * P))
    G2 = 2
    NB2 = -(-N // (G2 * P))
    assert H == P and TYPES <= P and N < NO_ROW

    ctx = ExitStack()
    with ctx:
        def sb(name, shape, dt=F32):
            return ctx.enter_context(nc.sbuf_tensor(name, shape, dt))

        def ring(name, shape, depth, dt=F32):
            whole = sb(name, [shape[0], depth, *shape[1:]], dt)
            return Ring(whole[:, i] for i in range(depth))

        def sem(name):
            return ctx.enter_context(nc.semaphore(name))

        def dram(name, shape, dt=F32):
            return nc.dram_tensor(name, shape, dt, kind="Internal").ap()

        dst_pad = dram("dst_pad", [EPAD + 2], I32)
        src_pad = dram("src_pad", [EPAD], I32)
        type_pad = dram("type_pad", [EPAD], I32)
        weight_pad = dram("weight_pad", [EPAD])
        edge_table = dram("edge_table", [P, EG * 4 * ET], I32)
        xa = dram("xa", [N, H])
        xb = dram("xb", [N, H])
        att_rows = dram("att_rows", [N, W0])
        msg_rows = dram("msg_rows", [N, H])

        psum = ctx.enter_context(nc.psum_tensor("psum", [P, 8, 512], F32))
        banks = [psum[:, i, :] for i in range(8)]
        row_banks = psum[:, 6:8, :].rearrange("p b (t f) -> p (b t) f", t=2)

        ident = sb("ident", [P, P])
        neg_ident = sb("neg_ident", [P, P])
        gate_heads = sb("gate_heads", [P, HEADS])
        head_first = sb("head_first", [P, HEADS])
        head_ones = sb("head_ones", [P, P])
        one = sb("one", [P, P])
        ones_bf = sb("ones_bf", [P, P], BF16)
        neg_half = sb("neg_half", [P, 2, G])
        w_nat = sb("w_nat", [P, 13, P])
        wT = sb("wT", [P, 16, P])
        POOL, FIN_X, FIN_A, MSG, IH, WS_T, HH, W3_T = 0, 1, 2, 3, 4, 7, 8, 11
        wqkvs = sb("wqkvs", [P, 4, P])
        w3 = sb("w3", [P, L3, P])
        cols = sb("cols", [P, 16])
        BQ, BK, BV, BS, BPOOL, WG, ASRC, ADST = 0, 1, 2, 3, 4, 5, 8, 10
        gate_w = sb("gate_w", [P, 2])
        bs_wide = sb("bs_wide", [P, P])
        products = sb("products", [P, 8])
        self_col = sb("self_col", [P, L3])
        att_wide = sb("att_wide", [P, 2 * L3, P])
        scal = sb("scal", [P, 4])
        embed = sb("embed", [P, 2, P])
        embed_b = sb("embed_b", [P, P])
        type_id = sb("type_id", [P, 1])
        wide = sb("wide", [P, 2 + 2 * L3, P])
        GAM0, BET0, GAM3, BET3 = 0, 1, 2, 2 + L3
        ROW_BS, ROW_FINAL, ROW_GRU, ROW_BIAS3, ROW_HH = 0, 1, 2, 3, 3 + L3
        rows = sb("rows", [1, 4 + L3, 512])
        split = sb("split", [P, 3 + L3, 512], BF16)
        FILL_R = 25
        ATT_P, MSG_P = 80, 125
        ATT_FILLS, MSG_FILLS = N // (ATT_P * FILL_R), N // (MSG_P * FILL_R)
        assert ATT_FILLS * ATT_P * FILL_R == N and MSG_FILLS * MSG_P * FILL_R == N and MSG_FILLS == 16
        EARLY_FILLS = 8
        zeros = sb("zeros", [MSG_P, FILL_R * W0])
        pad_vals = sb("pad_vals", [P, 512], I32)
        type_i = sb("type_i", [P, 1], I32)
        lists = sb("lists", [P, 3, 2, P], I32)
        lists_w = sb("lists_w", [P, 2, P])
        lists_f = sb("lists_f", [P, 4, 2, P])
        table_sb = sb("table_sb", [P, EG * 4 * ET], I32)

        etab = ring("etab", [P, 4 * ET], U, I32)
        dstb = ring("dstb", [P, EB + 1], 4, I32)
        x_src = ring("x_src", [P, ET, P], 4)
        x_dst = ring("x_dst", [P, ET, P], 4)
        typeb = Ring(b.rearrange("p t f -> p (t f)").bitcast(I32) for b in x_dst)
        srcT = ring("srcT", [P, EB], 2)
        dstT = ring("dstT", [P, EB], 2)
        same = ring("same", [P, EB], 2)
        fresh = ring("fresh", [P, EB], 2)
        e1 = ring("e1", [P, EB], 2)
        e2 = ring("e2", [P, EB], 2)
        top = ring("top", [P, EB + 1], 2)
        pair = ring("pair", [P, 2, EB], 2)
        expd = ring("expd", [P, 2, EB], 2)
        total = ring("total", [P, EB], 2)
        acc = ring("acc", [P, EB], 2)
        row_out = ring("row_out", [P, ET, W0], 8)

        x_in, x_res, msg_in, xT = x_src, x_dst, row_out, srcT
        x_deep = Ring(list(x_src) + list(x_dst))

        def x_ring(kind, turn):
            return x_in if (kind, turn) == ("n3", L3 - 1) else x_deep

        n1 = ring("n1", [P, G, P], 4)
        n2 = ring("n2", [P, G, P], 4)
        n3 = ring("n3", [P, G, P], 2)
        gates = ring("gates", [P, G2, 2, P], 2)
        y_all = sb("y_out", [P, 4, G * P])
        y_out = Ring(y_all[:, i].rearrange("p (g f) -> p g f", g=G) for i in range(4))
        rest0, rest1 = y_all[0:1, 0:3, :], sb("rest1", [1, 3, 512])
        small = ring("small", [P, 16, G], 4)
        stats = ring("stats", [P, 2, G, 6], 2)
        mv = ring("mv", [P, 2, G, 2], 4)
        neg_mean = ring("neg_mean", [P, 2, G], 4)
        var_eps = ring("var_eps", [P, 2, G], 4)
        rstd = ring("rstd", [P, 2, G], 4)
        shift = ring("shift", [P, 2, G], 4)
        inv_heads = ring("inv_heads", [P, ET, HEADS], 2)
        head_dots = ring("head_dots", [P, ET, HEADS], 2)

        s_pads = sem("pads_set")
        s_lists = sem("edge_lists_in_dram")
        s_weights = sem("weights_loaded")
        s_rows_in = sem("edge_rows_loaded")
        s_ident = sem("identity_made")
        s_const = sem("constants_made")
        s_turned = sem("setup_pe_done")
        s_prep = sem("setup_dve_done")
        s_table = sem("edge_table_stored")
        s_settled = sem("settled")
        s_list_steps = sem("edge_list_steps")
        s_zero = sem("zeros_made")
        s_fill_att = sem("att_rows_filled")
        s_fill_msg = sem("msg_rows_filled")

        softmax_edges = ("turned_src turned_dst copied_src copied_dst projected logits same fresh top carried "
                         "t0 d0 d1 exp total wv acc rows copied ")
        NAMES = {
            "e0": softmax_edges + "v_projected q prod inv dots",
            "e1": "weighted turned_src copied_src projected act same acc rows copied",
            "e2": "turned_src copied_src clipped onehot projected same acc rows copied",
            "e3": softmax_edges + "sloped h_projected",
            "n0": "turned copied product z gate gated mix stats mv scaled shifted act residual sum stats2 mv2 "
                  "moments rstd shift norm out",
            "n1": "turned copied product sum stats mv moments rstd shift out",
            "n2": "turned copied product gates rn npre n diff zd hn sum stats mv moments rstd shift out",
            "n3": "turned copied product sloped z top pair exp s0 s1 inv coef own with_x with_own y1 stats mv moments rstd "
                  "shift norm scaled out",
        }
        DMAS = {
            "e0": {"table": 2, "src": ET, "dst": ET, "scattered": ET},
            "e1": {"table": 2, "src": ET, "scattered": ET},
            "e2": {"table": 3, "src": ET, "scattered": ET},
            "e3": {"table": 2, "src": ET, "dst": ET, "scattered": ET},
            "n0": {"loaded": 2, "stored": 1}, "n1": {"loaded": 2, "stored": 1}, "n2": {"loaded": 2, "stored": 1},
            "n3": {"loaded": 2, "stored": 1},
        }
        passes = [("e0", 0), ("n0", 0), ("e1", 0), ("n1", 0), ("e2", 0), ("n2", 0)]
        for l in range(L3):
            passes += [("e3", l), ("n3", l)]
        sems, value = {}, {}

        def pass_signals(kind, turn):
            steps = EG if kind[0] == "e" else NB2 if kind == "n2" else NB
            names, dmas = NAMES[kind], dict(DMAS[kind])
            if kind == "n3" and turn == L3 - 1:
                names += " sum stats2 mv2 out2"
                dmas["res"] = 1
            powers = steps + {"n0": 6, "n1": 0, "n2": 1, "n3": 5 if turn == L3 - 1 else 4}.get(kind, 0)
            found = {}
            for name in names.split():
                key = ("edge_" if kind[0] == "e" else "node_") + name
                if key not in sems:
                    sems[key], value[key] = sem(key), 0
                found[name] = Signal(sems[key], powers if name in ("moments", "rstd", "shift") else steps, value[key])
                value[key] += found[name].steps
            for name, n in dmas.items():
                key = ("edge_" if kind[0] == "e" else "node_") + name
                if key not in sems:
                    sems[key], value[key] = [sem(f"{key}{u}") for u in range(U)], [0] * U
                found[name] = DmaSignals(sems[key], steps, n, value[key])
                value[key] = [v for _, v in found[name].end()]
            return found

        LAG = {"n0": 7, "n1": 3, "n2": 4, "n3": 6}
        STORE = {("n0", 0): 9, ("n1", 0): 6, ("n2", 0): 7, ("n3", 0): 7, ("n3", 1): 9}
        S = {p: pass_signals(*p) for p in passes}
        PREP_LISTS, PREP_TABLE, PREP_TURNED, PREP_ALL = 1, 2, 3, 19
        N_WEIGHTS = 54
        x_of = {("e0", 0): x, ("n0", 0): (x, xa), ("e1", 0): xa, ("n1", 0): (xa, xb),
                ("e2", 0): xb, ("n2", 0): (xb, xa), ("e3", 0): xa, ("n3", 0): (xa, xb),
                ("e3", 1): xb, ("n3", 1): (xb, out)}

        def node_rows(a, step, g, width):
            if isinstance(step.h, int):
                base = min(step.index * g * P, N - g * P)
            else:
                base = step.index * (g * P)
            flat = a.rearrange("n f -> (n f)")
            return flat[bass.ds(base * width, g * P * width)].rearrange("(p k) -> p k", p=P)

        def settled(eng):
            eng.sem_inc(s_settled, 1)

        def fill_att_rows(eng, pieces):
            eng.wait_ge(s_zero, 2)
            v = att_rows.rearrange("(p q) w -> p (q w)", p=ATT_P)
            w = FILL_R * W0
            for j in pieces:
                eng.dma_start(v[:, j * w:(j + 1) * w], zeros[0:ATT_P, :]).then_inc(s_fill_att, 16)

        block = ctx.enter_context(nc.Block())

        @block.sync
        def _(sp):
            n_w = [0]

            def load(to, frm):
                sp.dma_start(to, frm).then_inc(s_weights, 16)
                n_w[0] += 1

            sp.dma_start(dst_pad[1:E + 1].rearrange("(a b) -> a b", a=8), dst.rearrange("(a b) -> a b", a=8)).then_inc(s_lists, 16)
            sp.dma_start(src_pad[0:E].rearrange("(a b) -> a b", a=8), src.rearrange("(a b) -> a b", a=8)).then_inc(s_lists, 16)
            sp.dma_start(type_pad[0:E].rearrange("(a b) -> a b", a=8), edge_type.rearrange("(a b) -> a b", a=8)).then_inc(s_lists, 16)
            sp.dma_start(weight_pad[0:E].rearrange("(a b) -> a b", a=8), edge_weight.rearrange("(a b) -> a b", a=8)).then_inc(s_lists, 16)
            sp.wait_ge(s_pads, 3)
            pad = EPAD - E
            sp.dma_start(dst_pad[0:1].unsqueeze(0), pad_vals[0:1, 0:1]).then_inc(s_lists, 16)
            sp.dma_start(dst_pad[E + 1:EPAD + 2].unsqueeze(0), pad_vals[0:1, 1:pad + 2]).then_inc(s_lists, 16)
            sp.dma_start(src_pad[E:EPAD].unsqueeze(0), pad_vals[0:1, 256:256 + pad]).then_inc(s_lists, 16)
            sp.dma_start(type_pad[E:EPAD].unsqueeze(0), pad_vals[0:1, 256:256 + pad]).then_inc(s_lists, 16)
            sp.dma_start(weight_pad[E:EPAD].unsqueeze(0), pad_vals[0:1, 256:256 + pad].bitcast(F32)).then_inc(s_lists, 16)
            sp.wait_ge(s_lists, 9 * 16)
            for k, (a, off) in enumerate([(src_pad, 0), (dst_pad, 1), (dst_pad, 2), (weight_pad, 0)]):
                lo = a[off:off + P * P].rearrange("(t p) -> t p", p=P)
                hi = a[off + P * P:off + EPAD].rearrange("(t p) -> t p", p=P)
                to = lists_w if k == 3 else lists[:, k]
                sp.dma_start(to[:, 0, :], lo).then_inc(s_rows_in, 16)
                sp.dma_start(to[0:TILES - P, 1, :], hi).then_inc(s_rows_in, 16)

            for i, w in enumerate((Wq, Wk, Wv, Ws)):
                load(wqkvs[:, i, :], w)
            load(w3[:, :, :], W3.rearrange("l i o -> i l o"))
            load(w_nat[:, POOL, :], pool_w)
            load(w_nat[:, FIN_X:FIN_A + 1, :], final_w.rearrange("o (c i) -> o c i", c=2))
            load(w_nat[:, MSG, :], W_msg)
            ih = W_ih.rearrange("(c o) i -> o c i", c=3)
            load(w_nat[:, IH, :], ih[:, 2, :])
            load(w_nat[:, IH + 1:IH + 3, :], ih[:, 0:2, :])
            load(w_nat[:, WS_T, :], Ws)
            load(w_nat[:, HH:HH + 3, :], W_hh.rearrange("(c o) i -> o c i", c=3))
            load(w_nat[:, W3_T:W3_T + L3, :], W3.rearrange("l i o -> i l o"))
            for c, v in ((BQ, bq), (BK, bk), (BV, bv), (BS, bs), (BPOOL, pool_b)):
                load(cols[:, c:c + 1], v.unsqueeze(1))
            for c in range(3):
                load(cols[:, WG + c:WG + c + 1], Wg[c * P:(c + 1) * P, :])
            for l in range(L3):
                load(cols[:, ASRC + l:ASRC + l + 1], att_src[l].unsqueeze(1))
                load(cols[:, ADST + l:ADST + l + 1], att_dst[l].unsqueeze(1))
            load(scal[:, 0:1], alpha.partition_broadcast(P))
            load(scal[:, 1:2], bg.partition_broadcast(P))
            load(embed[0:TYPES, 0, :], edge_embed)
            load(embed[0:TYPES, 1, :], b_msg.partition_broadcast(TYPES))
            load(wide[:, GAM0, :], gamma0.partition_broadcast(P))
            load(wide[:, BET0, :], beta0.partition_broadcast(P))
            for l in range(L3):
                load(wide[:, GAM3 + l, :], gamma3[l].partition_broadcast(P))
                load(wide[:, BET3 + l, :], beta3[l].partition_broadcast(P))
            for g in range(G):
                load(rows[:, ROW_BS, g * H:(g + 1) * H], bs.unsqueeze(0))
                load(rows[:, ROW_FINAL, g * H:(g + 1) * H], final_b.unsqueeze(0))
                for l in range(L3):
                    load(rows[:, ROW_BIAS3 + l, g * H:(g + 1) * H], bias3[l].unsqueeze(0))
            sp.wait_ge(s_const, 1)
            load(rows[:, ROW_GRU, 0:H], b_ih[2 * H:3 * H].unsqueeze(0))
            load(rows[:, ROW_GRU, H:3 * H], b_ih[0:2 * H].unsqueeze(0))
            load(rows[:, ROW_HH, H:4 * H], b_hh.unsqueeze(0))
            assert n_w[0] == N_WEIGHTS, n_w

            sp.wait_ge(s_prep, PREP_TABLE)
            sp.dma_start(edge_table, table_sb[:, :]).then_inc(s_table, 16)
            sp.wait_ge(s_table, 16)

            def edge_loads(kind, turn):
                s = S[kind, turn]
                if kind == "e2":
                    sp.wait_ge(*S["n1", 0]["sum"].end())

                def body(step):
                    u = step.u
                    if kind == "e0" and isinstance(step.h, int) and step.index == 4:
                        fill_att_rows(sp, range(EARLY_FILLS, ATT_FILLS))
                    if step.back(U).exists(EG):
                        sp.wait_ge(*s["scattered"].at(step.back(U)))
                        settled(sp)
                    if step.back(4).exists(EG):
                        sp.wait_ge(*s["same"].at(step.back(4)))
                        settled(sp)
                        if kind == "e2":
                            sp.wait_ge(*s["clipped"].at(step.back(4)))
                            settled(sp)
                    sp.dma_start(etab[u][:, :], edge_table[:, bass.ds(step.index * (4 * ET), 4 * ET)]
                                 ).then_inc(s["table"].sem(step), 16)
                    sp.dma_start(dstb[u][:, :], dst_pad[bass.ds(step.index * EB, EB + 1)].partition_broadcast(P)
                                 ).then_inc(s["table"].sem(step), 16)
                    if kind == "e2":
                        sp.dma_start(typeb[u][0:TYPES, :],
                                     type_pad[bass.ds(step.index * EB, EB)].partition_broadcast(TYPES)
                                     ).then_inc(s["table"].sem(step), 16)
                run_steps(sp, EG, 0, body)

            def node_moves(kind, turn):
                s = S[kind, turn]
                g, nb = (G2, NB2) if kind == "n2" else (G, NB)
                x_now, x_new = x_of[kind, turn]
                msgs, w = (att_rows, W0) if kind in ("n0", "n3") else (msg_rows, H)
                x_last, x_depth = {"n0": ("residual", 8), "n1": ("sum", 8), "n2": ("sum", 8), "n3": ("with_x", len(x_ring(kind, turn)))}[kind]
                msg_last = {"n0": "mix", "n1": "sum", "n2": "turned", "n3": "y1"}[kind]
                out_sig = "out2" if (kind, turn) == ("n3", L3 - 1) else "out"
                for s_, v_ in S["e" + kind[1], turn]["scattered"].end():
                    sp.wait_ge(s_, v_)

                def body(step):
                    if step.exists(nb):
                        u = step.u
                        if step.back(x_depth).exists(nb):
                            sp.wait_ge(*s[x_last].at(step.back(x_depth)))
                            settled(sp)
                        sp.dma_start(x_ring(kind, turn)[u][:, 0:g, :].rearrange("p g f -> p (g f)"), node_rows(x_now, step, g, H)
                                     ).then_inc(s["loaded"].sem(step), 16)
                        if step.back(8).exists(nb):
                            sp.wait_ge(*s[msg_last].at(step.back(8)))
                            settled(sp)
                        to = msg_in[u][:, 0:g, :] if w == W0 else msg_in[u][:, :, :].rearrange(
                            "p g f -> p (g f)")[:, 0:g * H]
                        if w == W0:
                            to = to.rearrange("p g f -> p (g f)")
                        sp.dma_start(to, node_rows(msgs, step, g, w)).then_inc(s["loaded"].sem(step), 16)
                    late = step.back(3)
                    if out_sig == "out2" and late.exists(nb):
                        if late.back(4).exists(nb):
                            sp.wait_ge(*s["sum"].at(late.back(4)))
                            settled(sp)
                        sp.dma_start(x_res[late.u][:, :, :].rearrange("p g f -> p (g f)"),
                                     node_rows(xa, late, g, H)).then_inc(s["res"].sem(late), 16)
                    done = step.back(STORE[kind, turn])
                    if done.exists(nb):
                        sp.wait_ge(*s[out_sig].at(done))
                        if isinstance(done.h, int) and done.index == nb - 1:
                            sp.wait_ge(*s["stored"].at(done.back(1)))
                        settled(sp)
                        sp.dma_start(node_rows(x_new, done, g, H),
                                     y_out[done.u][:, 0:g, :].rearrange("p g f -> p (g f)")
                                     ).then_inc(s["stored"].sem(done), 16)
                run_steps(sp, nb, STORE[kind, turn], body)

            for kind, turn in passes:
                (edge_loads if kind[0] == "e" else node_moves)(kind, turn)
            for s_, v_ in S[passes[-1]]["stored"].end():
                sp.wait_ge(s_, v_)

        @block.gpsimd
        def _(pool):
            gp = nc.gpsimd
            gp.memset(pad_vals[:, 0:1], -1).then_inc(s_pads, 1)
            gp.memset(pad_vals[:, 1:256], PAD_DST).then_inc(s_pads, 1)
            gp.memset(pad_vals[:, 256:512], 0).then_inc(s_pads, 1)
            gp.memset(zeros[:, :], 0.0).then_inc(s_zero, 1)
            pool.wait_ge(s_zero, 1)
            gp.memset(zeros[:, :].rearrange("p (r w) -> p r w", w=W0)[:, :, W0 - 1:W0], -BIG
                      ).then_inc(s_zero, 1)
            gp.memset(ident[:, :], 0.0).then_inc(s_ident, 1)
            pool.wait_ge(s_ident, 1)
            gp.affine_select(out=ident[:, :], in_=ident[:, :], compare_op=ALU.not_equal, fill=1.0, base=0,
                             pattern=[[-1, P]], channel_multiplier=1).then_inc(s_ident, 1)
            gp.iota(type_i[:, :], pattern=[[0, 1]], base=0, channel_multiplier=1).then_inc(s_ident, 1)
            gp.memset(neg_half[:, :, :], -0.5).then_inc(s_ident, 1)
            pool.wait_ge(s_ident, 4)

            def edge_moves(kind, turn):
                s = S[kind, turn]
                x_now = x_of[kind, turn]
                target = att_rows if kind in ("e0", "e3") else msg_rows
                w = W0 if kind in ("e0", "e3") else H
                if kind == "e1":
                    pool.wait_ge(s_fill_msg, 16 * MSG_FILLS)
                if kind != "e0":
                    before = passes[passes.index((kind, turn)) - 1]
                    for s_, v_ in S[before]["stored"].end():
                        pool.wait_ge(s_, v_)

                def body(step):
                    u = step.u
                    if step.exists(EG):
                        pool.wait_ge(*s["table"].at(step))
                        if step.back(4).exists(EG):
                            pool.wait_ge(*s["turned_src"].at(step.back(4)))
                        settled(pool)
                        for k in range(ET):
                            gp.indirect_dma_start(
                                out=x_src[u][:, k, :], out_offset=None, in_=x_now,
                                in_offset=bass.IndirectOffsetOnAxis(ap=etab[u][:, k:k + 1], axis=0),
                            ).then_inc(s["src"].sem(step), 16)
                        if kind in ("e0", "e3"):
                            if step.back(4).exists(EG):
                                pool.wait_ge(*s["turned_dst"].at(step.back(4)))
                            settled(pool)
                            for k in range(ET):
                                gp.indirect_dma_start(
                                    out=x_dst[u][:, k, :], out_offset=None, in_=x_now,
                                    in_offset=bass.IndirectOffsetOnAxis(ap=etab[u][:, ET + k:ET + k + 1], axis=0),
                                ).then_inc(s["dst"].sem(step), 16)
                    done = step.back(3)
                    if done.exists(EG):
                        pool.wait_ge(*s["copied"].at(done))
                        if kind == "e0" and isinstance(done.h, int) and done.index == 0:
                            pool.wait_ge(s_fill_att, 16 * ATT_FILLS)
                            gp.memset(zeros[:, :].rearrange("p (r w) -> p r w", w=W0)[:, :, W0 - 1:W0], 0.0
                                      ).then_inc(s_zero, 1)
                        settled(pool)
                        for k in range(ET):
                            rows_k = (row_out[done.u][:, k, :] if w == W0 else
                                      row_out[done.u][:, :, :].rearrange("p t f -> p (t f)")[:, k * H:(k + 1) * H])
                            gp.indirect_dma_start(
                                out=target,
                                out_offset=bass.IndirectOffsetOnAxis(ap=etab[done.u][:, 2 * ET + k:2 * ET + k + 1], axis=0),
                                in_=rows_k, in_offset=None, bounds_check=N - 1, oob_is_err=False,
                            ).then_inc(s["scattered"].sem(done), 16)
                run_steps(pool, EG, 3, body)

            def powers(s, step, first, second, nb, g):
                u = step.u
                one = step.back(first).exists(nb)
                two = second is not None and step.back(second).exists(nb)
                k = 1 if second is None else 2
                if one:
                    pool.wait_ge(*s["mv"].at(step.back(first)))
                if two:
                    pool.wait_ge(*s["mv2"].at(step.back(second)))
                settled(pool)
                gp.tensor_scalar(neg_mean[u][:, 0:k, 0:g], mv[u][:, 0:k, 0:g, 0], -1.0, None, ALU.mult)
                gp.tensor_scalar(var_eps[u][:, 0:k, 0:g], mv[u][:, 0:k, 0:g, 1], EPS, None, ALU.add
                                 ).then_inc(s["moments"].sem, 1)
                pool.wait_ge(*s["moments"].at(step))
                gp.tensor_tensor(rstd[u][:, 0:k, 0:g], var_eps[u][:, 0:k, 0:g], neg_half[:, 0:k, 0:g], ALU.pow
                                 ).then_inc(s["rstd"].sem, 1)
                pool.wait_ge(*s["rstd"].at(step))
                gp.tensor_tensor(shift[u][:, 0:k, 0:g], neg_mean[u][:, 0:k, 0:g], rstd[u][:, 0:k, 0:g], ALU.mult
                                 ).then_inc(s["shift"].sem, 1)

            def along(i):
                return wide[:, i, :].unsqueeze(1).broadcast_to([P, G, P])

            def node_0(turn):
                s = S["n0", 0]

                def body(step):
                    four, five = step.back(4), step.back(5)
                    if four.exists(NB):
                        pool.wait_ge(*s["norm"].at(four))
                        gp.tensor_tensor(n2[four.u], n2[four.u], along(GAM0), ALU.mult).then_inc(s["scaled"].sem, 1)
                    if five.exists(NB):
                        pool.wait_ge(*s["act"].at(five))
                        gp.tensor_tensor(n3[five.u % 2], n3[five.u % 2], x_deep[five.u], ALU.add
                                         ).then_inc(s["residual"].sem, 1)
                    powers(s, step, 2, 6, NB, G)
                pool.wait_ge(s_prep, PREP_ALL)
                run_steps(pool, NB, 6, body)

            def node_1(turn):
                s = S["n1", 0]
                run_steps(pool, NB, 0, lambda step: powers(s, step, 0, None, NB, G))

            def node_2(turn):
                s = S["n2", 0]

                run_steps(pool, NB2, 1, lambda step: powers(s, step, 1, None, NB2, G2))

            def node_3(turn):
                s = S["n3", turn]
                final = turn == L3 - 1

                def body(step):
                    four = step.back(4)
                    if four.exists(NB):
                        pool.wait_ge(*s["norm"].at(four))
                        gp.tensor_tensor(n2[four.u], n2[four.u], along(GAM3 + turn), ALU.mult
                                         ).then_inc(s["scaled"].sem, 1)
                        pool.wait_ge(*s["scaled"].at(four))
                        if final:
                            pool.wait_ge(*s["res"].at(four))
                            gp.tensor_tensor(n2[four.u], n2[four.u], x_res[four.u], ALU.add).then_inc(s["sum"].sem, 1)
                        else:
                            if four.back(4).exists(NB):
                                pool.wait_ge(*s["stored"].at(four.back(4)))
                            gp.tensor_tensor(y_out[four.u], n2[four.u], along(BET3 + turn), ALU.add
                                             ).then_inc(s["out"].sem, 1)
                    powers(s, step, 2, 5 if final else None, NB, G)
                run_steps(pool, NB, 5 if final else 4, body)

            nodes = {"n0": node_0, "n1": node_1, "n2": node_2, "n3": node_3}
            for kind, turn in passes:
                if kind[0] == "e":
                    edge_moves(kind, turn)
                else:
                    nodes[kind](turn)

        @block.tensor
        def _(pe):
            te = nc.tensor
            pe.wait_ge(s_ident, 2)
            pe.wait_ge(s_prep, 1)
            for k in range(4):
                te.transpose(banks[k][:, 0:P], lists_f[:, k, 0, :], ident[:, :])
                last = te.transpose(banks[k][:, P:TILES], lists_f[0:TILES - P, k, 1, :],
                                    ident[0:TILES - P, 0:TILES - P])
            last.then_inc(s_turned, 1)
            pe.wait_ge(s_weights, 16 * N_WEIGHTS)
            for i in range(13):
                last = te.transpose(banks[4 + i // 4][:, (i % 4) * P:(i % 4 + 1) * P], w_nat[:, i, :], ident[:, :])
            last.then_inc(s_turned, 1)
            pe.wait_ge(s_prep, PREP_TURNED)
            te.matmul(banks[0][:, 0:1], wT[:, WS_T, :], gate_w[:, 0:1], start=True, stop=True)
            for l in range(L3):
                te.matmul(banks[0][:, 1 + l:2 + l], wT[:, W3_T + l, :], cols[:, ASRC + l:ASRC + l + 1],
                          start=True, stop=True)
                te.matmul(banks[0][:, 1 + L3 + l:2 + L3 + l], wT[:, W3_T + l, :], cols[:, ADST + l:ADST + l + 1],
                          start=True, stop=True)
            te.matmul(banks[0][:, 5:6], bs_wide[:, :], gate_w[:, 0:1], start=True, stop=True).then_inc(s_turned, 1)
            pe.wait_ge(s_prep, PREP_ALL)

            def turn_edges(s, step, which, bank, rows_in, ready, s_ready):
                pe.wait_ge(*ready)
                if step.back(1).exists(EG):
                    pe.wait_ge(*s["copied_" + which].at(step.back(1)))
                for k in range(ET):
                    last = te.transpose(banks[bank][:, k * P:(k + 1) * P], rows_in[:, k, :], ident[:, :])
                last.then_inc(s_ready.sem, 1)

            def edge(kind, turn):
                s = S[kind, turn]

                def body(step):
                    u, d = step.u, step.u % 2
                    before = step.back(1)
                    if step.exists(EG):
                        if kind == "e1":
                            turn_edges(s, step, "src", 0, x_src[u], s["weighted"].at(step), s["turned_src"])
                        else:
                            turn_edges(s, step, "src", 0, x_src[u], s["src"].at(step), s["turned_src"])
                        if kind in ("e0", "e3"):
                            turn_edges(s, step, "dst", 1, x_dst[u], s["dst"].at(step), s["turned_dst"])
                        pe.wait_ge(*s["copied_src"].at(step))
                        if kind == "e0":
                            if before.exists(EG):
                                pe.wait_ge(*s["prod"].at(before))
                            te.matmul(banks[2][:, :], wqkvs[:, 0, :], srcT[d][:, :], start=True, stop=True)
                            pe.wait_ge(*s["copied_dst"].at(step))
                            te.matmul(banks[3][:, :], wqkvs[:, 1, :], dstT[d][:, :], start=True, stop=True
                                      ).then_inc(s["projected"].sem, 1)
                            if before.exists(EG):
                                pe.wait_ge(*s["wv"].at(before))
                            te.matmul(banks[4][:, :], wqkvs[:, 2, :], srcT[d][:, :], start=True, stop=True
                                      ).then_inc(s["v_projected"].sem, 1)
                        elif kind == "e1":
                            if before.exists(EG):
                                pe.wait_ge(*s["act"].at(before))
                            te.matmul(banks[2][:, :], wT[:, POOL, :], srcT[d][:, :], start=True, stop=True
                                      ).then_inc(s["projected"].sem, 1)
                        elif kind == "e2":
                            if before.exists(EG):
                                pe.wait_ge(*s["acc"].at(before))
                            te.matmul(banks[2][:, :], wT[:, MSG, :], srcT[d][:, :], start=True, stop=False)
                            pe.wait_ge(*s["onehot"].at(step))
                            te.matmul(banks[2][:, :], embed_b[0:TYPES, :], e1[d][0:TYPES, :], start=False, stop=True
                                      ).then_inc(s["projected"].sem, 1)
                        else:
                            if before.exists(EG):
                                pe.wait_ge(*s["logits"].at(before))
                            te.matmul(banks[5][:, :], att_wide[:, turn, :], srcT[d][:, :], start=True, stop=False)
                            pe.wait_ge(*s["copied_dst"].at(step))
                            te.matmul(banks[5][:, :], att_wide[:, L3 + turn, :], dstT[d][:, :], start=False, stop=True
                                      ).then_inc(s["projected"].sem, 1)
                            if before.exists(EG):
                                pe.wait_ge(*s["wv"].at(before))
                            te.matmul(banks[4][:, :], w3[:, turn, :], srcT[d][:, :], start=True, stop=True
                                      ).then_inc(s["h_projected"].sem, 1)
                    if before.exists(EG):
                        b = before.u % 2
                        if before.back(1).exists(EG):
                            pe.wait_ge(*s["copied"].at(before.back(1)))
                        if kind == "e0":
                            pe.wait_ge(*s["acc"].at(before))
                            for k in range(ET):
                                cs = slice(k * P, (k + 1) * P)
                                te.transpose(row_banks[:, k, 0:P], acc[b][:, cs], ident[:, :])
                                te.matmul(row_banks[:, k, P:P + HEADS], acc[b][:, cs], gate_heads[:, :],
                                          start=True, stop=True)
                                last = te.matmul(row_banks[:, k, P + HEADS:P + 2 * HEADS], total[b][:, cs],
                                                 head_first[:, :], start=True, stop=True)
                        elif kind == "e3":
                            pe.wait_ge(*s["acc"].at(before))
                            for k in range(ET):
                                o = (k % 2) * 256
                                cs = slice(k * P, (k + 1) * P)
                                te.transpose(banks[6 + k // 2][:, o:o + P], acc[b][:, cs], ident[:, :])
                                te.matmul(banks[6 + k // 2][:, o + P:o + P + 1], total[b][0:1, cs], one[0:1, 0:1],
                                          start=True, stop=True)
                                last = te.matmul(banks[6 + k // 2][:, o + P + 1:o + P + 2],
                                                 top[b][0:1, k * P + 1:(k + 1) * P + 1], one[0:1, 0:1],
                                                 start=True, stop=True)
                        else:
                            pe.wait_ge(*s["acc"].at(before))
                            for k in range(ET):
                                cs = slice(k * P, (k + 1) * P)
                                if kind == "e1":
                                    last = te.matmul(banks[6][:, cs], acc[b][:, cs], wT[:, FIN_A, :],
                                                     start=True, stop=True)
                                else:
                                    last = te.transpose(banks[6][:, cs], acc[b][:, cs], ident[:, :])
                        last.then_inc(s["rows"].sem, 1)
                    if step.exists(EG) and kind == "e0":
                        pe.wait_ge(*s["prod"].at(step))
                        if before.exists(EG):
                            pe.wait_ge(*s["d1"].at(before))
                        te.matmul(banks[5][:, :], head_ones[:, :], e1[d][:, :], start=True, stop=True
                                  ).then_inc(s["logits"].sem, 1)
                run_steps(pe, EG, 1, body)

            def node(kind, turn):
                s = S[kind, turn]
                g, nb = (G2, NB2) if kind == "n2" else (G, NB)
                e = S["e" + kind[1], turn]
                pe.wait_ge(*e["copied"].end())

                def turn_rows(step):
                    u, d = step.u, step.u % 2
                    two = step.back(2)
                    if step.exists(nb):
                        pe.wait_ge(*s["loaded"].at(step))
                        if two.exists(nb):
                            pe.wait_ge(*s["copied"].at(two))
                        for k in range(g):
                            last = te.transpose(banks[d][:, k * P:(k + 1) * P], x_ring(kind, turn)[u][:, k, :], ident[:, :])
                        if kind == "n2":
                            msgs = msg_in[u][:, :, :].rearrange("p g f -> p (g f)")
                            for k in range(g):
                                last = te.transpose(banks[d][:, (g + k) * P:(g + k + 1) * P],
                                                    msgs[:, k * P:(k + 1) * P], ident[:, :])
                        last.then_inc(s["turned"].sem, 1)

                def products_of(now):
                    u, d = now.u, now.u % 2
                    two = now.back(2)
                    pe.wait_ge(*s["copied"].at(now))
                    if two.exists(nb):
                        pe.wait_ge(*s[{"n0": "gated", "n1": "sum", "n2": "npre", "n3": "own"}[kind]].at(two))
                    if kind == "n0":
                        te.matmul(banks[2 + d][:, :], ones_bf[:, :], split[:, 0, :], start=True, stop=True)
                        te.matmul(banks[2 + d][:, :].rearrange("p (g f) -> p g f", g=g), neg_ident[:, :],
                                  msg_in[u][:, :, 0:H], start=False, stop=True, skip_group_check=True)
                        for k in range(g):
                            te.matmul(banks[2 + d][:, k * P:(k + 1) * P], xT[d][:, k * P:(k + 1) * P], wqkvs[:, 3, :],
                                      start=False, stop=True, skip_group_check=True)
                            last = te.matmul(banks[4 + d][:, k:k + 1], xT[d][:, k * P:(k + 1) * P], products[:, 0:1],
                                             start=True, stop=True)
                    elif kind == "n1":
                        te.matmul(banks[2 + d][:, :], ones_bf[:, :], split[:, 1, :], start=True, stop=True)
                        te.matmul(banks[2 + d][:, :], ident[:, :],
                                  msg_in[u][:, :, :].rearrange("p g f -> p (g f)")[:, 0:g * P], start=False, stop=True,
                                  skip_group_check=True)
                        for k in range(g):
                            last = te.matmul(banks[2 + d][:, k * P:(k + 1) * P], xT[d][:, k * P:(k + 1) * P],
                                             wT[:, FIN_X, :], start=False, stop=True, skip_group_check=True)
                    elif kind == "n2":
                        for k in range(g):
                            bank = banks[2 + 2 * d + k]
                            te.matmul(bank[:, :], ones_bf[:, :], split[:, 2, :], start=True, stop=True)
                            te.matmul(bank[:, H:4 * H], xT[d][:, k * P:(k + 1) * P],
                                      wT[:, HH:HH + 3, :].rearrange("p c o -> p (c o)"),
                                      start=False, stop=True, skip_group_check=True)
                            last = te.matmul(bank[:, 0:3 * H], xT[d][:, (g + k) * P:(g + k + 1) * P],
                                             wT[:, IH:IH + 3, :].rearrange("p c o -> p (c o)"),
                                             start=False, stop=True, skip_group_check=True)
                    else:
                        for k in range(g):
                            xk = xT[d][:, k * P:(k + 1) * P]
                            te.matmul(banks[4 + d][:, k:k + 1], xk, self_col[:, turn:turn + 1], start=True, stop=True)
                            last = te.matmul(banks[2 + d][:, k * P:(k + 1) * P], xk, w3[:, turn, :],
                                             start=True, stop=True)
                    last.then_inc(s["product"].sem, 1)

                def sum_with_x(now):
                    d, two = now.u % 2, now.back(2)
                    if two.exists(nb):
                        pe.wait_ge(*s["y1"].at(two))
                    te.matmul(banks[6 + d][:, :], ones_bf[:, :], split[:, ROW_BIAS3 + turn, :], start=True, stop=True)
                    te.matmul(banks[6 + d][:, :].rearrange("p (g f) -> p g f", g=g), ident[:, :], x_ring(kind, turn)[now.u],
                              start=False, stop=True, skip_group_check=True).then_inc(s["with_x"].sem, 1)

                def sum_with_own(now):
                    d = now.u % 2
                    pe.wait_ge(*s["own"].at(now))
                    te.matmul(banks[6 + d][:, :].rearrange("p (g f) -> p g f", g=g), ident[:, :], n3[d],
                              start=False, stop=True, skip_group_check=True).then_inc(s["with_own"].sem, 1)

                def body(step):
                    if kind == "n3" and step.back(3).exists(nb):
                        sum_with_own(step.back(3))
                    turn_rows(step)
                    if step.back(1).exists(nb):
                        products_of(step.back(1))
                    if kind == "n3" and step.back(2).exists(nb):
                        sum_with_x(step.back(2))

                run_steps(pe, nb, 3 if kind == "n3" else 1, body)

            for kind, turn in passes:
                (edge if kind[0] == "e" else node)(kind, turn)

        @block.scalar
        def _(act):
            sc = nc.scalar
            act.wait_ge(s_rows_in, 8 * 16)
            fill_att_rows(act, range(EARLY_FILLS))

            def fill_msg_rows(j):
                v = msg_rows.rearrange("(p q) w -> p (q w)", p=MSG_P)
                w = FILL_R * H
                act.dma_start(v[:, bass.ds(j * w, w)], zeros[:, 0:w]).then_inc(s_fill_msg, 16)

            act.wait_ge(s_prep, PREP_ALL)

            def edge(kind, turn):
                s = S[kind, turn]

                def exponentials(step):
                    d = step.u % 2
                    act.wait_ge(*s["d1"].at(step))
                    act.wait_ge(*s["d0"].at(step))
                    if step.back(2).exists(EG):
                        act.wait_ge(*s["acc"].at(step.back(2)))
                    sc.activation(expd[d][:, :, :], pair[d][:, :, :], ACT.Exp).then_inc(s["exp"].sem, 1)

                def body(step):
                    d = step.u % 2
                    two, before = step.back(2), step.back(1)
                    if kind == "e0" and not isinstance(step.h, int) and step.u % 2 == 1:
                        act.wait_ge(s_zero, 3)
                        fill_msg_rows((step.h - 2) * (U // 2) + step.u // 2)
                    if step.exists(EG):
                        act.wait_ge(*s["turned_src"].at(step))
                        if two.exists(EG):
                            act.wait_ge(*s[{"e0": "v_projected", "e3": "h_projected"}.get(kind, "projected")].at(two))
                        sc.copy(srcT[d][:, :], banks[0][:, :]).then_inc(s["copied_src"].sem, 1)
                        if kind in ("e0", "e3"):
                            act.wait_ge(*s["turned_dst"].at(step))
                            sc.copy(dstT[d][:, :], banks[1][:, :]).then_inc(s["copied_dst"].sem, 1)
                        if kind == "e0" and before.exists(EG):
                            exponentials(before)
                        act.wait_ge(*s["projected"].at(step))
                        if kind == "e0":
                            if two.exists(EG):
                                act.wait_ge(*s["prod"].at(two))
                            sc.activation(e2[d][:, :], banks[2][:, :], ACT.Identity, bias=cols[:, BQ:BQ + 1]
                                          ).then_inc(s["q"].sem, 1)
                        elif kind == "e1":
                            if two.exists(EG):
                                act.wait_ge(*s["acc"].at(two))
                            sc.activation(e1[d][:, :], banks[2][:, :], ACT.Relu, bias=cols[:, BPOOL:BPOOL + 1]
                                          ).then_inc(s["act"].sem, 1)
                        elif kind == "e3":
                            if two.exists(EG):
                                act.wait_ge(*s["d1"].at(two))
                            sc.mul(e1[d][:, :], banks[5][:, :], SLOPE).then_inc(s["sloped"].sem, 1)
                    if before.exists(EG) and kind != "e0":
                        v = before.u
                        act.wait_ge(*s["rows"].at(before))
                        if before.back(U).exists(EG):
                            act.wait_ge(*s["scattered"].at(before.back(U)))
                        if kind == "e3":
                            last = sc.copy(row_out[v], row_banks[:, :, 0:W0])
                        else:
                            last = sc.copy(row_out[v][:, :, :].rearrange("p t f -> p (t f)")[:, 0:EB], banks[6][:, :])
                        last.then_inc(s["copied"].sem, 1)
                    if kind == "e3" and step.exists(EG):
                        exponentials(step)
                    if kind == "e0" and not step.exists(EG):
                        exponentials(before)
                run_steps(act, EG, 1, body)

            def node(kind, turn):
                s = S[kind, turn]
                g, nb = (G2, NB2) if kind == "n2" else (G, NB)
                final = turn == L3 - 1

                def normalise(computed, v, to, stat, sig):
                    act.wait_ge(*s["shift"].at(computed))
                    c = computed.u
                    for k in range(g):
                        last = sc.activation(to[:, k, :], v[:, k, :], ACT.Identity,
                                             scale=rstd[c][:, stat, k:k + 1], bias=shift[c][:, stat, k:k + 1])
                    last.then_inc(s[sig].sem, 1)

                def turned_x(step):
                    act.wait_ge(*s["turned"].at(step))
                    if step.back(2).exists(nb):
                        act.wait_ge(*s["product"].at(step.back(2)))
                    sc.copy(xT[step.u % 2][:, :], banks[step.u % 2][:, :]).then_inc(s["copied"].sem, 1)

                def first_norm(step):
                    mid = step.back(3)
                    if mid.exists(nb):
                        if kind == "n3" and final and mid.back(4).exists(nb):
                            act.wait_ge(*s["out2"].at(mid.back(4)))
                        elif mid.back(4).exists(nb):
                            act.wait_ge(*s["out"].at(mid.back(4)))
                        normalise(step.back(1), n1[mid.u], n2[mid.u], 0, "norm")

                def last_norm(step):
                    end = step.back(LAG[kind])
                    if end.exists(nb):
                        if end.back(4).exists(nb):
                            act.wait_ge(*s["stored"].at(end.back(4)))
                        computed = {"n0": 1, "n1": 3, "n2": 3, "n3": 1}[kind]
                        normalise(step.back(computed), (n1 if kind == "n1" else n2)[end.u], y_out[end.u],
                                  1 if kind in ("n0", "n3") else 0, "out2" if kind == "n3" else "out")

                def body(step):
                    now = step.back(1)
                    u, d = now.u, now.u % 2
                    if kind == "n0":
                        if step.exists(nb):
                            turned_x(step)
                        if now.exists(nb):
                            act.wait_ge(*s["z"].at(now))
                            sc.activation(small[u][:, 1, :], small[u][:, 0, :], ACT.Sigmoid, bias=scal[:, 2:3]
                                          ).then_inc(s["gate"].sem, 1)
                        if now.exists(nb):
                            act.wait_ge(*s["gate"].at(now))
                            for k in range(g):
                                last = sc.activation(n1[u][:, k, :], banks[2 + d][:, k * P:(k + 1) * P], ACT.Copy,
                                                     scale=small[u][:, 1, k:k + 1])
                            last.then_inc(s["gated"].sem, 1)
                        last_norm(step)
                        first_norm(step)
                    elif kind == "n1":
                        if step.exists(nb):
                            turned_x(step)
                        last_norm(step)
                    elif kind == "n2":
                        if step.exists(nb):
                            turned_x(step)
                        if now.exists(nb):
                            act.wait_ge(*s["product"].at(now))
                            if now.back(2).exists(nb):
                                act.wait_ge(*s["zd"].at(now.back(2)))
                            sc.activation(gates[d].rearrange("p k a f -> p k (a f)"),
                                          psum[:, 2 + 2 * d:4 + 2 * d, H:3 * H], ACT.Sigmoid
                                          ).then_inc(s["gates"].sem, 1)
                        last_norm(step)
                        if now.exists(nb):
                            act.wait_ge(*s["npre"].at(now))
                            if now.back(4).exists(nb):
                                act.wait_ge(*s["out"].at(now.back(4)))
                            sc.activation(n2[u][:, 0:g, :], n1[u][:, 0:g, :], ACT.Tanh).then_inc(s["n"].sem, 1)
                    else:
                        if now.exists(nb):
                            act.wait_ge(*s["pair"].at(now))
                            sc.activation(small[u][:, 4:6, :], small[u][:, 2:4, :], ACT.Exp).then_inc(s["exp"].sem, 1)
                        if step.exists(nb):
                            turned_x(step)
                        if final:
                            last_norm(step)
                        else:
                            first_norm(step)
                        if now.exists(nb):
                            act.wait_ge(*s["coef"].at(now))
                            if now.back(2).exists(nb):
                                act.wait_ge(*s["with_own"].at(now.back(2)))
                            for k in range(g):
                                last = sc.activation(n3[d][:, k, :], banks[2 + d][:, k * P:(k + 1) * P], ACT.Copy,
                                                     scale=small[u][:, 14, k:k + 1])
                            last.then_inc(s["own"].sem, 1)
                        if final:
                            first_norm(step)
                run_steps(act, nb, 3 if kind == "n3" and not final else LAG[kind], body)

            for kind, turn in passes:
                (edge if kind[0] == "e" else node)(kind, turn)

        @block.vector
        def _(dve):
            ve = nc.vector
            prep = [0]

            def step_done(ins, at=None):
                prep[0] += 1
                ins.then_inc(s_prep, 1)
                dve.wait_ge(s_prep, prep[0])
                assert at is None or prep[0] == at, prep[0]

            ve.memset(rows[:, ROW_GRU, :], 0.0)
            ve.memset(rows[:, ROW_HH, :], 0.0).then_inc(s_const, 1)
            ve.memset(ones_bf[:, :], 1.0)
            ve.memset(split[:, :, :], 0.0)
            ve.memset(head_ones[:, :], 0.0).then_inc(s_const, 1)
            dve.wait_ge(s_const, 2)
            for k in range(HEADS):
                b = slice(k * HEAD, (k + 1) * HEAD)
                ve.memset(head_ones[b, b], float(HEAD) ** -0.5)
            for u in range(4):
                ve.memset(mv[u], 1.0)
            ve.memset(gate_heads[:, :], 0.0)
            ve.memset(head_first[:, :], 0.0)
            for u in range(U):
                last = ve.memset(row_out[u][:, :, H:W0], -BIG)
            last.then_inc(s_const, 1)
            dve.wait_ge(s_const, 3)
            dve.wait_ge(s_rows_in, 8 * 16)
            T1 = TILES - P
            halves = ((slice(0, P), 0), (slice(0, T1), 1))
            chain = [0]

            def linked(ins):
                chain[0] += 1
                ins.then_inc(s_list_steps, 1)
                dve.wait_ge(s_list_steps, chain[0])

            for p, i in halves:
                ve.tensor_copy(lists_f[p, 0:3, i, :], lists[p, :, i, :])
                linked(ve.tensor_copy(lists_f[p, 3, i, :], lists_w[p, i, :]))
            for p, i in halves:
                linked(ve.tensor_tensor(lists_f[p, 2, i, :], lists_f[p, 1, i, :], lists_f[p, 2, i, :], ALU.is_equal))
                linked(ve.scalar_tensor_tensor(lists_f[p, 2, i, :], lists_f[p, 2, i, :], float(NO_ROW),
                                               lists_f[p, 1, i, :], ALU.mult, ALU.add))
                linked(ve.tensor_scalar(lists_f[p, 1, i, :], lists_f[p, 1, i, :], float(N - 1), None, ALU.min))
            step_done(ve.memset(one[:, :], 1.0), PREP_LISTS)
            dve.wait_ge(s_turned, 1)
            tab = table_sb[:, :].rearrange("p (g c k) -> p g c k", c=4, k=ET)
            for k in range(4):
                frm = banks[k][:, 0:TILES].rearrange("p (g k) -> p g k", k=ET)
                to = tab[:, :, k, :]
                if k == 3:
                    to = to.bitcast(F32)
                last = ve.tensor_copy(to, frm)
            step_done(last, PREP_TABLE)
            dve.wait_ge(s_turned, 2)
            for i in range(4):
                n = min(4, 13 - 4 * i)
                ve.tensor_copy(wT[:, 4 * i:4 * i + n, :].rearrange("p c o -> p (c o)"), banks[4 + i][:, 0:n * P])
            ve.tensor_tensor(gate_w[:, 0:1], cols[:, WG:WG + 1], cols[:, WG + 2:WG + 3], ALU.add)
            ve.tensor_tensor(gate_w[:, 1:2], cols[:, WG + 1:WG + 2], cols[:, WG + 2:WG + 3], ALU.subtract)
            step_done(ve.tensor_copy(bs_wide[:, :], cols[:, BS:BS + 1].broadcast_to([P, P])), PREP_TURNED)
            dve.wait_ge(s_turned, 3)
            step_done(ve.tensor_copy(products[:, 0:6], banks[0][:, 0:6]))
            step_done(ve.tensor_tensor(self_col[:, :], products[:, 1:1 + L3], products[:, 1 + L3:1 + 2 * L3], ALU.add))
            ve.tensor_tensor(scal[:, 2:3], products[:, 5:6], scal[:, 1:2], ALU.add)
            for i in range(2 * L3):
                ve.tensor_copy(att_wide[:, i, :], products[:, 1 + i:2 + i].broadcast_to([P, P]))
            dve.wait_ge(s_ident, 3)
            ve.tensor_copy(type_id[:, :], type_i[:, :])
            step_done(ve.tensor_tensor(embed_b[0:TYPES, :], embed[0:TYPES, 0, :], embed[0:TYPES, 1, :], ALU.add))
            for k in range(HEADS):
                b = slice(k * HEAD, (k + 1) * HEAD)
                ve.tensor_copy(gate_heads[b, k:k + 1], gate_w[b, 1:2])
                ve.memset(head_first[k * HEAD:k * HEAD + 1, k:k + 1], 1.0)
            ve.tensor_scalar(neg_ident[:, :], ident[:, :], -1.0, None, ALU.mult)
            step_done(ve.tensor_tensor(rows[:, ROW_GRU, :], rows[:, ROW_GRU, :], rows[:, ROW_HH, :], ALU.add))
            for r, n in ((ROW_BS, 3), (ROW_BIAS3, L3)):
                r0, r1, these = rest0[:, 0:n, :], rest1[:, 0:n, :], slice(r, r + n)
                step_done(ve.tensor_copy(split[0:1, these, :], rows[:, these, :]))
                step_done(ve.tensor_tensor(r0, rows[:, these, :], split[0:1, these, :], ALU.subtract))
                step_done(ve.tensor_copy(split[32:33, these, :], r0))
                step_done(ve.tensor_copy(r1, split[32:33, these, :]))
                step_done(ve.tensor_tensor(r0, r0, r1, ALU.subtract))
                step_done(ve.tensor_copy(split[64:65, these, :], r0), PREP_ALL if r == ROW_BIAS3 else None)

            def edge(kind, turn):
                s = S[kind, turn]

                def scale_rows(done):
                    b, v = done.u % 2, done.u
                    dve.wait_ge(*s["rows"].at(done))
                    ve.reciprocal(inv_heads[b], row_banks[:, :, P + HEADS:P + 2 * HEADS]).then_inc(s["inv"].sem, 1)
                    dve.wait_ge(*s["inv"].at(done))
                    ve.tensor_tensor(head_dots[b], row_banks[:, :, P:P + HEADS], inv_heads[b], ALU.mult
                                     ).then_inc(s["dots"].sem, 1)
                    if done.back(U).exists(EG):
                        dve.wait_ge(*s["scattered"].at(done.back(U)))
                    ve.tensor_tensor(row_out[v][:, :, 0:H].rearrange("p t (h f) -> p t h f", h=HEADS),
                                     row_banks[:, :, 0:H].rearrange("p t (h f) -> p t h f", h=HEADS),
                                     inv_heads[b].unsqueeze(3).broadcast_to([P, ET, HEADS, HEAD]), ALU.mult)
                    dve.wait_ge(*s["dots"].at(done))
                    ve.tensor_reduce(row_out[v][:, :, H], head_dots[b], mybir.AxisListType.X, ALU.add
                                     ).then_inc(s["copied"].sem, 1)

                def body(step):
                    if not step.exists(EG):
                        if kind == "e0":
                            scale_rows(step.back(1))
                        return
                    u, d = step.u, step.u % 2
                    o = 1 - d
                    before = step.back(1)
                    first = not before.exists(EG)
                    dve.wait_ge(*s["table"].at(step))
                    ve.tensor_tensor(same[d][:, :], dstb[u][:, 1:], dstb[u][:, 0:EB], ALU.is_equal
                                     ).then_inc(s["same"].sem, 1)
                    dve.wait_ge(*s["same"].at(step))
                    if kind == "e1":
                        dve.wait_ge(*s["src"].at(step))
                        w = etab[u][:, 3 * ET:4 * ET].bitcast(F32)
                        for k in range(ET):
                            last = ve.tensor_scalar(x_src[u][:, k, :], x_src[u][:, k, :], w[:, k:k + 1], None, ALU.mult)
                        last.then_inc(s["weighted"].sem, 1)
                        dve.wait_ge(*s["act"].at(step))
                        if step.back(2).exists(EG):
                            dve.wait_ge(*s["rows"].at(step.back(2)))
                        if not first:
                            dve.wait_ge(*s["acc"].at(before))
                        ve.tensor_tensor_scan(acc[d][:, :], same[d][:, :], e1[d][:, :],
                                              0.0 if first else acc[o][:, EB - 1:EB], ALU.mult, ALU.max
                                              ).then_inc(s["acc"].sem, 1)
                        return
                    if kind == "e2":
                        ve.tensor_scalar(e2[d][0:TYPES, :], typeb[u][0:TYPES, :], float(TYPES - 1), 0.0,
                                         ALU.min, ALU.max).then_inc(s["clipped"].sem, 1)
                        dve.wait_ge(*s["clipped"].at(step))
                        if step.back(2).exists(EG):
                            dve.wait_ge(*s["projected"].at(step.back(2)))
                        ve.tensor_scalar(e1[d][0:TYPES, :], e2[d][0:TYPES, :], type_id[0:TYPES, :], None, ALU.is_equal
                                         ).then_inc(s["onehot"].sem, 1)
                        dve.wait_ge(*s["projected"].at(step))
                        if step.back(2).exists(EG):
                            dve.wait_ge(*s["rows"].at(step.back(2)))
                        if not first:
                            dve.wait_ge(*s["acc"].at(before))
                        ve.tensor_tensor_scan(acc[d][:, :], same[d][:, :], banks[2][:, :],
                                              0.0 if first else acc[o][:, EB - 1:EB], ALU.mult, ALU.add
                                              ).then_inc(s["acc"].sem, 1)
                        return
                    ve.tensor_scalar(fresh[d][:, :], same[d][:, :], -1.0, BIG, ALU.add, ALU.mult
                                     ).then_inc(s["fresh"].sem, 1)
                    if kind == "e0":
                        dve.wait_ge(*s["q"].at(step))
                        if step.back(2).exists(EG):
                            dve.wait_ge(*s["logits"].at(step.back(2)))
                        ve.scalar_tensor_tensor(e1[d][:, :], banks[3][:, :], cols[:, BK:BK + 1], e2[d][:, :],
                                                ALU.add, ALU.mult).then_inc(s["prod"].sem, 1)
                        if not first:
                            scale_rows(before)
                    else:
                        dve.wait_ge(*s["sloped"].at(step))
                        ve.tensor_tensor(e1[d][:, :], e1[d][:, :], banks[5][:, :], ALU.max
                                         ).then_inc(s["logits"].sem, 1)
                    dve.wait_ge(*s["fresh"].at(step))
                    dve.wait_ge(*s["logits"].at(step))
                    logit = banks[5][:, :] if kind == "e0" else e1[d][:, :]
                    if step.back(2).exists(EG):
                        dve.wait_ge(*s["rows"].at(step.back(2)))
                    if first:
                        ve.memset(top[d][:, 0:1], 0.0).then_inc(s["carried"].sem, 1)
                    else:
                        dve.wait_ge(*s["top"].at(before))
                        ve.tensor_copy(top[d][:, 0:1], top[o][:, EB:EB + 1]).then_inc(s["carried"].sem, 1)
                    dve.wait_ge(*s["carried"].at(step))
                    ve.tensor_tensor_scan(top[d][:, 1:], fresh[d][:, :], logit, top[d][:, 0:1], ALU.add, ALU.max
                                          ).then_inc(s["top"].sem, 1)
                    if step.back(2).exists(EG):
                        dve.wait_ge(*s["exp"].at(step.back(2)))
                    dve.wait_ge(*s["top"].at(step))
                    ve.tensor_tensor(pair[d][:, 0, :], top[d][:, 0:EB], fresh[d][:, :], ALU.add
                                     ).then_inc(s["t0"].sem, 1)
                    ve.tensor_tensor(pair[d][:, 1, :], logit, top[d][:, 1:], ALU.subtract).then_inc(s["d1"].sem, 1)
                    dve.wait_ge(*s["t0"].at(step))
                    ve.tensor_tensor(pair[d][:, 0, :], pair[d][:, 0, :], top[d][:, 1:], ALU.subtract
                                     ).then_inc(s["d0"].sem, 1)
                    dve.wait_ge(*s["exp"].at(step))
                    if not first:
                        dve.wait_ge(*s["total"].at(before))
                    ve.tensor_tensor_scan(total[d][:, :], expd[d][:, 0, :], expd[d][:, 1, :],
                                          0.0 if first else total[o][:, EB - 1:EB], ALU.mult, ALU.add
                                          ).then_inc(s["total"].sem, 1)
                    if kind == "e0":
                        dve.wait_ge(*s["v_projected"].at(step))
                        ve.scalar_tensor_tensor(e1[d][:, :], banks[4][:, :], cols[:, BV:BV + 1], expd[d][:, 1, :],
                                                ALU.add, ALU.mult).then_inc(s["wv"].sem, 1)
                    else:
                        dve.wait_ge(*s["h_projected"].at(step))
                        ve.tensor_tensor(e2[d][:, :], banks[4][:, :], expd[d][:, 1, :], ALU.mult
                                         ).then_inc(s["wv"].sem, 1)
                    dve.wait_ge(*s["wv"].at(step))
                    if not first:
                        dve.wait_ge(*s["acc"].at(before))
                    ve.tensor_tensor_scan(acc[d][:, :], expd[d][:, 0, :], (e1 if kind == "e0" else e2)[d][:, :],
                                          0.0 if first else acc[o][:, EB - 1:EB], ALU.mult, ALU.add
                                          ).then_inc(s["acc"].sem, 1)
                run_steps(dve, EG, 1 if kind == "e0" else 0, body)

            def row_stats(block, v, stat, g, sig):
                for k in range(g):
                    last = ve.bn_stats(stats[block.u % 2][:, stat, k, :], v[:, k, :])
                last.then_inc(sig.sem, 1)

            def moments(s, block, step, stat, g, stats_sig, sig):
                dve.wait_ge(*stats_sig.at(block))
                if step.back(4).exists():
                    dve.wait_ge(*s["moments"].at(step.back(4)))
                settled(dve)
                for k in range(g):
                    last = ve.bn_aggr(mv[step.u][:, stat, k, :], stats[block.u % 2][:, stat, k, :])
                last.then_inc(sig.sem, 1)

            def along(i):
                return wide[:, i, :].unsqueeze(1).broadcast_to([P, G, P])

            def node_0(turn):
                s = S["n0", 0]

                def body(step):
                    two, four, five, six = (step.back(k) for k in (2, 4, 5, 6))
                    if two.exists(NB):
                        dve.wait_ge(*s["gated"].at(two))
                        ve.tensor_tensor(n1[two.u], n1[two.u], msg_in[two.u][:, :, 0:H], ALU.add
                                         ).then_inc(s["mix"].sem, 1)
                    if six.exists(NB):
                        dve.wait_ge(*s["sum"].at(six))
                        row_stats(six, n2[six.u], 1, G, s["stats2"])
                    if two.exists(NB):
                        dve.wait_ge(*s["mix"].at(two))
                        row_stats(two, n1[two.u], 0, G, s["stats"])
                    if six.exists(NB):
                        moments(s, six, step, 1, G, s["stats2"], s["mv2"])
                    if two.exists(NB):
                        moments(s, two, step, 0, G, s["stats"], s["mv"])
                    if four.exists(NB):
                        dve.wait_ge(*s["scaled"].at(four))
                        ve.tensor_tensor(n2[four.u], n2[four.u], along(BET0), ALU.add).then_inc(s["shifted"].sem, 1)
                    if five.exists(NB):
                        dve.wait_ge(*s["residual"].at(five))
                        ve.scalar_tensor_tensor(n2[five.u], n2[five.u], 0.0, n3[five.u % 2],
                                                ALU.max, ALU.add).then_inc(s["sum"].sem, 1)
                    if four.exists(NB):
                        dve.wait_ge(*s["shifted"].at(four))
                        if four.back(2).exists(NB):
                            dve.wait_ge(*s["sum"].at(four.back(2)))
                        ve.tensor_scalar(n3[four.u % 2], n2[four.u], 0.0, scal[:, 0:1], ALU.min, ALU.mult
                                         ).then_inc(s["act"].sem, 1)
                    if step.exists(NB):
                        dve.wait_ge(*s["loaded"].at(step))
                        dve.wait_ge(*s["product"].at(step))
                        ve.tensor_tensor(small[step.u][:, 0, :], banks[4 + step.u % 2][:, 0:G],
                                         msg_in[step.u][:, :, H], ALU.add).then_inc(s["z"].sem, 1)
                run_steps(dve, NB, 6, body)

            def node_1(turn):
                s = S["n1", 0]

                def body(step):
                    u, d = step.u, step.u % 2
                    dve.wait_ge(*s["product"].at(step))
                    if step.back(4).exists(NB):
                        dve.wait_ge(*s["out"].at(step.back(4)))
                    ve.scalar_tensor_tensor(n1[u].rearrange("p g f -> p (g f)"), banks[2 + d], 0.0,
                                            x_deep[u].rearrange("p g f -> p (g f)"), ALU.max, ALU.add
                                            ).then_inc(s["sum"].sem, 1)
                    dve.wait_ge(*s["sum"].at(step))
                    row_stats(step, n1[u], 0, G, s["stats"])
                    moments(s, step, step, 0, G, s["stats"], s["mv"])
                run_steps(dve, NB, 0, body)

            def node_2(turn):
                s = S["n2", 0]
                g = G2

                def body(step):
                    u, d = step.u, step.u % 2
                    one = step.back(1)
                    v, e = one.u, one.u % 2
                    gate_banks = psum[:, 2 + 2 * d:4 + 2 * d, :]
                    if step.exists(NB2):
                        dve.wait_ge(*s["gates"].at(step))
                        ve.tensor_tensor(n1[u][:, 0:g, :], gates[d][:, :, 0, :], gate_banks[:, :, 3 * H:4 * H], ALU.mult
                                         ).then_inc(s["rn"].sem, 1)
                    if one.exists(NB2):
                        dve.wait_ge(*s["n"].at(one))
                        ve.tensor_tensor(n3[e][:, 0:g, :], x_deep[v][:, 0:g, :], n2[v][:, 0:g, :], ALU.subtract
                                         ).then_inc(s["diff"].sem, 1)
                    if step.exists(NB2):
                        dve.wait_ge(*s["rn"].at(step))
                        ve.tensor_tensor(n1[u][:, 0:g, :], n1[u][:, 0:g, :], gate_banks[:, :, 0:H], ALU.add
                                         ).then_inc(s["npre"].sem, 1)
                    if one.exists(NB2):
                        dve.wait_ge(*s["diff"].at(one))
                        ve.tensor_tensor(n3[e][:, 0:g, :], n3[e][:, 0:g, :], gates[e][:, :, 1, :], ALU.mult
                                         ).then_inc(s["zd"].sem, 1)
                        ve.tensor_tensor(n2[v][:, 0:g, :], n2[v][:, 0:g, :], x_deep[v][:, 0:g, :], ALU.add
                                         ).then_inc(s["hn"].sem, 1)
                        dve.wait_ge(*s["zd"].at(one))
                        dve.wait_ge(*s["hn"].at(one))
                        ve.tensor_tensor(n2[v][:, 0:g, :], n2[v][:, 0:g, :], n3[e][:, 0:g, :], ALU.add
                                         ).then_inc(s["sum"].sem, 1)
                        dve.wait_ge(*s["sum"].at(one))
                        row_stats(one, n2[v], 0, g, s["stats"])
                        moments(s, one, step, 0, g, s["stats"], s["mv"])
                run_steps(dve, NB2, 1, body)

            def node_3(turn):
                s = S["n3", turn]
                final = turn == L3 - 1

                def body(step):
                    one, two, four, five = (step.back(k) for k in (1, 2, 4, 5))
                    sm1, sm, dots = small[one.u], small[step.u], banks[4 + step.u % 2][:, 0:G]
                    edge_top = msg_in[step.u][:, :, H + 1]

                    def message(k):
                        return ve.scalar_tensor_tensor(n1[two.u][:, k, :], msg_in[two.u][:, k, 0:H],
                                                       small[two.u][:, 13, k:k + 1],
                                                       banks[6 + two.u % 2][:, k * P:(k + 1) * P],
                                                       ALU.mult, ALU.add)

                    if two.exists(NB):
                        dve.wait_ge(*s["with_own"].at(two))
                        if two.back(4).exists(NB):
                            dve.wait_ge(*s["norm"].at(two.back(4)))
                        message(0)
                        message(1)
                    if one.exists(NB):
                        dve.wait_ge(*s["exp"].at(one))
                        ve.tensor_tensor(sm1[:, 6, :], sm1[:, 4, :], msg_in[one.u][:, :, H], ALU.mult
                                         ).then_inc(s["s0"].sem, 1)
                    if two.exists(NB):
                        message(2)
                    if one.exists(NB):
                        dve.wait_ge(*s["s0"].at(one))
                        ve.tensor_tensor(sm1[:, 7, :], sm1[:, 6, :], sm1[:, 5, :], ALU.add).then_inc(s["s1"].sem, 1)
                    if two.exists(NB):
                        message(3).then_inc(s["y1"].sem, 1)
                    if one.exists(NB):
                        dve.wait_ge(*s["s1"].at(one))
                        ve.reciprocal(sm1[:, 12, :], sm1[:, 7, :]).then_inc(s["inv"].sem, 1)
                        dve.wait_ge(*s["inv"].at(one))
                        ve.tensor_tensor(sm1[:, 13, :], sm1[:, 4, :], sm1[:, 12, :], ALU.mult)
                        ve.tensor_tensor(sm1[:, 14, :], sm1[:, 5, :], sm1[:, 12, :], ALU.mult
                                         ).then_inc(s["coef"].sem, 1)
                    if final and five.exists(NB):
                        dve.wait_ge(*s["out"].at(five))
                        row_stats(five, n2[five.u], 1, G, s["stats2"])
                    if two.exists(NB):
                        dve.wait_ge(*s["y1"].at(two))
                        row_stats(two, n1[two.u], 0, G, s["stats"])
                    if final and five.exists(NB):
                        moments(s, five, step, 1, G, s["stats2"], s["mv2"])
                    if step.exists(NB):
                        dve.wait_ge(*s["loaded"].at(step))
                        dve.wait_ge(*s["product"].at(step))
                        ve.tensor_scalar(sm[:, 15, :], dots, SLOPE, None, ALU.mult).then_inc(s["sloped"].sem, 1)
                    if two.exists(NB):
                        moments(s, two, step, 0, G, s["stats"], s["mv"])
                    if step.exists(NB):
                        dve.wait_ge(*s["sloped"].at(step))
                        ve.tensor_tensor(sm[:, 0, :], sm[:, 15, :], dots, ALU.max).then_inc(s["z"].sem, 1)
                        dve.wait_ge(*s["z"].at(step))
                        ve.tensor_tensor(sm[:, 1, :], sm[:, 0, :], edge_top, ALU.max).then_inc(s["top"].sem, 1)
                        dve.wait_ge(*s["top"].at(step))
                        ve.tensor_tensor(sm[:, 2, :], edge_top, sm[:, 1, :], ALU.subtract)
                        ve.tensor_tensor(sm[:, 3, :], sm[:, 0, :], sm[:, 1, :], ALU.subtract
                                         ).then_inc(s["pair"].sem, 1)
                    if final and four.exists(NB):
                        dve.wait_ge(*s["sum"].at(four))
                        ve.tensor_tensor(n2[four.u], n2[four.u], along(BET3 + turn), ALU.add
                                         ).then_inc(s["out"].sem, 1)
                run_steps(dve, NB, 5 if final else 4, body)

            nodes = {"n0": node_0, "n1": node_1, "n2": node_2, "n3": node_3}
            for kind, turn in passes:
                if kind[0] == "e":
                    edge(kind, turn)
                else:
                    nodes[kind](turn)


_INS = ['x', 'src', 'dst', 'edge_type_9', 'edge_weight',
        'L0_gnn_Wq', 'L0_gnn_bq', 'L0_gnn_Wk', 'L0_gnn_bk', 'L0_gnn_Wv', 'L0_gnn_bv', 'L0_gnn_Ws', 'L0_gnn_bs',
        'L0_gnn_Wg', 'L0_gnn_bg', 'L0_gnn_gamma', 'L0_gnn_beta', 'L0_gnn_alpha',
        'L1_gnn_pool_w', 'L1_gnn_pool_b', 'L1_gnn_final_w', 'L1_gnn_final_b',
        'L2_gnn_W_msg', 'L2_gnn_b_msg', 'L2_gnn_edge_embed', 'L2_gnn_W_ih', 'L2_gnn_W_hh', 'L2_gnn_b_ih', 'L2_gnn_b_hh',
        'L3_gnn_W', 'L3_gnn_att_src', 'L3_gnn_att_dst', 'L3_gnn_bias', 'L3_gnn_gamma', 'L3_gnn_beta']


def kernel(**inputs):
    import numpy as np
    import concourse.bacc as bacc
    from concourse import mybir as _mybir
    from concourse.bass_utils import run_bass_kernel_spmd

    nc = bacc.Bacc("TRN2", target_bir_lowering=False, num_devices=1)
    arrays, args = {}, []
    for name in _INS:
        a = np.ascontiguousarray(inputs[name])
        arrays[f"in_{name}"] = a
        args.append(nc.dram_tensor(f"in_{name}", a.shape, _mybir.dt.from_np(a.dtype), kind="ExternalInput").ap())
    out = nc.dram_tensor("out_x", inputs["x"].shape, _mybir.dt.float32, kind="ExternalOutput").ap()
    gnn_kernel(nc, *args, out)
    result = run_bass_kernel_spmd(nc, [arrays], core_ids=[0])
    return result.results[0]["out_x"]
```
